# Optimizing a Trainium2 kernel written in Bass

```python
import numpy as np
import jax
import jax.numpy as jnp

def _softmax(x, axis=-1):
    return jax.nn.softmax(x, axis=axis)

def _gelu(x):
    return jax.nn.gelu(x, approximate=True)

def _silu(x):
    return jax.nn.silu(x)

def _sigmoid(x):
    return jax.nn.sigmoid(x)

def _layernorm(x, axis=-1, eps=1e-05):
    m = jnp.mean(x, axis=axis, keepdims=True)
    v = jnp.var(x, axis=axis, keepdims=True)
    return (x - m) / jnp.sqrt(v + eps)

def _scatter_add(tgt, idx, src, axis=0):
    return tgt.at[idx].add(src)

def _segment_sum(src, seg, n):
    return jax.ops.segment_sum(src, seg, n)
kernel_name = 'mk_adaln_d2_jaxref_r8_750dd2'

def setup_inputs(seed: int=0):
    np.random.seed(seed)
    _w = jnp.asarray

    def _L0_attn_setup():
        import jax, jax.numpy as jnp
        import numpy as np
        DELTA_SCALE = 0.99
        DELTA_MIN = 0.01

        def _scan_combine(left, right):
            a_l, u_l = left
            a_r, u_r = right
            return (a_l * a_r, a_r * u_l + u_r)
        key = jax.random.key(seed)
        ks = jax.random.split(key, 6)
        B, S, Dm, N = (8, 512, 128, 16)
        x = jax.random.normal(ks[0], (B, S, Dm), dtype=jnp.float32)
        A = jax.random.normal(ks[1], (N,), dtype=jnp.float32) * 0.1 - 1.0
        W_b = jax.random.normal(ks[2], (N, Dm), dtype=jnp.float32) / np.sqrt(Dm)
        b_b = jnp.zeros((N,), dtype=jnp.float32)
        W_c = jax.random.normal(ks[3], (Dm, N), dtype=jnp.float32) / np.sqrt(N)
        b_c = jnp.zeros((Dm,), dtype=jnp.float32)
        D = jnp.ones((Dm,), dtype=jnp.float32)
        W_t = jax.random.normal(ks[4], (1, Dm), dtype=jnp.float32) / np.sqrt(Dm)
        b_t = jnp.zeros((1,), dtype=jnp.float32)
        W_o = jax.random.normal(ks[5], (Dm, Dm), dtype=jnp.float32) / np.sqrt(Dm)
        b_o = jnp.zeros((Dm,), dtype=jnp.float32)
        return {'x': x, 'A': A, 'W_b': W_b, 'b_b': b_b, 'W_c': W_c, 'b_c': b_c, 'D': D, 'W_t': W_t, 'b_t': b_t, 'W_o': W_o, 'b_o': b_o}
    _L0_attn_in = _L0_attn_setup()

    def _L0_ffn_setup():
        import jax, jax.numpy as jnp
        import numpy as np
        E = 8
        K = 2
        S = 1
        THRESHOLD = 0.7
        NORM_TOPK = True
        H = 128
        F = 128
        B, SEQ = (2, 128)
        key = jax.random.key(seed)
        k1, k2, k3, k4, k5 = jax.random.split(key, 5)
        hidden_states = jax.random.normal(k1, (B, SEQ, H), jnp.float32)
        gate_weight = jax.random.normal(k2, (E, H), jnp.float32) * 0.02
        gate_up_proj = jax.random.normal(k3, (E, 2 * F, H), jnp.float32) * 0.02
        down_proj = jax.random.normal(k4, (E, H, F), jnp.float32) * 0.02
        sim = jax.random.uniform(k5, (E, E), jnp.float32)
        sim = (sim + sim.T) / 2.0
        sim = sim.at[jnp.arange(E), jnp.arange(E)].set(1.0)
        return {'hidden_states': hidden_states, 'gate_weight': gate_weight, 'gate_up_proj': gate_up_proj, 'down_proj': down_proj, 'similarity_matrix': sim}
    _L0_ffn_in = _L0_ffn_setup()
    _L0_c = _w((lambda *s: np.random.randn(*s).astype(np.float32) * 0.05)(16, 128))
    _L0_wmod = _w((lambda *s: np.random.randn(*s).astype(np.float32) * 0.05)(128, 6 * 128) * 128 ** (-0.5))

    def _L1_attn_setup():
        import jax, jax.numpy as jnp
        import numpy as np
        from math import sqrt
        HEADS = 16
        MODEL_DIM = 128
        DIM_PER_HEAD = MODEL_DIM // HEADS
        MAX_REL_POS = 32
        ROPE_BASE = 10000.0
        NEG_INF = -1e+18

        def _rope_cos_sin(seq_len, dim):
            inv_freq = 1.0 / ROPE_BASE ** (jnp.arange(0, dim, 2, dtype=jnp.float32) / dim)
            t = jnp.arange(seq_len, dtype=jnp.float32)
            ang = jnp.outer(t, inv_freq)
            return (jnp.cos(ang), jnp.sin(ang))

        def _apply_rotary_interleave(x, cos, sin):
            B, H, L, D = x.shape
            x_ = x.reshape(B, H, L, D // 2, 2)
            xe, xo = (x_[..., 0], x_[..., 1])
            c = cos[None, None, :, :]
            s = sin[None, None, :, :]
            oe = xe * c - xo * s
            oo = xe * s + xo * c
            return jnp.stack([oe, oo], axis=-1).reshape(B, H, L, D)
        key = jax.random.key(seed)
        ks = jax.random.split(key, 6)
        B, L = (2, 128)
        scale = 0.02
        x = jax.random.normal(ks[0], (B, L, MODEL_DIM), dtype=jnp.float32)
        w_q = jax.random.normal(ks[1], (MODEL_DIM, MODEL_DIM), dtype=jnp.float32) * scale
        w_k = jax.random.normal(ks[2], (MODEL_DIM, MODEL_DIM), dtype=jnp.float32) * scale
        w_v = jax.random.normal(ks[3], (MODEL_DIM, MODEL_DIM), dtype=jnp.float32) * scale
        w_o = jax.random.normal(ks[4], (MODEL_DIM, MODEL_DIM), dtype=jnp.float32) * scale
        rel_emb = jax.random.normal(ks[5], (2 * MAX_REL_POS + 1, DIM_PER_HEAD), dtype=jnp.float32) * scale
        return {'x': x, 'w_q': w_q, 'w_k': w_k, 'w_v': w_v, 'w_o': w_o, 'rel_emb': rel_emb}
    _L1_attn_in = _L1_attn_setup()

    def _L1_ffn_setup():
        import jax, jax.numpy as jnp
        import numpy as np
        B, T, C = (2, 64, 128)
        I = 512
        E = 8
        K = 2
        key = jax.random.key(seed)
        ks = jax.random.split(key, 8)
        s = 0.02
        return {'x': jax.random.normal(ks[0], (B, T, C), jnp.float32), 'Wr1': jax.random.normal(ks[1], (C, C // 4), jnp.float32) * s, 'br1': jnp.zeros((C // 4,), jnp.float32), 'Wr2': jax.random.normal(ks[2], (C // 4, E), jnp.float32) * s, 'br2': jnp.zeros((E,), jnp.float32), 'Ws1': jax.random.normal(ks[3], (C, I), jnp.float32) * s, 'bs1': jnp.zeros((I,), jnp.float32), 'Ws2': jax.random.normal(ks[4], (I, C), jnp.float32) * s, 'bs2': jnp.zeros((C,), jnp.float32), 'We1': jax.random.normal(ks[5], (E, C, I), jnp.float32) * s, 'be1': jnp.zeros((E, I), jnp.float32), 'We2': jax.random.normal(ks[6], (E, I, C), jnp.float32) * s, 'be2': jnp.zeros((E, C), jnp.float32)}
    _L1_ffn_in = _L1_ffn_setup()
    _L1_c = _w((lambda *s: np.random.randn(*s).astype(np.float32) * 0.05)(16, 128))
    _L1_wmod = _w((lambda *s: np.random.randn(*s).astype(np.float32) * 0.05)(128, 6 * 128) * 128 ** (-0.5))
    _d = {'L0_attn_x': _L0_attn_in['x'], 'L0_attn_A': _L0_attn_in['A'], 'L0_attn_W_b': _L0_attn_in['W_b'], 'L0_attn_b_b': _L0_attn_in['b_b'], 'L0_attn_W_c': _L0_attn_in['W_c'], 'L0_attn_b_c': _L0_attn_in['b_c'], 'L0_attn_D': _L0_attn_in['D'], 'L0_attn_W_t': _L0_attn_in['W_t'], 'L0_attn_b_t': _L0_attn_in['b_t'], 'L0_attn_W_o': _L0_attn_in['W_o'], 'L0_attn_b_o': _L0_attn_in['b_o'], 'L0_ffn_gate_weight': _L0_ffn_in['gate_weight'], 'L0_ffn_gate_up_proj': _L0_ffn_in['gate_up_proj'], 'L0_ffn_down_proj': _L0_ffn_in['down_proj'], 'L0_ffn_similarity_matrix': _L0_ffn_in['similarity_matrix'], 'L0_c': _L0_c, 'L0_wmod': _L0_wmod, 'L1_attn_w_q': _L1_attn_in['w_q'], 'L1_attn_w_k': _L1_attn_in['w_k'], 'L1_attn_w_v': _L1_attn_in['w_v'], 'L1_attn_w_o': _L1_attn_in['w_o'], 'L1_attn_rel_emb': _L1_attn_in['rel_emb'], 'L1_ffn_Wr1': _L1_ffn_in['Wr1'], 'L1_ffn_br1': _L1_ffn_in['br1'], 'L1_ffn_Wr2': _L1_ffn_in['Wr2'], 'L1_ffn_br2': _L1_ffn_in['br2'], 'L1_ffn_Ws1': _L1_ffn_in['Ws1'], 'L1_ffn_bs1': _L1_ffn_in['bs1'], 'L1_ffn_Ws2': _L1_ffn_in['Ws2'], 'L1_ffn_bs2': _L1_ffn_in['bs2'], 'L1_ffn_We1': _L1_ffn_in['We1'], 'L1_ffn_be1': _L1_ffn_in['be1'], 'L1_ffn_We2': _L1_ffn_in['We2'], 'L1_ffn_be2': _L1_ffn_in['be2'], 'L1_c': _L1_c, 'L1_wmod': _L1_wmod}
    _x0 = _d['L0_attn_x']
    _d['L0_attn_x'] = jax.random.normal(jax.random.fold_in(jax.random.key(seed), 1), (16, 256, 128), dtype=_x0.dtype)
    del _x0
    return _d

def reference(L0_attn_x, L0_attn_A, L0_attn_W_b, L0_attn_b_b, L0_attn_W_c, L0_attn_b_c, L0_attn_D, L0_attn_W_t, L0_attn_b_t, L0_attn_W_o, L0_attn_b_o, L0_ffn_gate_weight, L0_ffn_gate_up_proj, L0_ffn_down_proj, L0_ffn_similarity_matrix, L0_c, L0_wmod, L1_attn_w_q, L1_attn_w_k, L1_attn_w_v, L1_attn_w_o, L1_attn_rel_emb, L1_ffn_Wr1, L1_ffn_br1, L1_ffn_Wr2, L1_ffn_br2, L1_ffn_Ws1, L1_ffn_bs1, L1_ffn_Ws2, L1_ffn_bs2, L1_ffn_We1, L1_ffn_be1, L1_ffn_We2, L1_ffn_be2, L1_c, L1_wmod):

    def _L0_attn_ref(x, A, W_b, b_b, W_c, b_c, D, W_t, b_t, W_o, b_o):
        import jax, jax.numpy as jnp
        import numpy as np
        DELTA_SCALE = 0.99
        DELTA_MIN = 0.01

        def _scan_combine(left, right):
            a_l, u_l = left
            a_r, u_r = right
            return (a_l * a_r, a_r * u_l + u_r)
        delta = jax.nn.sigmoid(jnp.einsum('bsd,od->bso', x, W_t) + b_t)
        delta = delta * DELTA_SCALE + DELTA_MIN
        Bu = jnp.einsum('bsd,nd->bsn', x, W_b) + b_b
        A_exp = jnp.exp(A[None, None, :] * delta)
        _, h = jax.lax.associative_scan(_scan_combine, (A_exp, Bu), axis=1)
        outputs = jnp.einsum('bsn,dn->bsd', h, W_c) + b_c
        y = outputs + x * D[None, None, :]
        y = jnp.einsum('bsd,od->bso', y, W_o) + b_o
        return y

    def _L0_ffn_ref(hidden_states, gate_weight, gate_up_proj, down_proj, similarity_matrix):
        import jax, jax.numpy as jnp
        import numpy as np
        E = 8
        K = 2
        S = 1
        THRESHOLD = 0.7
        NORM_TOPK = True
        H = 128
        F = 128
        B, SEQ = (2, 128)
        b, s, h = hidden_states.shape
        x = hidden_states.reshape(-1, h)
        N = x.shape[0]
        logits = x @ gate_weight.T
        probs = jax.nn.softmax(logits.astype(jnp.float32), axis=-1)
        top_w, top_i = jax.lax.top_k(probs, K)
        if NORM_TOPK:
            top_w = top_w / jnp.clip(jnp.sum(top_w, -1, keepdims=True), 1e-12)
        primary_mask = jnp.zeros((E,), bool).at[top_i[:, :S].reshape(-1)].set(True)
        sim = jnp.where(primary_mask[None, :], similarity_matrix.astype(jnp.float32), -jnp.inf)
        best_j = jnp.argmax(sim, axis=-1)
        best_sim = jnp.max(sim, axis=-1)
        ids = jnp.arange(E)
        expert_map = jnp.where(~primary_mask & (best_sim >= THRESHOLD), best_j, ids)
        rerouted = expert_map[top_i]
        rows = jnp.arange(N)[:, None]
        dense = jnp.zeros((N, E), top_w.dtype).at[rows, rerouted].add(top_w)
        fw, fi = jax.lax.top_k(dense, K)
        combine = jnp.zeros((N, E), fw.dtype).at[rows, fi].add(jnp.where(fw > 0, fw, 0.0))
        gu = jnp.einsum('nh,efh->enf', x, gate_up_proj)
        g, u = jnp.split(gu, 2, axis=-1)
        hmid = jax.nn.silu(g) * u
        y = jnp.einsum('enf,ehf->enh', hmid, down_proj)
        out = jnp.einsum('ne,enh->nh', combine, y)
        return out.reshape(b, s, h)

    def _L1_attn_ref(x, w_q, w_k, w_v, w_o, rel_emb):
        import jax, jax.numpy as jnp
        import numpy as np
        from math import sqrt
        HEADS = 16
        MODEL_DIM = 128
        DIM_PER_HEAD = MODEL_DIM // HEADS
        MAX_REL_POS = 32
        ROPE_BASE = 10000.0
        NEG_INF = -1e+18

        def _rope_cos_sin(seq_len, dim):
            inv_freq = 1.0 / ROPE_BASE ** (jnp.arange(0, dim, 2, dtype=jnp.float32) / dim)
            t = jnp.arange(seq_len, dtype=jnp.float32)
            ang = jnp.outer(t, inv_freq)
            return (jnp.cos(ang), jnp.sin(ang))

        def _apply_rotary_interleave(x, cos, sin):
            B, H, L, D = x.shape
            x_ = x.reshape(B, H, L, D // 2, 2)
            xe, xo = (x_[..., 0], x_[..., 1])
            c = cos[None, None, :, :]
            s = sin[None, None, :, :]
            oe = xe * c - xo * s
            oo = xe * s + xo * c
            return jnp.stack([oe, oo], axis=-1).reshape(B, H, L, D)
        B, L, _ = x.shape

        def shape(t):
            return t.reshape(B, L, HEADS, DIM_PER_HEAD).transpose(0, 2, 1, 3)
        q = shape(x @ w_q.T)
        k = shape(x @ w_k.T)
        v = shape(x @ w_v.T)
        cos, sin = _rope_cos_sin(L, DIM_PER_HEAD)
        q = _apply_rotary_interleave(q, cos, sin)
        k = _apply_rotary_interleave(k, cos, sin)
        q = q / sqrt(DIM_PER_HEAD)
        scores = jnp.einsum('bhqd,bhkd->bhqk', q, k)
        pos = jnp.arange(L)
        rel_idx = jnp.clip(pos[None, :] - pos[:, None], -MAX_REL_POS, MAX_REL_POS) + MAX_REL_POS
        rel = rel_emb[rel_idx]
        scores = scores + jnp.einsum('bhqd,qkd->bhqk', q, rel)
        causal = jnp.tril(jnp.ones((L, L), dtype=bool))
        scores = jnp.where(causal[None, None], scores, NEG_INF)
        attn = jax.nn.softmax(scores, axis=-1)
        ctx = jnp.einsum('bhqk,bhkd->bhqd', attn, v)
        ctx = ctx + jnp.einsum('bhqk,qkd->bhqd', attn, rel)
        out = ctx.transpose(0, 2, 1, 3).reshape(B, L, MODEL_DIM) @ w_o.T
        return out

    def _L1_ffn_ref(x, Wr1, br1, Wr2, br2, Ws1, bs1, Ws2, bs2, We1, be1, We2, be2):
        import jax, jax.numpy as jnp
        import numpy as np
        B, T, C = (2, 64, 128)
        I = 512
        E = 8
        K = 2
        Bb, Tt, Cc = x.shape
        xf = x.reshape(-1, Cc)
        logits = jax.nn.relu(xf @ Wr1 + br1) @ Wr2 + br2
        gates = jax.nn.softmax(logits, axis=-1)
        tg, ti = jax.lax.top_k(gates, K)
        tg = jax.nn.softmax(tg / K, axis=-1)
        out = jax.nn.silu(xf @ Ws1 + bs1) @ Ws2 + bs2
        for e in range(E):
            h = jax.nn.silu(xf @ We1[e] + be1[e]) @ We2[e] + be2[e]
            w = jnp.sum(tg * (ti == e), axis=-1)
            out = out + w[:, None] * h
        return out.reshape(Bb, Tt, Cc)
    x = L0_attn_x
    mod = (_silu(L0_c) @ L0_wmod).reshape(L0_c.shape[0], 6, 1, -1)
    sa, ca, ga, sb, cb, gb = (mod[:, 0], mod[:, 1], mod[:, 2], mod[:, 3], mod[:, 4], mod[:, 5])
    ga = (2 * (ga >= 0) - 1) * jnp.maximum(jnp.abs(ga), 0.25)
    gb = (2 * (gb >= 0) - 1) * jnp.maximum(jnp.abs(gb), 0.25)
    h = _layernorm(x, axis=-1) * (1 + ca) + sa
    x = x + ga * _L0_attn_ref(h, L0_attn_A, L0_attn_W_b, L0_attn_b_b, L0_attn_W_c, L0_attn_b_c, L0_attn_D, L0_attn_W_t, L0_attn_b_t, L0_attn_W_o, L0_attn_b_o)
    h = _layernorm(x, axis=-1) * (1 + cb) + sb
    x = x + gb * _L0_ffn_ref(h, L0_ffn_gate_weight, L0_ffn_gate_up_proj, L0_ffn_down_proj, L0_ffn_similarity_matrix)
    mod = (_silu(L1_c) @ L1_wmod).reshape(L1_c.shape[0], 6, 1, -1)
    sa, ca, ga, sb, cb, gb = (mod[:, 0], mod[:, 1], mod[:, 2], mod[:, 3], mod[:, 4], mod[:, 5])
    ga = (2 * (ga >= 0) - 1) * jnp.maximum(jnp.abs(ga), 0.25)
    gb = (2 * (gb >= 0) - 1) * jnp.maximum(jnp.abs(gb), 0.25)
    h = _layernorm(x, axis=-1) * (1 + ca) + sa
    x = x + ga * _L1_attn_ref(h, L1_attn_w_q, L1_attn_w_k, L1_attn_w_v, L1_attn_w_o, L1_attn_rel_emb)
    h = _layernorm(x, axis=-1) * (1 + cb) + sb
    x = x + gb * _L1_ffn_ref(h, L1_ffn_Wr1, L1_ffn_br1, L1_ffn_Wr2, L1_ffn_br2, L1_ffn_Ws1, L1_ffn_bs1, L1_ffn_Ws2, L1_ffn_bs2, L1_ffn_We1, L1_ffn_be1, L1_ffn_We2, L1_ffn_be2)
    return x

_drawn_inputs = setup_inputs


def setup_inputs(seed=0):
    import zlib

    import numpy as np

    out = dict(_drawn_inputs(seed))
    spreads = {'L0_attn_b_b': (0.0, 0.1),
     'L0_attn_b_c': (0.0, 0.437),
     'L0_attn_D': (1.0, 0.2),
     'L0_attn_b_o': (0.0, 0.33),
     'L1_ffn_br1': (0.0, 0.8),
     'L1_ffn_br2': (0.0, 0.337),
     'L1_ffn_bs1': (0.0, 0.8),
     'L1_ffn_bs2': (0.0, 0.39),
     'L1_ffn_be1': (0.0, 0.8),
     'L1_ffn_be2': (0.0, 0.454)}
    factors = {'L0_attn_A': 2.986,
     'L0_ffn_gate_weight': 8.0,
     'L0_ffn_gate_up_proj': 8.0,
     'L0_ffn_down_proj': 8.0,
     'L1_attn_w_q': 8.0,
     'L1_attn_w_k': 8.0,
     'L1_attn_w_v': 8.0,
     'L1_attn_w_o': 8.0,
     'L1_attn_rel_emb': 8.0,
     'L1_ffn_Wr1': 6.506,
     'L1_ffn_Wr2': 5.246,
     'L1_ffn_Ws1': 4.683,
     'L1_ffn_Ws2': 4.337,
     'L1_ffn_We1': 6.677,
     'L1_ffn_We2': 6.103}
    for name, (base, spread) in spreads.items():
        noise = np.random.default_rng([zlib.crc32(name.encode()), seed]).standard_normal(out[name].shape)
        drawn = base * np.exp(spread * noise) if base else spread * noise
        out[name] = jnp.asarray(drawn.astype(out[name].dtype))
    for name, factor in factors.items():
        out[name] = (out[name] * factor).astype(out[name].dtype)
    return out
```

```python
from contextlib import ExitStack

import concourse.bass as bass
from concourse import mybir

F32 = mybir.dt.float32
BF16 = mybir.dt.bfloat16
ALU = mybir.AluOpType
ACT = mybir.ActivationFunctionType
AX = mybir.AxisListType.X

P = 128
B, S, D = 16, 256, 128
TOK = B * S
NT = TOK // P
CH = 512
NC = TOK // CH
TPC = CH // P
N = 16
H, HD = 16, 8
REL = 32
EPS = 1e-5
NEG = -1e18
E = 8
F0 = 128
I1 = 512
KB1 = I1 // P
THRESHOLD = 0.7
NP = B // 2
HS = 2 * H
X0 = 160
QB = X0 + P
RING = 3
VW = HD + 1
LOWEST = -3e38
W1W = I1 + I1 + KB1


def build(nc, A, out):
    ctx = ExitStack()
    with ctx:
        def sb(name, shape, dt=F32):
            return ctx.enter_context(nc.sbuf_tensor("sb_" + name, shape, dt))

        def sem(name):
            return ctx.enter_context(nc.semaphore(name))

        bank = [ctx.enter_context(nc.psum_tensor(f"bank{i}", [P, 512], F32)) for i in range(8)]

        def scratch(name, shape, dt=F32):
            return nc.dram_tensor(name, shape, dt).ap()

        X = sb("X", [P, NT, D])
        GATE = sb("GATE", [P, 2, B, D])
        ident = sb("ident", [P, P])
        identb = sb("identb", [P, P], BF16)
        ones = sb("ones", [P, P])
        cT = sb("cT", [P, 2, B])
        scT = sb("scT", [P, 2, B])
        MOD = sb("MOD", [P, 2, 6, B])
        GG = sb("GG", [B, 4, D])
        GT1 = sb("GT1", [B, 4, D])
        ST = sb("ST", [P, NT, 6])
        MV = sb("MV", [P, NT, 2])
        RSTD = sb("RSTD", [P, NT])
        SD = sb("SD", [P, NT])
        XN = sb("XN", [P, 2, TPC, D])
        epsc = sb("epsc", [P, 1])
        TMP = sb("TMP", [P, 2, CH])
        ARENA = 154 * 1024 // 4
        arena = sb("arena", [P, ARENA])

        class Region:

            def __init__(self, at=0):
                self.at = at

            def take(self, n, dt=F32):
                words = n if dt == F32 else (n + 1) // 2
                v = arena[:, self.at:self.at + words]
                self.at += words
                assert self.at <= ARENA, self.at * 4
                return v if dt == F32 else v.bitcast(BF16)

        R = Region()
        hT = R.take(TOK)
        ACC = R.take(NT * D).rearrange("p (t d) -> p t d", t=NT)
        dense_base = R.at

        R = Region(dense_base)
        wmod = R.take(2 * 6 * D).rearrange("p (l n) -> p l n", l=2)
        WBpad = R.take(240)
        WTpad = R.take(240)
        Wcr = R.take(P)
        WoT = R.take(D)
        M2 = R.take(D)
        small = R.take(16)
        bcol = R.take(1)
        borow = R.take(D)
        crow = R.take(D)
        blockmask = R.take(8)
        ZM = R.take(8 * D).rearrange("p (b o) -> p b o", b=8)
        EZ = R.take(2 * S).rearrange("p (h t) -> p h t", h=2)
        SIG = R.take(2 * S).rearrange("p (h t) -> p h t", h=2)
        AE = R.take(2 * S).rearrange("p (h t) -> p h t", h=2)
        BU = R.take(2 * S).rearrange("p (h t) -> p h t", h=2)
        HSC = R.take(2 * S).rearrange("p (h t) -> p h t", h=2)

        R = Region(dense_base)
        gateT = R.take(E)
        sim = R.take(E * E).rearrange("p (i j) -> p i j", i=E)
        iota = R.take(E)
        NE = NT * E
        def table(n=NE):
            return R.take(n)
        LG, PR, EQ, OH1, OH2, CD, WT = [table().rearrange("p (t e) -> p t e", t=NT) for _ in range(7)]
        m1, m2, ssum, idx, w1, w2 = [table(NT) for _ in range(6)]
        cnt, pm = table(E), table(E)
        sm, smq, smc = [table(E * E).rearrange("p (i j) -> p i j", i=E) for _ in range(3)]
        bs, bj, cnd, emap = [table(E) for _ in range(4)]
        MM = table(E * E).rearrange("p (i j) -> p i j", i=E)
        WD = R.take(NE).rearrange("p (e t) -> p e t", e=E)
        WE = R.take((E + 1) * NT).rearrange("p (e t) -> p e t", e=E + 1)
        wstep = R.take(2 * NT).rearrange("p (s t) -> p s t", s=2)
        moe_base = R.at
        W0 = R.take(2 * 3 * F0).rearrange("p (s n) -> p s n", s=2)
        SG = R.take(2 * CH).rearrange("p (s n) -> p s n", s=2)
        HM0 = R.take(2 * CH).rearrange("p (s n) -> p s n", s=2)
        R = Region(moe_base)
        Wr1 = R.take(32)
        Wr2 = R.take(E)
        br1 = R.take(1)
        RT1 = R.take(2 * CH).rearrange("p (s n) -> p s n", s=2)
        be2 = R.take(D)
        WCT = R.take(2 * CH).rearrange("p (s n) -> p s n", s=2)
        W1 = R.take(2 * W1W).rearrange("p (s n) -> p s n", s=2)
        HM1 = R.take(2 * KB1 * CH).rearrange("p (s k n) -> p s k n", s=2, k=KB1)

        R = Region(dense_base)
        Wqkv = R.take(5 * D).rearrange("p (w n) -> p w n", w=5)
        ropes = R.take(4 * S).rearrange("p (w t) -> p w t", w=4)
        rel0 = R.take(1)
        relv = R.take(HD)
        RT_1 = R.take(2 * CH).rearrange("p (s n) -> p s n", s=2)
        RT_2 = R.take(2 * CH).rearrange("p (s n) -> p s n", s=2)
        QR = R.take(2 * CH).rearrange("p (s n) -> p s n", s=2)
        KR = R.take(2 * CH).rearrange("p (s n) -> p s n", s=2)
        HI = R.take(4 * CH, BF16).rearrange("p (s w n) -> p s w n", s=2, w=2)
        LO = R.take(4 * CH, BF16).rearrange("p (s w n) -> p s w n", s=2, w=2)
        VT = R.take(2 * TPC * H * VW).rearrange("p (s t n) -> p s t n", s=2, t=TPC)

        R = Region(0)
        QG = R.take(HS * S, BF16).rearrange("p (h q) -> p h q", h=HS)
        KG = R.take(HS * S, BF16).rearrange("p (h q) -> p h q", h=HS)
        BH = R.take(HS * QB, BF16).rearrange("p (h q) -> p h q", h=HS)
        BL = R.take(HS * QB, BF16).rearrange("p (h q) -> p h q", h=HS)
        PT0 = R.take(HS * S).rearrange("p (h q) -> p h q", h=HS)
        PT1 = R.take(HS * P).rearrange("p (h q) -> p h q", h=HS)
        relk = R.take(X0 * HD).rearrange("p (x d) -> p x d", d=HD)
        GTf = R.take(X0 + P)
        GTB = R.take(X0 + P, BF16)
        rel0r = R.take(HD)
        rel0c = R.take(1)
        MX0 = R.take(HS * 8).rearrange("p (h b) -> p h b", h=HS)
        MX1 = R.take(HS * 4).rearrange("p (h b) -> p h b", h=HS)
        NM = R.take(2 * 32, BF16).rearrange("p (c n) -> p c n", c=2)
        VS = R.take(TPC * H * VW).rearrange("p (t h v) -> p t h v", t=TPC, h=H)
        CTS = R.take(2 * CH).rearrange("p (s n) -> p s n", s=2)
        RS = R.take(HS * 64).rearrange("p (h i) -> p h i", h=HS)
        half_mask = R.take(1)
        attn_end = R.at

        R = Region(0)
        C1 = R.take(2 * CH).rearrange("p (s n) -> p s n", s=2)
        R1 = R.take(2 * CH).rearrange("p (s n) -> p s n", s=2)
        DN = R.take(2 * CH).rearrange("p (s n) -> p s n", s=2)
        DR = R.take(2 * CH).rearrange("p (s n) -> p s n", s=2)
        CX = R.take(2 * CH).rearrange("p (s n) -> p s n", s=2)
        sel16 = R.take(P)
        woT1 = R.take(D)

        gD = scratch("gates", [4, B, D])
        qD = scratch("q_parts", [2, P, TOK], BF16)
        kD = scratch("k_parts", [2, P, TOK], BF16)
        vD = scratch("v_rows", [TOK, H * VW])
        cD = scratch("context", [P, TOK])
        rD = scratch("context_rel", [P, TOK])
        dD = scratch("denominators", [H, TOK])

        s_const = sem("s_const")
        s_x = sem("s_x")
        s_set = sem("s_set")
        s_cm = sem("s_cm")
        s_mod = sem("s_mod")
        s_gg = sem("s_gg")
        s_gst = sem("s_gst")
        s_gld = sem("s_gld")
        s_dv = sem("s_dv")
        s_mv = sem("s_mv")
        s_sd = sem("s_sd")
        s_xn = sem("s_xn")
        s_tr = sem("s_tr")
        s_hT = sem("s_hT")
        s_m1 = sem("s_m1")
        s_zm = sem("s_zm")
        s_ssm = sem("s_ssm")
        s_ez = sem("s_ez")
        s_sig = sem("s_sig")
        s_ae = sem("s_ae")
        s_hs = sem("s_hs")
        s_y = sem("s_y")
        s_yr = sem("s_yr")
        s_wm = [sem("s_wm0"), sem("s_wm1")]
        s_lg = sem("s_lg")
        s_el = sem("s_el")
        s_cnt = sem("s_cnt")
        s_oh = sem("s_oh")
        s_w = [[sem(f"s_w{m}{k}") for k in range(2)] for m in range(2)]
        s_up = [sem("s_up0"), sem("s_up1")]
        s_act = [sem("s_act0"), sem("s_act1")]
        s_hm = sem("s_hm")
        s_dn = [sem("s_dn0"), sem("s_dn1")]
        s_acc = [sem("s_acc0"), sem("s_acc1")]
        s_ws = [sem("s_ws0"), sem("s_ws1")]
        s_wp = sem("s_wp")
        s_pj = sem("s_pj")
        s_rot = sem("s_rot")
        s_hi = sem("s_hi")
        s_lo = sem("s_lo")
        s_v = sem("s_v")
        s_qst = [sem("s_qst0"), sem("s_qst1")]
        s_tab = sem("s_tab")
        s_tb = sem("s_tb")
        s_in = sem("s_in")
        s_vin = sem("s_vin")
        s_gen = sem("s_gen")
        s_bh = sem("s_bh")
        s_bl = sem("s_bl")
        s_r1 = sem("s_r1")
        s_mx = sem("s_mx")
        s_mc = sem("s_mc")
        s_tm = sem("s_tm")
        s_nm = sem("s_nm")
        s_mr = sem("s_mr")
        s_r2 = sem("s_r2")
        s_ex = sem("s_ex")
        s_pv = sem("s_pv")
        s_pe = sem("s_pe")
        s_rl = sem("s_rl")
        s_re = sem("s_re")
        s_cst = [sem("s_cst0"), sem("s_cst1")]
        s_rst = sem("s_rst")
        s_cin = [sem("s_cin0"), sem("s_cin1")]
        s_wo = sem("s_wo")
        s_dr = sem("s_dr")
        s_db = sem("s_db")
        s_cx = sem("s_cx")
        s_out = sem("s_out")

        block = ctx.enter_context(nc.Block())

        def chunk(ap, c):
            return ap[:, c * CH:(c + 1) * CH]

        def wait(eng, s, v):
            if isinstance(v, int) and v <= 0:
                return
            eng.wait_ge(s, v)

        @block.sync
        def _(sp):
            n = [0]

            def const(dst, src):
                sp.dma_start(dst, src).then_inc(s_const, 16)
                n[0] += 1

            const(cT[:, :, :], A["cT"])
            const(wmod[:, :, :], A["wmod"])
            for c in range(NC):
                sp.dma_start(X[:, c * TPC:(c + 1) * TPC, :],
                             A["x"][c * CH:(c + 1) * CH, :].rearrange("(t p) d -> p t d", p=P)).then_inc(s_x, 16)
            const(ident[:, :], A["ident"])
            const(WBpad[:, 112:128], A["wbT"])
            const(WTpad[:, 112:128], A["wt16"])
            const(Wcr[:, :], A["wc8"])
            const(WoT[:, :], A["woT0"])
            const(small[:, 0:1], A["bb8"])
            const(small[:, 1:2], A["A8"])
            const(small[:, 2:3], A["bt"])
            const(small[:, 3:4], A["Dv"])
            const(bcol[:, :], A["bc"])
            const(borow[0:1, :], A["bo"])
            const(blockmask[:, :], A["blockmask"])
            assert n[0] == 14
            sp.wait_ge(s_gg, 1)
            sp.dma_start(gD.rearrange("g b f -> b g f"), GG[:, :, :]).then_inc(s_gst, 16)
            sp.wait_ge(s_gst, 16)
            sp.dma_start(GATE[:, :, :, :].rearrange("p g b f -> p (g b f)"),
                         gD[0:2].rearrange("g b f -> (g b f)").partition_broadcast(P)).then_inc(s_gld, 16)

            sp.wait_ge(s_yr, NC)
            for dst, src in ((gateT[:, :], A["gateT"]), (sim[:, :, :], A["sim"]), (iota[:, :], A["iota"])):
                sp.dma_start(dst, src).then_inc(s_wm[0], 16)

            def w0_load(e, k):
                sp.dma_start(W0[:, k, :], A["w0"][e]).then_inc(s_w[0][k], 16)

            w0_load(0, 0)
            w0_load(1, 1)
            with sp.Fori(0, E // 2 - 1) as i:
                for k in range(2):
                    sp.wait_ge(s_dn[0], (2 * i + k + 1) * NC)
                    w0_load(2 * i + k + 2, k)

            sp.wait_ge(s_acc[0], E * NC + NC)
            sp.dma_start(GATE[:, :, :, :].rearrange("p g b f -> p (g b f)"),
                         gD[2:4].rearrange("g b f -> (g b f)").partition_broadcast(P)).then_inc(s_gld, 16)
            for dst, src in ((Wqkv[:, :, :], A["wqkv"]), (ropes[:, :, :], A["ropes"]), (rel0[:, :], A["rel0"]),
                             (relv[:, :], A["rel0r"])):
                sp.dma_start(dst, src).then_inc(s_wp, 16)
            for c in range(NC):
                sp.wait_ge(s_hi, 2 * (c + 1))
                sp.wait_ge(s_lo, 2 * (c + 1))
                sp.wait_ge(s_v, c + 1)
                k = c % 2
                for w, dst in ((0, qD), (1, kD)):
                    sp.dma_start(chunk(dst[0], c), HI[:, k, w, :]).then_inc(s_qst[k], 16)
                    sp.dma_start(chunk(dst[1], c), LO[:, k, w, :]).then_inc(s_qst[k], 16)
                sp.dma_start(vD[c * CH:(c + 1) * CH, :].rearrange("(t p) n -> p t n", p=P),
                             VT[:, k, :, :]).then_inc(s_qst[k], 16)
            for k in range(2):
                sp.wait_ge(s_qst[k], 16 * 5 * NC // 2)

            for dst, src in ((relk[:, :, :], A["relk"]), (GTf[0:25, :], A["gt"]), (rel0r[:, :], A["rel0r"]),
                             (rel0c[0:25, :], A["rel0c"]), (half_mask[0:25, :], A["lowrows"])):
                sp.dma_start(dst, src).then_inc(s_tab, 16)
            sp.wait_ge(s_tb, 1)
            sp.dma_start(QG[24:25, :, :], A["onesrow"]).then_inc(s_tab, 16)
            sp.dma_start(KG[25:26, :, :], A["onesrow"]).then_inc(s_tab, 16)

            def load_pair(i, first):
                at = i * CH
                if not first:
                    sp.wait_ge(s_r2, i * 24)
                for r, part in ((0, 0), (8, 0), (16, 1)):
                    sp.dma_start(QG[r:r + 8, :, :].rearrange("d (h s) q -> d h (s q)", h=H),
                                 qD[part, :, bass.ds(at, CH)].rearrange("(h d) t -> d h t", h=H)).then_inc(s_in, 16)
                for r, part in ((0, 0), (8, 1), (16, 0)):
                    sp.dma_start(KG[r:r + 8, :, :].rearrange("d (h s) q -> d h (s q)", h=H),
                                 kD[part, :, bass.ds(at, CH)].rearrange("(h d) t -> d h t", h=H)).then_inc(s_in, 16)
                sp.dma_start(QG[25:26, :, :], A["zerorow"]).then_inc(s_in, 16)

            def load_values(i, first):
                if not first:
                    sp.wait_ge(s_pv, i * 4)
                sp.dma_start(VS[:, :, :, :].rearrange("p t h v -> p t (h v)"),
                             vD[bass.ds(i * CH, CH), :].rearrange("(t p) n -> p t n", p=P)).then_inc(s_vin, 16)

            def move_maxima(i):
                sp.wait_ge(s_nm, i + 1)
                for g in range(2):
                    sp.dma_start(QG[25:26, g * H:(g + 1) * H, :].rearrange("o h q -> o (h q)"),
                                 NM[:, g, :]).then_inc(s_mr, 16)

            def store_pair(i):
                for w in range(4):
                    s, hb = w // 2, w % 2
                    sp.wait_ge(s_pe, i * 4 + w + 1)
                    at = i * CH + s * S
                    for j in range(4):
                        src = CTS[32 * j:32 * j + HD, w % 2, :].rearrange("d (g q) -> d g q", g=2)
                        sp.dma_start(
                            cD.rearrange("(g j d) t -> j d g t", g=4, j=4)[j, :, 2 * hb:2 * hb + 2, bass.ds(at, S)],
                            src).then_inc(s_cst[w % 2], 16)
                        den = CTS[32 * j + HD:32 * j + HD + 1, w % 2, :].rearrange("d (g q) -> d g q", g=2)
                        sp.dma_start(
                            dD.rearrange("(g j d) t -> j d g t", g=4, j=4)[j, :, 2 * hb:2 * hb + 2, bass.ds(at, S)],
                            den).then_inc(s_cst[w % 2], 16)
                sp.wait_ge(s_re, i * 4 + 4)
                for s in range(2):
                    for j in range(4):
                        sp.dma_start(
                            rD.rearrange("(h d) t -> d h t", h=H)[:, :, bass.ds(i * CH + s * S + 64 * j, 64)],
                            RS[32 * j:32 * j + HD, :, :].rearrange("d (h s) i -> d h s i", s=2)[:, :, s, :]
                        ).then_inc(s_rst, 16)

            load_pair(0, True)
            load_values(0, True)
            move_maxima(0)
            with sp.Fori(1, NP) as i:
                load_pair(i, False)
                move_maxima(i)
                load_values(i, False)
                store_pair(i - 1)
            store_pair(NP - 1)

            for s, k in ((s_cst[0], 16 * 16 * NP), (s_cst[1], 16 * 16 * NP), (s_rst, 16 * 8 * NP)):
                sp.wait_ge(s, k)
            sp.dma_start(sel16[0:H, :], A["sel16"]).then_inc(s_wo, 16)
            sp.dma_start(woT1[:, :], A["woT1"]).then_inc(s_wo, 16)
            for c in range(NC):
                if c >= 2:
                    sp.wait_ge(s_cx, c - 1)
                for dst, src in ((C1[:, c % 2, :], cD), (R1[:, c % 2, :], rD), (DN[0:H, c % 2, :], dD)):
                    sp.dma_start(dst, chunk(src, c)).then_inc(s_cin[c % 2], 16)

            sp.wait_ge(s_yr, 2 * NC)
            for dst, src in ((Wr1[:, :], A["wr1"]), (Wr2[0:33, :], A["wr2"]), (br1[0:32, :], A["br1"]),
                             (be2[0:E + 1, :], A["be2"]), (iota[:, :], A["iota"])):
                sp.dma_start(dst, src).then_inc(s_wm[1], 16)

            def w1_load(e, k):
                sp.dma_start(W1[:, k, :], A["w1"][e]).then_inc(s_w[1][k], 16)

            w1_load(0, 0)
            w1_load(1, 1)
            with sp.Fori(0, E // 2 - 1) as i:
                for k in range(2):
                    sp.wait_ge(s_dn[1], (2 * i + k + 1) * NC)
                    w1_load(2 * i + k + 2, k)
            sp.wait_ge(s_dn[1], (E - 1) * NC)
            w1_load(E, 0)
            for c in range(NC):
                sp.wait_ge(s_acc[1], (E + 1) * NC + NC + c + 1)
                sp.dma_start(out[c * CH:(c + 1) * CH, :].rearrange("(t p) d -> p t d", p=P),
                             X[:, c * TPC:(c + 1) * TPC, :]).then_inc(s_out, 16)
            sp.wait_ge(s_out, 16 * NC)

        @block.gpsimd
        def _(pool):
            nc.gpsimd.memset(WBpad[:, 0:112], 0.0)
            nc.gpsimd.memset(WBpad[:, 128:240], 0.0)
            nc.gpsimd.memset(WTpad[:, 0:112], 0.0)
            nc.gpsimd.memset(WTpad[:, 128:240], 0.0)
            nc.gpsimd.memset(ones[:, :], 1.0).then_inc(s_set, 1)

        @block.scalar
        def _(act):
            act.wait_ge(s_const, 16 * 14)
            nc.scalar.activation(scT[:, :, :], cT[:, :, :], ACT.Silu).then_inc(s_cm, 1)

            def layer_norm(n):
                l, first = n // 2, 3 * (n % 2)
                act.wait_ge(s_mv, n + 1)
                nc.scalar.activation(SD[:, :], MV[:, :, 1], ACT.Sqrt, bias=epsc[:, :]).then_inc(s_sd, 1)
                for c in range(NC):
                    act.wait_ge(s_tr, n * NC + c + 1)
                    for s in range(2):
                        b = 2 * c + s
                        ins = nc.scalar.activation(hT[:, b * S:(b + 1) * S], bank[c % 2][:, s * S:(s + 1) * S],
                                                   ACT.Identity, scale=MOD[:, l, first + 1, b:b + 1],
                                                   bias=MOD[:, l, first, b:b + 1])
                    ins.then_inc(s_hT, 1)

            layer_norm(0)
            for h in range(2):
                act.wait_ge(s_ssm, h + 1)
                nc.scalar.activation(EZ[:, h, :], bank[2 + h][:, S:2 * S], ACT.Exp, scale=-1.0,
                                     bias=small[:, 4:5]).then_inc(s_ez, 1)
            for h in range(2):
                act.wait_ge(s_sig, h + 1)
                nc.scalar.activation(AE[:, h, :], SIG[:, h, :], ACT.Exp, scale=small[:, 5:6],
                                     bias=small[:, 6:7]).then_inc(s_ae, 1)

            layer_norm(1)
            act.wait_ge(s_lg, 1)
            nc.scalar.activation(PR[:, :, :], LG[:, :, :], ACT.Exp).then_inc(s_el, 1)

            def moe0(i, first):
                for j in range(2 * NC):
                    u = i * 2 * NC + j
                    act.wait_ge(s_up[0], u + 1)
                    wait(act, s_hm, u - 1)
                    nc.scalar.activation(SG[:, j % 2, :], bank[j % 2][:, :], ACT.Silu).then_inc(s_act[0], 1)

            moe0(0, True)
            with act.Fori(1, E // 2) as i:
                moe0(i, False)

            layer_norm(2)
            for c in range(NC):
                k = c % 2
                if c >= 2:
                    act.wait_ge(s_qst[k], 16 * 5 * (c // 2))
                for w, src in ((0, QR), (1, KR)):
                    act.wait_ge(s_rot, 6 * c + 3 * w + 3)
                    nc.scalar.copy(HI[:, k, w, :], src[:, k, :]).then_inc(s_hi, 1)

            def bias_high(i):
                if not (isinstance(i, int) and i == 0):
                    act.wait_ge(s_r2, i * 24)
                for g in range(18):
                    act.wait_ge(s_gen, i * 18 + g + 1)
                    at = g * 16
                    nc.scalar.copy(BH[:, :, at:at + 16].rearrange("p h q -> p q h"),
                                   bank[g % RING][:, :].rearrange("p (q h) -> p q h", h=HS)).then_inc(s_bh, 1)

            def exponentials(i):
                for r in range(24):
                    act.wait_ge(s_r2, i * 24 + r + 1)
                    dst = PT0[:, 2 * r:2 * r + 2, :] if r < 16 else PT1[:, 4 * (r - 16):4 * (r - 16) + 4, :]
                    q = S if r < 16 else P
                    nc.scalar.activation(dst, bank[r % RING][:, :].rearrange("p (h q) -> p h q", q=q),
                                         ACT.Exp).then_inc(s_ex, 1)

            def values_out(i):
                for w in range(4):
                    act.wait_ge(s_pv, i * 4 + w + 1)
                    v = 128 * (2 * i + w // 2)
                    wait(act, s_cst[w % 2], v)
                    nc.scalar.copy(CTS[:, w % 2, :], bank[3 + w % 2][:, :]).then_inc(s_pe, 1)

            bias_high(0)
            exponentials(0)
            with act.Fori(1, NP) as i:
                bias_high(i)
                values_out(i - 1)
                exponentials(i)
            values_out(NP - 1)

            layer_norm(3)
            act.wait_ge(s_lg, 2)
            nc.scalar.activation(PR[:, :, :], LG[:, :, :], ACT.Exp).then_inc(s_el, 1)
            act.wait_ge(s_lg, 3)
            nc.scalar.activation(w2[:, :], m2[:, :], ACT.Exp).then_inc(s_el, 1)

            def moe1_unit(u, k):
                act.wait_ge(s_dn[1], u - 1) if not isinstance(u, int) or u >= 2 else None
                for b in range(KB1):
                    act.wait_ge(s_up[1], u * KB1 + b + 1)
                    nc.scalar.activation(HM1[:, u_slot[0], b, :], bank[b][:, :], ACT.Silu,
                                         bias=W1[:, k, 2 * I1 + b:2 * I1 + b + 1]).then_inc(s_act[1], 1)

            u_slot = [0]
            for c in range(NC):
                u_slot[0] = c % 2
                moe1_unit(c, 0)
            with act.Fori(0, E // 2) as i:
                for j in range(2 * NC):
                    u_slot[0] = j % 2
                    moe1_unit(i * 2 * NC + NC + j, 1 - j // NC)

        @block.vector
        def _(dve):
            chain = [0]

            def link(ins):
                chain[0] += 1
                ins.then_inc(s_dv, 1)
                dve.wait_ge(s_dv, chain[0])

            v = nc.vector
            v.memset(epsc[:, :], EPS)
            for i in range(8):
                link(v.memset(bank[i][:, :], 0.0))
            dve.wait_ge(s_const, 16 * 14)
            v.tensor_copy(identb[:, :], ident[:, :])
            v.tensor_scalar(small[:, 4:5], small[:, 2:3], -1.0, None, ALU.mult)
            v.tensor_scalar(small[:, 5:6], small[:, 1:2], 0.99, None, ALU.mult)
            v.tensor_scalar(small[:, 6:7], small[:, 1:2], 0.01, None, ALU.mult)
            link(v.tensor_scalar(M2[:, :], WoT[:, :], small[:, 3:4], None, ALU.mult))

            dve.wait_ge(s_mod, 1)
            link(v.tensor_copy(MOD[:, :, :, :].rearrange("p l m b -> p (l m b)"), bank[0][:, 0:2 * 6 * B]))
            for m in (1, 4):
                link(v.tensor_scalar(MOD[:, :, m, :], MOD[:, :, m, :], 1.0, None, ALU.add))
            gsrc = bank[1][0:B, :].rearrange("p (g f) -> p g f", g=4)
            v.tensor_scalar(GT1[:, :, :], gsrc, 0.0, 2.0, ALU.is_ge, ALU.mult)
            link(v.tensor_scalar(GG[:, :, :], gsrc, -1.0, None, ALU.mult))
            link(v.scalar_tensor_tensor(out=GG[:, :, :].rearrange("p g f -> p (g f)"),
                                        in0=GG[:, :, :].rearrange("p g f -> p (g f)"), scalar=0.25,
                                        in1=bank[1][0:B, :], op0=ALU.max, op1=ALU.max))
            ins = v.scalar_tensor_tensor(out=GG[:, :, :].rearrange("p g f -> p (g f)"),
                                         in0=GT1[:, :, :].rearrange("p g f -> p (g f)"), scalar=-1.0,
                                         in1=GG[:, :, :].rearrange("p g f -> p (g f)"), op0=ALU.add, op1=ALU.mult)
            ins.then_inc(s_gg, 1)
            dve.wait_ge(s_m1, 1)
            for b in range(8):
                v.tensor_scalar(ZM[:, b, :], bank[4][:, 0:D], blockmask[:, b:b + 1], None, ALU.mult)
            v.tensor_tensor(crow[0:1, :], bank[5][0:1, 0:D], borow[0:1, :], ALU.add).then_inc(s_zm, 1)

            def layer_norm(n):
                for t in range(NT):
                    if n == 0 and t % TPC == 0:
                        dve.wait_ge(s_x, 16 * NC)
                    ins = v.bn_stats(ST[:, t, :], X[:, t, :])
                link(ins)
                for t in range(NT):
                    ins = v.bn_aggr(MV[:, t, :], ST[:, t, :])
                ins.then_inc(s_mv, 1)
                dve.wait_ge(s_sd, n + 1)
                link(v.reciprocal(RSTD[:, :], SD[:, :]))
                for c in range(NC):
                    wait(dve, s_tr, n * NC + c - 1)
                    for t in range(TPC):
                        T = c * TPC + t
                        ins = v.tensor_scalar(XN[:, c % 2, t, :], X[:, T, :], MV[:, T, 0:1], RSTD[:, T:T + 1],
                                              ALU.subtract, ALU.mult)
                    ins.then_inc(s_xn, 1)

            def add_gated(c, src, g, done):
                t4 = TMP[:, c % 2, :].rearrange("p (b t f) -> p b t f", b=2, t=2)
                for b in range(2):
                    gate = GATE[:, g, 2 * c + b, :].unsqueeze(1).to_broadcast([P, 2, D])
                    ins = v.tensor_tensor(t4[:, b], src[:, b], gate, ALU.mult)
                link(ins)
                xs = X[:, c * TPC:(c + 1) * TPC, :].rearrange("p t f -> p (t f)")
                ins = v.tensor_tensor(xs, xs, TMP[:, c % 2, :], ALU.add)
                ins.then_inc(done, 1)

            layer_norm(0)
            for h in range(2):
                dve.wait_ge(s_ez, h + 1)
                link(v.tensor_scalar(SIG[:, h, :], EZ[:, h, :], 1.0, None, ALU.add))
                v.reciprocal(SIG[:, h, :], SIG[:, h, :]).then_inc(s_sig, 1)
            for h in range(2):
                link(v.tensor_scalar(BU[:, h, :], bank[2 + h][:, 0:S], small[:, 0:1], None, ALU.add))
                dve.wait_ge(s_ae, h + 1)
                v.tensor_tensor_scan(HSC[:, h, :], AE[:, h, :], BU[:, h, :], 0.0, ALU.mult, ALU.add).then_inc(s_hs, 1)
            dve.wait_ge(s_gld, 16)
            for c in range(NC):
                dve.wait_ge(s_y, c + 1)
                add_gated(c, bank[6 + c % 2][:, :].rearrange("p (b t f) -> p b t f", b=2, t=2), 0, s_yr)
            dve.wait_ge(s_yr, NC)

            def bc_e(a):
                return a.unsqueeze(2).to_broadcast([P, NT, E])

            iota3 = iota[:, :].unsqueeze(1).to_broadcast([P, NT, E])

            def pick(values, best, onehot):
                link(v.tensor_reduce(best, values, AX, ALU.max))
                link(v.tensor_tensor(EQ[:, :, :], values, bc_e(best), ALU.is_lt))
                link(v.tensor_scalar(EQ[:, :, :], EQ[:, :, :], float(E), None, ALU.mult))
                link(v.tensor_tensor(EQ[:, :, :], EQ[:, :, :], iota3, ALU.add))
                link(v.tensor_reduce(idx[:, :], EQ[:, :, :], AX, ALU.min))
                return v.tensor_tensor(onehot, iota3, bc_e(idx[:, :]), ALU.is_equal)

            def softmax_shift(m):
                lg = bank[2][:, 0:NE].rearrange("p (t e) -> p t e", t=NT)
                link(v.tensor_reduce(m1[:, :], lg, AX, ALU.max))
                v.tensor_tensor(LG[:, :, :], lg, bc_e(m1[:, :]), ALU.subtract).then_inc(s_lg, 1)

            def softmax_end():
                link(v.tensor_reduce(ssum[:, :], PR[:, :, :], AX, ALU.add))
                link(v.reciprocal(ssum[:, :], ssum[:, :]))
                link(v.tensor_tensor(PR[:, :, :], PR[:, :, :], bc_e(ssum[:, :]), ALU.mult))

            def second(m):
                link(v.tensor_tensor(CD[:, :, :], PR[:, :, :], OH1[:, :, :], ALU.subtract))
                link(v.scalar_tensor_tensor(out=CD[:, :, :], in0=OH1[:, :, :], scalar=-4.0, in1=CD[:, :, :],
                                            op0=ALU.mult, op1=ALU.add))
                link(pick(CD[:, :, :], m, OH2[:, :, :]))

            layer_norm(1)
            dve.wait_ge(s_wm[0], 16 * 3)
            dve.wait_ge(s_cnt, 1)
            softmax_shift(0)
            dve.wait_ge(s_el, 1)
            softmax_end()
            link(pick(PR[:, :, :], m1[:, :], OH1[:, :, :]))
            v.tensor_reduce(cnt[:, :], OH1[:, :, :].rearrange("p t e -> p e t"), AX, ALU.add).then_inc(s_oh, 1)
            second(m2[:, :])
            link(v.tensor_tensor(ssum[:, :], m1[:, :], m2[:, :], ALU.add))
            link(v.tensor_scalar(ssum[:, :], ssum[:, :], 1e-12, None, ALU.max))
            link(v.reciprocal(ssum[:, :], ssum[:, :]))
            v.tensor_tensor(w1[:, :], m1[:, :], ssum[:, :], ALU.mult)
            link(v.tensor_tensor(w2[:, :], m2[:, :], ssum[:, :], ALU.mult))
            v.tensor_tensor(OH1[:, :, :], OH1[:, :, :], bc_e(w1[:, :]), ALU.mult)
            link(v.tensor_tensor(OH2[:, :, :], OH2[:, :, :], bc_e(w2[:, :]), ALU.mult))
            link(v.tensor_tensor(WT[:, :, :], OH1[:, :, :], OH2[:, :, :], ALU.add))
            dve.wait_ge(s_cnt, 2)
            link(v.tensor_scalar(pm[:, :], bank[3][:, 0:E], 0.5, None, ALU.is_ge))
            pmj = pm[:, :].unsqueeze(1).to_broadcast([P, E, E])
            link(v.tensor_scalar(smq[:, :, :], pmj, 1.0, -LOWEST, ALU.subtract, ALU.mult))
            link(v.tensor_tensor(sm[:, :, :], sim[:, :, :], pmj, ALU.mult))
            link(v.tensor_tensor(sm[:, :, :], sm[:, :, :], smq[:, :, :], ALU.add))
            link(v.tensor_reduce(bs[:, :], sm[:, :, :], AX, ALU.max))
            link(v.tensor_tensor(smc[:, :, :], sm[:, :, :], bs[:, :].unsqueeze(2).to_broadcast([P, E, E]), ALU.is_lt))
            link(v.tensor_scalar(smc[:, :, :], smc[:, :, :], float(E), None, ALU.mult))
            iotaj = iota[:, :].unsqueeze(1).to_broadcast([P, E, E])
            link(v.tensor_tensor(smc[:, :, :], smc[:, :, :], iotaj, ALU.add))
            link(v.tensor_reduce(bj[:, :], smc[:, :, :], AX, ALU.min))
            link(v.tensor_scalar(cnd[:, :], bs[:, :], THRESHOLD, None, ALU.is_ge))
            link(v.scalar_tensor_tensor(out=cnd[:, :], in0=pm[:, :], scalar=0.5, in1=cnd[:, :],
                                        op0=ALU.is_lt, op1=ALU.mult))
            link(v.tensor_tensor(bj[:, :], bj[:, :], iota[:, :], ALU.subtract))
            link(v.tensor_tensor(bj[:, :], bj[:, :], cnd[:, :], ALU.mult))
            link(v.tensor_tensor(emap[:, :], bj[:, :], iota[:, :], ALU.add))
            link(v.tensor_tensor(MM[:, :, :], emap[:, :].unsqueeze(2).to_broadcast([P, E, E]), iotaj, ALU.is_equal))
            for i in range(E):
                wi = WT[:, :, i].unsqueeze(1).to_broadcast([P, E, NT])
                mi = MM[:, i, :].unsqueeze(2).to_broadcast([P, E, NT])
                dst = WD if i == 0 else CD.rearrange("p t e -> p (t e)").rearrange("p (e t) -> p e t", e=E)
                link(v.tensor_tensor(dst[:, :, :], wi, mi, ALU.mult))
                if i:
                    link(v.tensor_tensor(WD[:, :, :], WD[:, :, :], dst[:, :, :], ALU.add))
            link(v.memset(ACC[:, :, :], 0.0))

            def accumulate(m, u, j, src):
                c = j % NC
                dve.wait_ge(s_dn[m], u + 1)
                wait(dve, s_acc[m], u - NC + 1 + (NC if m else 0))
                for t in range(TPC):
                    T = c * TPC + t
                    ins = v.scalar_tensor_tensor(out=ACC[:, T, :], in0=src[:, t * D:(t + 1) * D],
                                                 scalar=wstep[:, (j // NC) % 2, T:T + 1], in1=ACC[:, T, :],
                                                 op0=ALU.mult, op1=ALU.add)
                ins.then_inc(s_acc[m], 1)

            def step_weights(m, i, table, e0, n):
                wait(dve, s_acc[m], e0)
                ins = v.tensor_copy(wstep[:, 0:n, :], table)
                ins.then_inc(s_ws[m], 1)

            def moe0(i):
                step_weights(0, i, WD[:, bass.ds(2 * i, 2), :], i * 2 * NC, 2)
                dve.wait_ge(s_ws[0], i + 1)
                for j in range(2 * NC):
                    u = i * 2 * NC + j
                    dve.wait_ge(s_act[0], u + 1)
                    wait(dve, s_dn[0], u - 1)
                    v.tensor_tensor(HM0[:, j % 2, :], SG[:, j % 2, :], bank[2 + j % 2][:, :], ALU.mult).then_inc(s_hm, 1)
                    if j:
                        accumulate(0, u - 1, j - 1, bank[4 + (j - 1) % 2])
                accumulate(0, u, 2 * NC - 1, bank[4 + 1])

            moe0(0)
            with dve.Fori(1, E // 2) as i:
                moe0(i)
            dve.wait_ge(s_acc[0], E * NC)
            for c in range(NC):
                add_gated(c, ACC[:, c * TPC:(c + 1) * TPC, :].rearrange("p (b t) f -> p b t f", b=2), 1, s_acc[0])
            dve.wait_ge(s_acc[0], E * NC + NC)

            layer_norm(2)
            dve.wait_ge(s_wp, 16 * 4)
            link(v.memset(VT[:, :, :, :], 1.0))
            for c in range(NC):
                k = c % 2
                for w in range(2):
                    rope = [ropes[:, 2 * w + r, :].unsqueeze(1).to_broadcast([P, 2, S]) for r in range(2)]
                    r1, r2 = ((RT_1[:, k, :], RT_2[:, k, :]))
                    if w == 1 or c:
                        dve.wait_ge(s_rot, 6 * c + 3 * w)
                    dve.wait_ge(s_pj, 5 * c + 2 * w + 1)
                    v.tensor_tensor(r1.rearrange("p (s t) -> p s t", s=2),
                                    bank[2 * w][:, :].rearrange("p (s t) -> p s t", s=2), rope[0], ALU.mult
                                    ).then_inc(s_rot, 1)
                    dve.wait_ge(s_pj, 5 * c + 2 * w + 2)
                    v.tensor_tensor(r2.rearrange("p (s t) -> p s t", s=2),
                                    bank[2 * w + 1][:, :].rearrange("p (s t) -> p s t", s=2), rope[1], ALU.mult
                                    ).then_inc(s_rot, 1)
                    dve.wait_ge(s_rot, 6 * c + 3 * w + 2)
                    if w == 0:
                        v.tensor_tensor(QR[:, k, :], r1, r2, ALU.add).then_inc(s_rot, 1)
                    else:
                        v.scalar_tensor_tensor(out=KR[:, k, :], in0=r1, scalar=rel0[:, 0:1], in1=r2,
                                               op0=ALU.add, op1=ALU.add).then_inc(s_rot, 1)
                if c >= 2:
                    dve.wait_ge(s_qst[k], 16 * 5 * (c // 2))
                dve.wait_ge(s_pj, 5 * c + 5)
                for t in range(TPC):
                    ins = v.tensor_tensor(VT[:, k, t, :].rearrange("p (h v) -> p h v", v=VW)[:, :, 0:HD],
                                          bank[4][:, t * D:(t + 1) * D].rearrange("p (h v) -> p h v", v=HD),
                                          relv[:, :].unsqueeze(1).to_broadcast([P, H, HD]), ALU.add)
                ins.then_inc(s_v, 1)
                dve.wait_ge(s_rot, 6 * c + 6)
                for w, src in ((0, QR), (1, KR)):
                    dve.wait_ge(s_hi, 2 * c + w + 1)
                    v.tensor_tensor(LO[:, k, w, :], src[:, k, :], HI[:, k, w, :], ALU.subtract).then_inc(s_lo, 1)

            for k in range(2):
                dve.wait_ge(s_qst[k], 16 * 5 * NC // 2)
            v.memset(QG[:, :, :].bitcast(F32), 0.0)
            v.memset(KG[:, :, :].bitcast(F32), 0.0).then_inc(s_tb, 1)
            link(v.memset(GTB[:, :], 0.0))
            dve.wait_ge(s_tab, 16 * 7)
            v.tensor_tensor(relk[:, :, :], relk[:, :, :], rel0r[:, :].unsqueeze(1).to_broadcast([P, X0, HD]), ALU.subtract)
            link(v.tensor_scalar(GTf[0:25, :], GTf[0:25, :], rel0c[0:25, :], None, ALU.subtract))
            link(v.tensor_copy(GTB[0:25, :], GTf[0:25, :]))
            link(v.tensor_tensor(GTf[0:25, :], GTf[0:25, :], GTB[0:25, :], ALU.subtract))
            link(v.tensor_scalar(GTf[0:25, :], GTf[0:25, :], half_mask[0:25, :], None, ALU.mult))
            link(v.tensor_scalar(rel0c[0:25, :], half_mask[0:25, :], -1.0, 1.0, ALU.mult, ALU.add))
            v.scalar_tensor_tensor(out=GTB[0:25, :], in0=GTB[0:25, :], scalar=rel0c[0:25, :], in1=GTf[0:25, :],
                                   op0=ALU.mult, op1=ALU.add).then_inc(s_tb, 1)

            def bias_low(i):
                for g in range(18):
                    dve.wait_ge(s_bh, i * 18 + g + 1)
                    at = g * 16
                    v.tensor_tensor(BL[:, :, at:at + 16].rearrange("p h q -> p q h"),
                                    bank[g % RING][:, :].rearrange("p (q h) -> p q h", h=HS),
                                    BH[:, :, at:at + 16].rearrange("p h q -> p q h"), ALU.subtract).then_inc(s_bl, 1)

            def maxima(i):
                for r in range(24):
                    dve.wait_ge(s_r1, i * 24 + r + 1)
                    dst = MX0[:, 2 * r:2 * r + 2, :] if r < 16 else MX1[:, 4 * (r - 16):4 * (r - 16) + 4, :]
                    v.tensor_reduce(dst.rearrange("p h b -> p (h b)"),
                                    bank[r % RING][:, :].rearrange("p (b c) -> p b c", c=32), AX, ALU.max,
                                    apply_transpose=True).then_inc(s_mx, 1)
                dve.wait_ge(s_mx, (i + 1) * 24)
                v.tensor_tensor(MX0[:, :, 4:8], MX0[:, :, 4:8], MX1[:, :, :], ALU.max).then_inc(s_mc, 1)

            def row_maxima(i):
                dve.wait_ge(s_tm, i + 1)
                wait(dve, s_mr, i * 32)
                v.tensor_reduce(NM[:, :, :], bank[7][:, 0:2 * P].rearrange("p (h g c) -> p h c g", h=2, g=4),
                                AX, ALU.max, negate=True).then_inc(s_nm, 1)

            def relative_out(i):
                for w in range(4):
                    dve.wait_ge(s_rl, i * 4 + w + 1)
                    if w == 0:
                        wait(dve, s_rst, i * 16 * 8)
                    v.tensor_copy(RS[:, :, 16 * w:16 * w + 16].rearrange("p h i -> p i h"),
                                  bank[5 + w % 2][:, :].rearrange("p (i h) -> p i h", h=HS)).then_inc(s_re, 1)

            bias_low(0)
            maxima(0)
            row_maxima(0)
            with dve.Fori(1, NP) as i:
                bias_low(i)
                maxima(i)
                row_maxima(i)
                relative_out(i - 1)
            relative_out(NP - 1)

            dve.wait_ge(s_gld, 32)
            for c in range(NC + 1):
                if c < NC:
                    k = c % 2
                    dve.wait_ge(s_cin[k], 48 * (c // 2 + 1))
                    wait(dve, s_db, c - 1)
                    v.reciprocal(DR[0:H, k, :], DN[0:H, k, :]).then_inc(s_dr, 1)
                    link(v.tensor_tensor(C1[:, k, :], C1[:, k, :], R1[:, k, :], ALU.add))
                    dve.wait_ge(s_db, c + 1)
                    wait(dve, s_y, NC + c - 1)
                    v.tensor_tensor(CX[:, k, :], C1[:, k, :], bank[k][:, :], ALU.mult).then_inc(s_cx, 1)
                if c:
                    dve.wait_ge(s_y, NC + c)
                    add_gated(c - 1, bank[6 + (c - 1) % 2][:, :].rearrange("p (b t f) -> p b t f", b=2, t=2), 0, s_yr)
            dve.wait_ge(s_yr, 2 * NC)

            layer_norm(3)
            dve.wait_ge(s_wm[1], 16 * 5)
            link(v.memset(RT1[32:33, :, :], 1.0))
            for c in range(NC):
                dve.wait_ge(s_cnt, 3 + c)
                wait(dve, s_m1, 1 + c - 1)
                v.tensor_scalar(RT1[0:32, c % 2, :], bank[3 + c % 2][0:32, :], br1[0:32, :], 0.0, ALU.add, ALU.max
                                ).then_inc(s_oh, 1)
            dve.wait_ge(s_m1, 1 + NC)
            softmax_shift(1)
            dve.wait_ge(s_el, 2)
            softmax_end()
            link(pick(PR[:, :, :], m1[:, :], OH1[:, :, :]))
            second(m2[:, :])
            link(v.tensor_tensor(m2[:, :], m2[:, :], m1[:, :], ALU.subtract))
            v.tensor_scalar(m2[:, :], m2[:, :], 0.5, None, ALU.mult).then_inc(s_lg, 1)
            dve.wait_ge(s_el, 3)
            link(v.tensor_scalar(ssum[:, :], w2[:, :], 1.0, None, ALU.add))
            link(v.reciprocal(w1[:, :], ssum[:, :]))
            link(v.tensor_tensor(w2[:, :], w2[:, :], w1[:, :], ALU.mult))
            v.tensor_tensor(OH1[:, :, :], OH1[:, :, :], bc_e(w1[:, :]), ALU.mult)
            link(v.tensor_tensor(OH2[:, :, :], OH2[:, :, :], bc_e(w2[:, :]), ALU.mult))
            v.memset(WE[:, 0, :], 1.0)
            link(v.tensor_tensor(WE[:, 1:, :].rearrange("p e t -> p t e"), OH1[:, :, :], OH2[:, :, :], ALU.add))
            v.tensor_copy(idx[:, :], w1[:, :]).then_inc(s_lg, 1)
            for c in range(NC):
                dve.wait_ge(s_ssm, 2 + 2 * c + 1)
                v.tensor_copy(WCT[0:E + 1, c % 2, :], bank[c % 2][0:E + 1, :]).then_inc(s_hs, 1)
                dve.wait_ge(s_ssm, 2 + 2 * c + 2)
                v.tensor_copy(ACC[:, c * TPC:(c + 1) * TPC, :].rearrange("p t f -> p (t f)"), bank[2 + c % 2][:, :]
                              ).then_inc(s_acc[1], 1)

            def moe1(i, e, n, u0):
                for j in range(n * NC):
                    if j == 0:
                        wait(dve, s_acc[1], NC + u0)
                        v.tensor_copy(wstep[:, 0:n, :], WE[:, e, :] if n == 1 else WE[:, bass.ds(e, n), :]
                                      ).then_inc(s_ws[1], 1)
                        dve.wait_ge(s_ws[1], i + 1)
                    accumulate(1, u0 + j, j, bank[4 + j % 2])

            moe1(0, 0, 1, 0)
            with dve.Fori(0, E // 2) as i:
                moe1(i + 1, 2 * i + 1, 2, NC + i * 2 * NC)
            dve.wait_ge(s_acc[1], (E + 1) * NC + NC)
            for c in range(NC):
                add_gated(c, ACC[:, c * TPC:(c + 1) * TPC, :].rearrange("p (b t) f -> p b t f", b=2), 1, s_acc[1])

        @block.tensor
        def _(pe):
            mm = nc.tensor.matmul

            pe.wait_ge(s_cm, 1)
            pe.wait_ge(s_set, 1)
            pe.wait_ge(s_dv, 8)
            for l in range(2):
                for m in range(6):
                    at = (l * 6 + m) * B
                    mm(bank[0][:, at:at + B], wmod[:, l, m * D:(m + 1) * D], scT[:, l, :], start=True, stop=True)
            for l in range(2):
                for g, m in ((0, 2), (1, 5)):
                    at = (2 * l + g) * D
                    ins = mm(bank[1][0:B, at:at + D], scT[:, l, :], wmod[:, l, m * D:(m + 1) * D], start=True, stop=True)
            ins.then_inc(s_mod, 1)
            mm(bank[4][:, 0:D], Wcr[:, :], WoT[:, :], start=True, stop=True)
            mm(bank[5][0:1, 0:D], bcol[:, :], WoT[:, :], start=True, stop=True).then_inc(s_m1, 1)

            def layer_norm(n):
                for c in range(NC):
                    pe.wait_ge(s_xn, n * NC + c + 1)
                    wait(pe, s_hT, n * NC + c - 1)
                    if n == 0 and c == 0:
                        pe.wait_ge(s_gg, 1)
                    for t in range(TPC):
                        ins = nc.tensor.transpose(bank[c % 2][:, t * P:(t + 1) * P], XN[:, c % 2, t, :], ident[:, :])
                    ins.then_inc(s_tr, 1)

            layer_norm(0)
            for h in range(2):
                pe.wait_ge(s_hT, (h + 1) * NC // 2)
                for pad, at in ((WTpad, S), (WBpad, 0)):
                    for b in range(8):
                        ins = mm(bank[2 + h][:, at:at + S], pad[:, 112 - N * b:240 - N * b],
                                 hT[:, (8 * h + b) * S:(8 * h + b + 1) * S], start=(b == 0), stop=(b == 7))
                ins.then_inc(s_ssm, 1)
            pe.wait_ge(s_zm, 1)
            for c in range(NC):
                pe.wait_ge(s_hs, c // 4 + 1)
                wait(pe, s_yr, c - 1)
                for t in range(TPC):
                    T = c * TPC + t
                    b = T // 2
                    dst = bank[6 + c % 2][:, t * D:(t + 1) * D]
                    at = (T % 2) * P
                    mm(dst, HSC[:, b // 8, at:at + P], ZM[:, b % 8, :], start=True, stop=False)
                    mm(dst, hT[:, T * P:(T + 1) * P], M2[:, :], start=False, stop=False)
                    ins = mm(dst, ones[0:1, :], crow[0:1, :], start=False, stop=True)
                ins.then_inc(s_y, 1)

            layer_norm(1)
            pe.wait_ge(s_wm[0], 16 * 3)
            for T in range(NT):
                if T % TPC == 0:
                    pe.wait_ge(s_hT, NC + T // TPC + 1)
                ins = mm(bank[2][:, T * E:(T + 1) * E], hT[:, T * P:(T + 1) * P], gateT[:, :], start=True, stop=True)
            ins.then_inc(s_cnt, 1)
            pe.wait_ge(s_oh, 1)
            mm(bank[3][:, 0:E], ones[:, :], cnt[:, :], start=True, stop=True).then_inc(s_cnt, 1)

            def down0(u, j):
                k = (j // NC) % 2
                pe.wait_ge(s_hm, u + 1)
                wait(pe, s_acc[0], u - 1)
                for t in range(TPC):
                    ins = mm(bank[4 + j % 2][:, t * D:(t + 1) * D], HM0[:, j % 2, t * P:(t + 1) * P],
                             W0[:, k, 2 * F0:3 * F0], start=True, stop=True)
                ins.then_inc(s_dn[0], 1)

            def moe0(i):
                for j in range(2 * NC):
                    u = i * 2 * NC + j
                    k, c = j // NC, j % NC
                    if c == 0:
                        pe.wait_ge(s_w[0][k], 16 * i + 16)
                    if j == 0 and isinstance(i, int):
                        pe.wait_ge(s_ws[0], 1)
                    wait(pe, s_hm, u - 1)
                    mm(bank[j % 2][:, :], W0[:, k, 0:F0], chunk(hT, c), start=True, stop=True)
                    mm(bank[2 + j % 2][:, :], W0[:, k, F0:2 * F0], chunk(hT, c), start=True, stop=True
                       ).then_inc(s_up[0], 1)
                    if j:
                        down0(u - 1, j - 1)
                down0(u, 2 * NC - 1)

            moe0(0)
            with pe.Fori(1, E // 2) as i:
                moe0(i)

            layer_norm(2)
            pe.wait_ge(s_wp, 16 * 4)
            for c in range(NC):
                pe.wait_ge(s_hT, 3 * NC)
                for w in range(4):
                    if c:
                        pe.wait_ge(s_rot, 6 * (c - 1) + 3 * (w // 2) + w % 2 + 1)
                    mm(bank[w][:, :], Wqkv[:, w, :], chunk(hT, c), start=True, stop=True).then_inc(s_pj, 1)
                wait(pe, s_v, c)
                for t in range(TPC):
                    T = c * TPC + t
                    ins = mm(bank[4][:, t * D:(t + 1) * D], hT[:, T * P:(T + 1) * P], Wqkv[:, 4, :],
                             start=True, stop=True)
                ins.then_inc(s_pj, 1)

            def relative_scores(i):
                pe.wait_ge(s_in, (i + 1) * 16 * 7)
                for g in range(18):
                    if g < RING:
                        if not isinstance(i, int):
                            pe.wait_ge(s_ex, (i - 1) * 24 + 21 + g + 1)
                    else:
                        pe.wait_ge(s_bl, i * 18 + g - RING + 1)
                    for x in range(16):
                        q = g * 16 + x
                        local = q if q < X0 else q - X0
                        col = q if q < X0 else q - X0 + P
                        ins = mm(bank[g % RING][:, x * HS:(x + 1) * HS], GTB[:, X0 - local:X0 - local + P],
                                 QG[:, :, col], start=True, stop=True)
                    ins.then_inc(s_gen, 1)

            def scores(i, rnd):
                done = s_r1 if rnd == 1 else s_r2
                for r in range(24):
                    if r < RING:
                        if rnd == 1:
                            pe.wait_ge(s_bl, i * 18 + 15 + r + 1)
                        else:
                            pe.wait_ge(s_mx, i * 24 + 21 + r + 1)
                    else:
                        pe.wait_ge(s_mx if rnd == 1 else s_ex, i * 24 + r - RING + 1)
                    if r == 0 and rnd == 1:
                        pe.wait_ge(s_bl, i * 18 + 18)
                    dst = bank[r % RING]
                    if r < 16:
                        d3 = dst[:, :].rearrange("p (h q) -> p h q", q=S)
                        for x in range(2):
                            h = 2 * r + x
                            mm(d3[:, x, :], KG[:, h, 0:P], QG[:, h, :], start=(x == 0), stop=False,
                               skip_group_check=True)
                        ins = mm(d3[:, :, 0:X0], identb[:, :], BH[:, 2 * r:2 * r + 2, 0:X0], start=False,
                                 stop=(rnd == 1), skip_group_check=True)
                        if rnd == 2:
                            ins = mm(d3[:, :, 0:X0], identb[:, :], BL[:, 2 * r:2 * r + 2, 0:X0], start=False,
                                     stop=True, skip_group_check=True)
                    else:
                        h0 = 4 * (r - 16)
                        for x in range(4):
                            mm(dst[:, x * P:(x + 1) * P], KG[:, h0 + x, P:S], QG[:, h0 + x, P:S], start=(x == 0),
                               stop=False, skip_group_check=True)
                        ins = mm(dst[:, :].rearrange("p (h q) -> p h q", q=P), identb[:, :], BH[:, h0:h0 + 4, X0:QB],
                                 start=False, stop=(rnd == 1), skip_group_check=True)
                        if rnd == 2:
                            ins = mm(dst[:, :].rearrange("p (h q) -> p h q", q=P), identb[:, :],
                                     BL[:, h0:h0 + 4, X0:QB], start=False, stop=True, skip_group_check=True)
                    ins.then_inc(done, 1)

            def transpose_maxima(i):
                pe.wait_ge(s_mc, i + 1)
                wait(pe, s_nm, i)
                for g in range(2):
                    ins = nc.tensor.transpose(bank[7][:, g * P:(g + 1) * P],
                                              MX0[:, g * H:(g + 1) * H, :].rearrange("p h b -> p (h b)"), ident[:, :])
                ins.then_inc(s_tm, 1)

            def weighted_values(i):
                pe.wait_ge(s_vin, (i + 1) * 16)
                pe.wait_ge(s_ex, (i + 1) * 24)
                for w in range(4):
                    s, hb = w // 2, w % 2
                    pe.wait_ge(s_pe, i * 4 + w - 1 if w >= 2 else i * 4)
                    for g in range(2):
                        for j in range(4):
                            h = 4 * (2 * hb + g) + j
                            mm(bank[3 + w % 2][32 * j:32 * j + VW, g * S:(g + 1) * S], VS[:, 2 * s, h, :],
                               PT0[:, 2 * h + s, :], start=True, stop=False, skip_group_check=True)
                        for j in range(4):
                            h = 4 * (2 * hb + g) + j
                            ins = mm(bank[3 + w % 2][32 * j:32 * j + VW, g * S + P:(g + 1) * S],
                                     VS[:, 2 * s + 1, h, :], PT1[:, 2 * h + s, :], start=False, stop=True,
                                     skip_group_check=True)
                    ins.then_inc(s_pv, 1)

            def weighted_relative(i):
                for w in range(4):
                    pe.wait_ge(s_re, i * 4 + w - 1 if w >= 2 else i * 4)
                    for x in range(16):
                        a = 16 * w + x
                        for j in range(4):
                            q = 64 * j + a
                            dst = bank[5 + w % 2][32 * j:32 * j + HD, x * HS:(x + 1) * HS]
                            if q < P:
                                ins = mm(dst, relk[:, q, :], PT0[:, :, q], start=True, stop=True,
                                         skip_group_check=True)
                            else:
                                near = q < P + REL - 1
                                ins = mm(dst, relk[:, q - P, :], PT1[:, :, q - P], start=True, stop=not near,
                                         skip_group_check=True)
                                if near:
                                    ins = mm(dst, relk[:, q, :], PT0[:, :, q], start=False, stop=True,
                                             skip_group_check=True)
                    ins.then_inc(s_rl, 1)

            pe.wait_ge(s_tab, 16 * 7)
            pe.wait_ge(s_tb, 2)
            relative_scores(0)
            scores(0, 1)
            transpose_maxima(0)
            pe.wait_ge(s_mr, 32)
            scores(0, 2)
            with pe.Fori(1, NP) as i:
                relative_scores(i)
                scores(i, 1)
                transpose_maxima(i)
                weighted_values(i - 1)
                weighted_relative(i - 1)
                pe.wait_ge(s_mr, (i + 1) * 32)
                scores(i, 2)
            weighted_values(NP - 1)
            weighted_relative(NP - 1)

            pe.wait_ge(s_wo, 32)
            for c in range(NC + 1):
                if c < NC:
                    pe.wait_ge(s_dr, c + 1)
                    wait(pe, s_cx, c - 1)
                    mm(bank[c % 2][:, :], sel16[0:H, :], DR[0:H, c % 2, :], start=True, stop=True).then_inc(s_db, 1)
                if c:
                    k = (c - 1) % 2
                    pe.wait_ge(s_cx, c)
                    wait(pe, s_yr, NC + c - 2)
                    for t in range(TPC):
                        ins = mm(bank[6 + k][:, t * D:(t + 1) * D], CX[:, k, t * P:(t + 1) * P], woT1[:, :],
                                 start=True, stop=True)
                    ins.then_inc(s_y, 1)

            layer_norm(3)
            pe.wait_ge(s_wm[1], 16 * 5)
            for c in range(NC + 1):
                if c < NC:
                    pe.wait_ge(s_hT, 3 * NC + c + 1)
                    wait(pe, s_oh, 1 + c - 1) if c >= 2 else None
                    mm(bank[3 + c % 2][0:32, :], Wr1[:, :], chunk(hT, c), start=True, stop=True).then_inc(s_cnt, 1)
                if c:
                    pe.wait_ge(s_oh, 1 + c)
                    for t in range(TPC):
                        T = (c - 1) * TPC + t
                        ins = mm(bank[2][:, T * E:(T + 1) * E], RT1[0:33, (c - 1) % 2, t * P:(t + 1) * P],
                                 Wr2[0:33, :], start=True, stop=True)
                    ins.then_inc(s_m1, 1)
            pe.wait_ge(s_lg, 4)
            for c in range(NC):
                wait(pe, s_hs, 2 + c - 1) if c >= 2 else None
                for t in range(TPC):
                    T = c * TPC + t
                    ins = nc.tensor.transpose(bank[c % 2][0:E + 1, t * P:(t + 1) * P], WE[:, :, T], ident[:, :])
                ins.then_inc(s_ssm, 1)
                pe.wait_ge(s_hs, 2 + c + 1)
                wait(pe, s_acc[1], c - 1)
                for t in range(TPC):
                    ins = mm(bank[2 + c % 2][:, t * D:(t + 1) * D], WCT[0:E + 1, c % 2, t * P:(t + 1) * P],
                             be2[0:E + 1, :], start=True, stop=True)
                ins.then_inc(s_ssm, 1)

            def up1(u, j, k):
                c = j % NC
                for b in range(KB1):
                    if isinstance(u, int) and u == 0:
                        pe.wait_ge(s_acc[1], NC)
                    else:
                        pe.wait_ge(s_act[1], (u - 1) * KB1 + b + 1)
                    mm(bank[b][:, :], W1[:, k, b * P:(b + 1) * P], chunk(hT, c), start=True, stop=True
                       ).then_inc(s_up[1], 1)

            def down1(u, j, k):
                pe.wait_ge(s_act[1], (u + 1) * KB1)
                wait(pe, s_acc[1], NC + u - 1)
                for t in range(TPC):
                    for b in range(KB1):
                        ins = mm(bank[4 + j % 2][:, t * D:(t + 1) * D], HM1[:, j % 2, b, t * P:(t + 1) * P],
                                 W1[:, k, I1 + b * D:I1 + (b + 1) * D], start=(b == 0), stop=(b == KB1 - 1))
                ins.then_inc(s_dn[1], 1)

            def moe1(n, u0, slot, arrived):
                for j in range(n * NC):
                    k = slot[j // NC]
                    if j % NC == 0:
                        pe.wait_ge(s_w[1][k], arrived[j // NC])
                    up1(u0 + j, j, k)
                    if j:
                        down1(u0 + j - 1, j - 1, slot[(j - 1) // NC])
                down1(u0 + n * NC - 1, n * NC - 1, slot[n - 1])

            moe1(1, 0, [0], [16])
            with pe.Fori(0, E // 2) as i:
                moe1(2, NC + i * 2 * NC, [1, 0], [16 * i + 16, 16 * i + 32])


_SHAPE = (16, 256, 128)


def constants():
    import numpy as np
    k = {}
    k["ident"] = np.eye(P, dtype=np.float32)
    k["blockmask"] = np.repeat(np.eye(8, dtype=np.float32), N, axis=0)
    k["iota"] = np.tile(np.arange(E, dtype=np.float32), (P, 1))
    k["onesrow"] = np.ones((1, HS, S), dtype=np.uint16) * np.uint16(0x3F80)
    k["zerorow"] = np.zeros((1, HS, S), dtype=np.uint16)
    k["sel16"] = np.repeat(np.eye(H, dtype=np.float32), HD, axis=1)
    low = np.zeros((25, 1), np.float32)
    low[8:16] = 1
    k["lowrows"] = low
    freq = (np.float32(1.0) / np.float32(10000.0) ** (np.arange(0, HD, 2, dtype=np.float32) / np.float32(HD)))
    ang = np.outer(np.arange(S, dtype=np.float32), freq.astype(np.float32)).astype(np.float32)
    cos = np.repeat(np.cos(ang), 2, axis=1).T
    sin = np.repeat(np.sin(ang), 2, axis=1).T.copy()
    sin[0::2] *= -1
    cos, sin = np.tile(cos, (H, 1)), np.tile(sin, (H, 1))
    r = np.float32(HD) ** np.float32(-0.5)
    k["ropes"] = np.stack([cos * r, sin * r, cos, sin], axis=1).astype(np.float32)
    return k


def kernel(**inputs):
    import numpy as np
    import concourse.bacc as bacc
    from concourse.bass_utils import run_bass_kernel_spmd

    a = {n: np.asarray(x) for n, x in inputs.items()}
    k = constants()
    L = {}
    L["x"] = a["L0_attn_x"].reshape(TOK, D)
    L["cT"] = np.stack([a["L0_c"].T, a["L1_c"].T], axis=1)
    L["wmod"] = np.stack([a["L0_wmod"], a["L1_wmod"]], axis=1)
    L["wbT"] = a["L0_attn_W_b"].T
    L["wt16"] = np.repeat(a["L0_attn_W_t"].T, N, axis=1)
    L["wc8"] = np.tile(a["L0_attn_W_c"], (1, 8))
    L["woT0"] = a["L0_attn_W_o"].T
    L["bb8"] = np.tile(a["L0_attn_b_b"], 8)[:, None]
    L["A8"] = np.tile(a["L0_attn_A"], 8)[:, None]
    L["bt"] = np.tile(a["L0_attn_b_t"], P)[:, None]
    L["Dv"] = a["L0_attn_D"][:, None]
    L["bc"] = a["L0_attn_b_c"][:, None]
    L["bo"] = a["L0_attn_b_o"][None, :]
    L["gateT"] = a["L0_ffn_gate_weight"].T
    L["sim"] = np.tile(a["L0_ffn_similarity_matrix"][None], (P, 1, 1))
    L["w0"] = np.concatenate([a["L0_ffn_gate_up_proj"].transpose(0, 2, 1), a["L0_ffn_down_proj"].transpose(0, 2, 1)],
                             axis=2)
    swap = np.arange(D).reshape(-1, 2)[:, ::-1].reshape(-1)
    wq, wk, wv = a["L1_attn_w_q"], a["L1_attn_w_k"], a["L1_attn_w_v"]
    L["wqkv"] = np.stack([wq.T, wq[swap].T, wk.T, wk[swap].T, wv.T], axis=1)
    L["woT1"] = a["L1_attn_w_o"].T
    rel = a["L1_attn_rel_emb"]
    L["rel0"] = np.tile(rel[0], H)[:, None]
    L["rel0r"] = np.tile(rel[0][None], (P, 1))
    L["relk"] = rel[np.clip(np.arange(P)[:, None] - np.arange(X0)[None, :], -REL, REL) + REL]
    gt = rel[np.clip(np.arange(X0 + P) - X0, -REL, REL) + REL].T
    mask = np.where(np.arange(X0 + P)[None, :] > X0, np.float32(NEG), np.float32(0.0))
    L["gt"] = np.concatenate([gt, gt, gt, mask], axis=0)
    L["rel0c"] = np.concatenate([rel[0], rel[0], rel[0], np.zeros(1, np.float32)])[:, None]
    L["wr1"] = a["L1_ffn_Wr1"]
    L["wr2"] = np.concatenate([a["L1_ffn_Wr2"], a["L1_ffn_br2"][None]], axis=0)
    L["br1"] = a["L1_ffn_br1"][:, None]
    L["be2"] = np.concatenate([a["L1_ffn_bs2"][None], a["L1_ffn_be2"]], axis=0)
    up = np.concatenate([a["L1_ffn_Ws1"][None], a["L1_ffn_We1"]], axis=0)
    down = np.concatenate([a["L1_ffn_Ws2"][None], a["L1_ffn_We2"]], axis=0)
    down = down.reshape(E + 1, KB1, P, D).transpose(0, 2, 1, 3).reshape(E + 1, P, KB1 * D)
    bias = np.concatenate([a["L1_ffn_bs1"][None], a["L1_ffn_be1"]], axis=0).reshape(E + 1, KB1, P).transpose(0, 2, 1)
    L["w1"] = np.concatenate([up, down, bias], axis=2)
    L.update(k)

    nc = bacc.Bacc("TRN2", target_bir_lowering=False, num_devices=1)
    arrays, args = {}, {}
    for name, v in L.items():
        v = np.ascontiguousarray(v)
        arrays[f"in_{name}"] = v
        dt = BF16 if v.dtype == np.uint16 else mybir.dt.from_np(v.dtype)
        if v.dtype == np.uint16:
            import ml_dtypes
            v = v.view(ml_dtypes.bfloat16)
            arrays[f"in_{name}"] = v
        args[name] = nc.dram_tensor(f"in_{name}", v.shape, dt, kind="ExternalInput").ap()
    out = nc.dram_tensor("out_dram", (TOK, D), F32, kind="ExternalOutput").ap()
    build(nc, args, out)
    r = run_bass_kernel_spmd(nc, [arrays], core_ids=[0])
    return r.results[0]["out_dram"].reshape(_SHAPE)
```

```python
from contextlib import ExitStack

import concourse.bass as bass
from concourse import mybir

F32 = mybir.dt.float32
BF16 = mybir.dt.bfloat16
U32 = mybir.dt.uint32
ALU = mybir.AluOpType
ACT = mybir.ActivationFunctionType
AX = mybir.AxisListType.X

P = 128
B, S, D = 16, 256, 128
TOK = B * S
NT = TOK // P
CH = 512
NC = TOK // CH
TPC = CH // P
N = 16
H, HD = 16, 8
REL = 32
EPS = 1e-5
NEG = -1e18
E = 8
F0 = 128
I1 = 512
KB1 = I1 // P
THRESHOLD = 0.7
RANK_AT = 1
NP = B // 2
HS = 2 * H
X0 = 160
QB = X0 + P
RING = 3
VW = HD + 1
LOWEST = -3e38
W1W = I1 + I1 + KB1
GT = 256
UT = 4
NG = -(-((2 * TOK + E * (GT - 1)) // GT) // UT) * UT
RW = D + 1
KT = TOK // GT


def build(nc, A, out):
    ctx = ExitStack()
    with ctx:
        def sb(name, shape, dt=F32):
            return ctx.enter_context(nc.sbuf_tensor("sb_" + name, shape, dt))

        def sem(name):
            return ctx.enter_context(nc.semaphore(name))

        bank = [ctx.enter_context(nc.psum_tensor(f"bank{i}", [P, 512], F32)) for i in range(8)]

        def scratch(name, shape, dt=F32):
            return nc.dram_tensor(name, shape, dt).ap()

        X = sb("X", [P, NT, D])
        GATE = sb("GATE", [P, 2, B, D])
        ident = sb("ident", [P, P])
        identb = sb("identb", [P, P], BF16)
        ones = sb("ones", [P, P])
        cT = sb("cT", [P, 2, B])
        scT = sb("scT", [P, 2, B])
        MOD = sb("MOD", [P, 2, 6, B])
        GG = sb("GG", [B, 4, D])
        GT1 = sb("GT1", [B, 4, D])
        ST = sb("ST", [P, NT, 6])
        MV = sb("MV", [P, NT, 2])
        RSTD = sb("RSTD", [P, NT])
        SD = sb("SD", [P, NT])
        XN = sb("XN", [P, 2, TPC, D])
        epsc = sb("epsc", [P, 1])
        TMP = sb("TMP", [P, 2, CH])
        ARENA = 154 * 1024 // 4
        arena = sb("arena", [P, ARENA])

        class Region:

            def __init__(self, at=0):
                self.at = at

            def take(self, n, dt=F32):
                words = n if dt == F32 else (n + 1) // 2
                v = arena[:, self.at:self.at + words]
                self.at += words
                assert self.at <= ARENA, self.at * 4
                return v if dt == F32 else v.bitcast(BF16)

        R = Region()
        hT = R.take(TOK)
        ACC = R.take(NT * D).rearrange("p (t d) -> p t d", t=NT)
        dense_base = R.at

        R = Region(dense_base)
        wmod = R.take(2 * 6 * D).rearrange("p (l n) -> p l n", l=2)
        WBpad = R.take(240)
        WTpad = R.take(240)
        Wcr = R.take(P)
        WoT = R.take(D)
        M2 = R.take(D)
        small = R.take(16)
        bcol = R.take(1)
        borow = R.take(D)
        crow = R.take(D)
        blockmask = R.take(8)
        ZM = R.take(8 * D).rearrange("p (b o) -> p b o", b=8)
        EZ = R.take(2 * S).rearrange("p (h t) -> p h t", h=2)
        SIG = R.take(2 * S).rearrange("p (h t) -> p h t", h=2)
        AE = R.take(2 * S).rearrange("p (h t) -> p h t", h=2)
        BU = R.take(2 * S).rearrange("p (h t) -> p h t", h=2)
        HSC = R.take(2 * S).rearrange("p (h t) -> p h t", h=2)

        R = Region(dense_base)
        gateT = R.take(E)
        sim = R.take(E * E).rearrange("p (i j) -> p i j", i=E)
        iota = R.take(E)
        NE = NT * E
        def table(n=NE):
            return R.take(n)
        LG, PR, EQ, OH1, OH2, CD, WT = [table().rearrange("p (t e) -> p t e", t=NT) for _ in range(7)]
        m1, m2, ssum, idx, w1, w2 = [table(NT) for _ in range(6)]
        cnt, pm = table(E), table(E)
        sm, smq, smc = [table(E * E).rearrange("p (i j) -> p i j", i=E) for _ in range(3)]
        bs, bj, cnd, emap = [table(E) for _ in range(4)]
        MM = table(E * E).rearrange("p (i j) -> p i j", i=E)
        WD = R.take(NE).rearrange("p (e t) -> p e t", e=E)
        WE = R.take((E + 1) * NT).rearrange("p (e t) -> p e t", e=E + 1)
        wstep = R.take(2 * NT).rearrange("p (s t) -> p s t", s=2)
        moe_base = R.at
        W0 = R.take(2 * 3 * F0).rearrange("p (s n) -> p s n", s=2)
        SG = R.take(2 * CH).rearrange("p (s n) -> p s n", s=2)
        HM0 = R.take(2 * CH).rearrange("p (s n) -> p s n", s=2)
        R = Region(moe_base)
        Wr1 = R.take(32)
        Wr2 = R.take(E)
        br1 = R.take(1)
        RT1 = R.take(2 * CH).rearrange("p (s n) -> p s n", s=2)
        be2 = R.take(D)
        WCT = R.take(2 * CH).rearrange("p (s n) -> p s n", s=2)
        rowid = R.take(2 * NT).rearrange("p (k t) -> p k t", k=2)
        steps = R.take(2 * 64).rearrange("p (k n) -> p k n", k=2)
        below = R.take(P)
        ME, IN, EX = [R.take(NE).rearrange("p (e t) -> p e t", e=E) for _ in range(3)]
        tot, tiles, upto, offs = [R.take(E) for _ in range(4)]
        cmp = R.take(64 * E)
        dest = [R.take(NT).bitcast(U32) for _ in range(2)]
        texp = R.take(NG)
        texpu = R.take(NG).bitcast(U32)
        ROWS = [R.take(NT * RW).rearrange("p (t n) -> p t n", t=NT) for _ in range(2)]
        W1S = R.take(W1W)
        W1 = R.take(UT * W1W).rearrange("p (s n) -> p s n", s=UT)
        moe_units = R.at
        HM1 = R.take(2 * KB1 * CH).rearrange("p (s k n) -> p s k n", s=2, k=KB1)
        R = Region(moe_units)
        HMT = R.take(2 * KB1 * GT).rearrange("p (s k n) -> p s k n", s=2, k=KB1)
        XR = R.take(UT * 2 * RW).rearrange("p (s r n) -> p s r n", s=UT, r=2)
        rid = R.take(UT * 2).rearrange("p (s r) -> p s r", s=UT).bitcast(U32)
        XT = R.take(2 * GT).rearrange("p (s n) -> p s n", s=2)
        YS = R.take(UT * GT).rearrange("p (s r n) -> p s r n", s=UT, r=2)
        YG = [r.rearrange("p t n -> p (t n)")[:, 0:NT * D].rearrange("p (t n) -> p t n", t=NT) for r in ROWS]

        R = Region(dense_base)
        Wqkv = R.take(5 * D).rearrange("p (w n) -> p w n", w=5)
        ropes = R.take(4 * S).rearrange("p (w t) -> p w t", w=4)
        rel0 = R.take(1)
        relv = R.take(HD)
        RT_1 = R.take(2 * CH).rearrange("p (s n) -> p s n", s=2)
        RT_2 = R.take(2 * CH).rearrange("p (s n) -> p s n", s=2)
        QR = R.take(2 * CH).rearrange("p (s n) -> p s n", s=2)
        KR = R.take(2 * CH).rearrange("p (s n) -> p s n", s=2)
        HI = R.take(4 * CH, BF16).rearrange("p (s w n) -> p s w n", s=2, w=2)
        LO = R.take(4 * CH, BF16).rearrange("p (s w n) -> p s w n", s=2, w=2)
        VT = R.take(2 * TPC * H * VW).rearrange("p (s t n) -> p s t n", s=2, t=TPC)

        R = Region(0)
        QG = R.take(HS * S, BF16).rearrange("p (h q) -> p h q", h=HS)
        KG = R.take(HS * S, BF16).rearrange("p (h q) -> p h q", h=HS)
        BH = R.take(HS * QB, BF16).rearrange("p (h q) -> p h q", h=HS)
        BL = R.take(HS * QB, BF16).rearrange("p (h q) -> p h q", h=HS)
        PT0 = R.take(HS * S).rearrange("p (h q) -> p h q", h=HS)
        PT1 = R.take(HS * P).rearrange("p (h q) -> p h q", h=HS)
        relk = R.take(X0 * HD).rearrange("p (x d) -> p x d", d=HD)
        GTf = R.take(X0 + P)
        GTB = R.take(X0 + P, BF16)
        rel0r = R.take(HD)
        rel0c = R.take(1)
        MX0 = R.take(HS * 8).rearrange("p (h b) -> p h b", h=HS)
        MX1 = R.take(HS * 4).rearrange("p (h b) -> p h b", h=HS)
        NM = R.take(2 * 32, BF16).rearrange("p (c n) -> p c n", c=2)
        VS = R.take(TPC * H * VW).rearrange("p (t h v) -> p t h v", t=TPC, h=H)
        CTS = R.take(2 * CH).rearrange("p (s n) -> p s n", s=2)
        RS = R.take(HS * 64).rearrange("p (h i) -> p h i", h=HS)
        half_mask = R.take(1)
        attn_end = R.at

        R = Region(0)
        C1 = R.take(2 * CH).rearrange("p (s n) -> p s n", s=2)
        R1 = R.take(2 * CH).rearrange("p (s n) -> p s n", s=2)
        DN = R.take(2 * CH).rearrange("p (s n) -> p s n", s=2)
        DR = R.take(2 * CH).rearrange("p (s n) -> p s n", s=2)
        CX = R.take(2 * CH).rearrange("p (s n) -> p s n", s=2)
        sel16 = R.take(P)
        woT1 = R.take(D)

        gD = scratch("gates", [4, B, D])
        qD = scratch("q_parts", [2, P, TOK], BF16)
        kD = scratch("k_parts", [2, P, TOK], BF16)
        vD = scratch("v_rows", [TOK, H * VW])
        cD = scratch("context", [P, TOK])
        rD = scratch("context_rel", [P, TOK])
        dD = scratch("denominators", [H, TOK])
        xsD = scratch("dispatched_rows", [NG * GT, RW])
        yD = scratch("expert_results", [2 * TOK + NG * GT // 8, D])

        s_const = sem("s_const")
        s_x = sem("s_x")
        s_set = sem("s_set")
        s_cm = sem("s_cm")
        s_mod = sem("s_mod")
        s_gg = sem("s_gg")
        s_gst = sem("s_gst")
        s_gld = sem("s_gld")
        s_dv = sem("s_dv")
        s_mv = sem("s_mv")
        s_sd = sem("s_sd")
        s_xn = sem("s_xn")
        s_tr = sem("s_tr")
        s_hT = sem("s_hT")
        s_m1 = sem("s_m1")
        s_zm = sem("s_zm")
        s_ssm = sem("s_ssm")
        s_ez = sem("s_ez")
        s_sig = sem("s_sig")
        s_ae = sem("s_ae")
        s_hs = sem("s_hs")
        s_y = sem("s_y")
        s_yr = sem("s_yr")
        s_wm = [sem("s_wm0"), sem("s_wm1")]
        s_lg = sem("s_lg")
        s_el = sem("s_el")
        s_cnt = sem("s_cnt")
        s_oh = sem("s_oh")
        s_w = [[sem(f"s_w{m}{k}") for k in range(2)] for m in range(2)]
        s_up = [sem("s_up0"), sem("s_up1")]
        s_act = [sem("s_act0"), sem("s_act1")]
        s_hm = sem("s_hm")
        s_dn = [sem("s_dn0"), sem("s_dn1")]
        s_acc = [sem("s_acc0"), sem("s_acc1")]
        s_ws = [sem("s_ws0"), sem("s_ws1")]
        s_wp = sem("s_wp")
        s_pj = sem("s_pj")
        s_rot = sem("s_rot")
        s_hi = sem("s_hi")
        s_lo = sem("s_lo")
        s_v = sem("s_v")
        s_qst = [sem("s_qst0"), sem("s_qst1")]
        s_tab = sem("s_tab")
        s_tb = sem("s_tb")
        s_in = sem("s_in")
        s_vin = sem("s_vin")
        s_gen = sem("s_gen")
        s_bh = sem("s_bh")
        s_bl = sem("s_bl")
        s_r1 = sem("s_r1")
        s_mx = sem("s_mx")
        s_mc = sem("s_mc")
        s_tm = sem("s_tm")
        s_nm = sem("s_nm")
        s_mr = sem("s_mr")
        s_r2 = sem("s_r2")
        s_ex = sem("s_ex")
        s_pv = sem("s_pv")
        s_pe = sem("s_pe")
        s_rl = sem("s_rl")
        s_re = sem("s_re")
        s_cst = [sem("s_cst0"), sem("s_cst1")]
        s_rst = sem("s_rst")
        s_cin = [sem("s_cin0"), sem("s_cin1")]
        s_wo = sem("s_wo")
        s_dr = sem("s_dr")
        s_db = sem("s_db")
        s_cx = sem("s_cx")
        s_out = sem("s_out")
        s_pad = sem("s_pad")
        s_back = sem("s_back")
        s_rows = sem("s_rows")
        s_ids = sem("s_ids")
        s_tot = sem("s_tot")
        s_rank = sem("s_rank")
        s_dest = sem("s_dest")
        s_disp = sem("s_disp")
        s_sw = sem("s_sw")
        s_sup = sem("s_sup")
        s_sact = sem("s_sact")
        s_sdn = sem("s_sdn")
        s_sout = sem("s_sout")
        s_wct = sem("s_wct")
        s_wcc = sem("s_wcc")
        s_res = sem("s_res")
        s_ew = [sem(f"s_ew{k}") for k in range(UT)]
        s_xr = [sem(f"s_xr{k}") for k in range(UT)]
        s_xp = sem("s_xp")
        s_xt = sem("s_xt")
        s_ys = sem("s_ys")
        s_yo = [sem(f"s_yo{k}") for k in range(UT)]
        s_yl = [sem(f"s_yl{c}") for c in range(NC)]
        s_turn = sem("s_turn")
        s_y1 = sem("s_y1")
        s_y2 = sem("s_y2")
        s_fin = sem("s_fin")

        block = ctx.enter_context(nc.Block())

        def chunk(ap, c):
            return ap[:, c * CH:(c + 1) * CH]

        def wait(eng, s, v):
            if isinstance(v, int) and v <= 0:
                return
            eng.wait_ge(s, v)

        @block.sync
        def _(sp):
            n = [0]

            def const(dst, src):
                sp.dma_start(dst, src).then_inc(s_const, 16)
                n[0] += 1

            const(cT[:, :, :], A["cT"])
            const(wmod[:, :, :], A["wmod"])
            for c in range(NC):
                sp.dma_start(X[:, c * TPC:(c + 1) * TPC, :],
                             A["x"][c * CH:(c + 1) * CH, :].rearrange("(t p) d -> p t d", p=P)).then_inc(s_x, 16)
            const(ident[:, :], A["ident"])
            const(WBpad[:, 112:128], A["wbT"])
            const(WTpad[:, 112:128], A["wt16"])
            const(Wcr[:, :], A["wc8"])
            const(WoT[:, :], A["woT0"])
            const(small[:, 0:1], A["bb8"])
            const(small[:, 1:2], A["A8"])
            const(small[:, 2:3], A["bt"])
            const(small[:, 3:4], A["Dv"])
            const(bcol[:, :], A["bc"])
            const(borow[0:1, :], A["bo"])
            const(blockmask[:, :], A["blockmask"])
            assert n[0] == 14
            half = NG * GT // 8
            for x in range(8):
                sp.dma_start(xsD[x * half:(x + 1) * half, :], A["padding"]).then_inc(s_pad, 16)
            sp.wait_ge(s_gg, 1)
            sp.dma_start(gD.rearrange("g b f -> b g f"), GG[:, :, :]).then_inc(s_gst, 16)
            sp.wait_ge(s_gst, 16)
            sp.dma_start(GATE[:, :, :, :].rearrange("p g b f -> p (g b f)"),
                         gD[0:2].rearrange("g b f -> (g b f)").partition_broadcast(P)).then_inc(s_gld, 16)

            sp.wait_ge(s_yr, NC)
            for dst, src in ((gateT[:, :], A["gateT"]), (sim[:, :, :], A["sim"]), (iota[:, :], A["iota"])):
                sp.dma_start(dst, src).then_inc(s_wm[0], 16)

            def w0_load(e, k):
                sp.dma_start(W0[:, k, :], A["w0"][e]).then_inc(s_w[0][k], 16)

            w0_load(0, 0)
            w0_load(1, 1)
            with sp.Fori(0, E // 2 - 1) as i:
                for k in range(2):
                    sp.wait_ge(s_dn[0], (2 * i + k + 1) * NC)
                    w0_load(2 * i + k + 2, k)

            sp.wait_ge(s_acc[0], E * NC + NC)
            sp.dma_start(GATE[:, :, :, :].rearrange("p g b f -> p (g b f)"),
                         gD[2:4].rearrange("g b f -> (g b f)").partition_broadcast(P)).then_inc(s_gld, 16)
            for dst, src in ((Wqkv[:, :, :], A["wqkv"]), (ropes[:, :, :], A["ropes"]), (rel0[:, :], A["rel0"]),
                             (relv[:, :], A["rel0r"])):
                sp.dma_start(dst, src).then_inc(s_wp, 16)
            for c in range(NC):
                sp.wait_ge(s_hi, 2 * (c + 1))
                sp.wait_ge(s_lo, 2 * (c + 1))
                sp.wait_ge(s_v, c + 1)
                k = c % 2
                for w, dst in ((0, qD), (1, kD)):
                    sp.dma_start(chunk(dst[0], c), HI[:, k, w, :]).then_inc(s_qst[k], 16)
                    sp.dma_start(chunk(dst[1], c), LO[:, k, w, :]).then_inc(s_qst[k], 16)
                sp.dma_start(vD[c * CH:(c + 1) * CH, :].rearrange("(t p) n -> p t n", p=P),
                             VT[:, k, :, :]).then_inc(s_qst[k], 16)
            for k in range(2):
                sp.wait_ge(s_qst[k], 16 * 5 * NC // 2)

            for dst, src in ((relk[:, :, :], A["relk"]), (GTf[0:25, :], A["gt"]), (rel0r[:, :], A["rel0r"]),
                             (rel0c[0:25, :], A["rel0c"]), (half_mask[0:25, :], A["lowrows"])):
                sp.dma_start(dst, src).then_inc(s_tab, 16)
            sp.wait_ge(s_tb, 1)
            sp.dma_start(QG[24:25, :, :], A["onesrow"]).then_inc(s_tab, 16)
            sp.dma_start(KG[25:26, :, :], A["onesrow"]).then_inc(s_tab, 16)

            def load_pair(i, first):
                at = i * CH
                if not first:
                    sp.wait_ge(s_r2, i * 24)
                for r, part in ((0, 0), (8, 0), (16, 1)):
                    sp.dma_start(QG[r:r + 8, :, :].rearrange("d (h s) q -> d h (s q)", h=H),
                                 qD[part, :, bass.ds(at, CH)].rearrange("(h d) t -> d h t", h=H)).then_inc(s_in, 16)
                for r, part in ((0, 0), (8, 1), (16, 0)):
                    sp.dma_start(KG[r:r + 8, :, :].rearrange("d (h s) q -> d h (s q)", h=H),
                                 kD[part, :, bass.ds(at, CH)].rearrange("(h d) t -> d h t", h=H)).then_inc(s_in, 16)
                sp.dma_start(QG[25:26, :, :], A["zerorow"]).then_inc(s_in, 16)

            def load_values(i, first):
                if not first:
                    sp.wait_ge(s_pv, i * 4)
                sp.dma_start(VS[:, :, :, :].rearrange("p t h v -> p t (h v)"),
                             vD[bass.ds(i * CH, CH), :].rearrange("(t p) n -> p t n", p=P)).then_inc(s_vin, 16)

            def move_maxima(i):
                sp.wait_ge(s_nm, i + 1)
                for g in range(2):
                    sp.dma_start(QG[25:26, g * H:(g + 1) * H, :].rearrange("o h q -> o (h q)"),
                                 NM[:, g, :]).then_inc(s_mr, 16)

            def store_values(i):
                for w in range(4):
                    s, hb = w // 2, w % 2
                    sp.wait_ge(s_pe, i * 4 + w + 1)
                    at = i * CH + s * S
                    for j in range(4):
                        src = CTS[32 * j:32 * j + HD, w % 2, :].rearrange("d (g q) -> d g q", g=2)
                        sp.dma_start(
                            cD.rearrange("(g j d) t -> j d g t", g=4, j=4)[j, :, 2 * hb:2 * hb + 2, bass.ds(at, S)],
                            src).then_inc(s_cst[w % 2], 16)
                        den = CTS[32 * j + HD:32 * j + HD + 1, w % 2, :].rearrange("d (g q) -> d g q", g=2)
                        sp.dma_start(
                            dD.rearrange("(g j d) t -> j d g t", g=4, j=4)[j, :, 2 * hb:2 * hb + 2, bass.ds(at, S)],
                            den).then_inc(s_cst[w % 2], 16)

            def store_relative(i):
                sp.wait_ge(s_re, i * 4 + 4)
                for s in range(2):
                    for j in range(4):
                        sp.dma_start(
                            rD.rearrange("(h d) t -> d h t", h=H)[:, :, bass.ds(i * CH + s * S + 64 * j, 64)],
                            RS[32 * j:32 * j + HD, :, :].rearrange("d (h s) i -> d h s i", s=2)[:, :, s, :]
                        ).then_inc(s_rst, 16)

            load_pair(0, True)
            load_values(0, True)
            move_maxima(0)
            with sp.Fori(1, NP) as i:
                load_pair(i, False)
                store_values(i - 1)
                load_values(i, False)
                move_maxima(i)
                store_relative(i - 1)
            store_values(NP - 1)
            store_relative(NP - 1)

            for s, k in ((s_cst[0], 16 * 16 * NP), (s_cst[1], 16 * 16 * NP), (s_rst, 16 * 8 * NP)):
                sp.wait_ge(s, k)
            sp.dma_start(sel16[0:H, :], A["sel16"]).then_inc(s_wo, 16)
            sp.dma_start(woT1[:, :], A["woT1"]).then_inc(s_wo, 16)
            for c in range(NC):
                if c >= 2:
                    sp.wait_ge(s_cx, c - 1)
                for dst, src in ((C1[:, c % 2, :], cD), (R1[:, c % 2, :], rD), (DN[0:H, c % 2, :], dD)):
                    sp.dma_start(dst, chunk(src, c)).then_inc(s_cin[c % 2], 16)

            sp.wait_ge(s_yr, 2 * NC)
            for dst, src in ((Wr1[:, :], A["wr1"]), (Wr2[0:33, :], A["wr2"]), (br1[0:32, :], A["br1"]),
                             (be2[0:E + 1, :], A["be2"]), (iota[:, :], A["iota"])):
                sp.dma_start(dst, src).then_inc(s_wm[1], 16)

            for dst, src in ((rowid[:, :, :], A["rowid"]), (steps[:, :, :], A["steps"]), (below[:, :], A["below"])):
                sp.dma_start(dst, src).then_inc(s_wm[1], 16)
            sp.dma_start(W1S[:, :], A["w1s"]).then_inc(s_sw, 16)

            def load_tile(j, k):
                sp.dma_start(XR[:, k, :, :], xsD[bass.ds(j * GT, GT), :].rearrange("(r p) n -> p r n", p=P)
                             ).then_inc(s_xr[k], 16)
                e = sp.value_load(texpu[0:1, bass.ds(j, 1)], min_val=0, max_val=E - 1)
                sp.dma_start(W1[:, k, :], A["w1"][bass.ds(e, 1)].rearrange("o p n -> p (o n)")).then_inc(s_ew[k], 16)

            sp.wait_ge(s_dest, 1)
            sp.wait_ge(s_sdn, NC)
            sp.wait_ge(s_disp, 16 * 2 * NT)
            for k in range(UT):
                load_tile(k, k)
            with sp.Fori(1, NG // UT) as i:
                for k in range(UT):
                    sp.wait_ge(s_dn[1], i * UT - UT + k + 1)
                    load_tile(i * UT + k, k)

            for k in range(UT):
                sp.wait_ge(s_yo[k], 32 * (NG // UT))
            for c in range(NC):
                for k in range(2):
                    at = k * TOK + c * CH
                    sp.dma_start(YG[k][:, c * TPC:(c + 1) * TPC, :],
                                 yD[at:at + CH, :].rearrange("(t p) d -> p t d", p=P)).then_inc(s_yl[c], 16)
            for c in range(NC):
                sp.wait_ge(s_fin, c + 1)
                sp.dma_start(out[c * CH:(c + 1) * CH, :].rearrange("(t p) d -> p t d", p=P),
                             X[:, c * TPC:(c + 1) * TPC, :]).then_inc(s_out, 16)
            sp.wait_ge(s_out, 16 * NC)

        @block.gpsimd
        def _(pool):
            nc.gpsimd.memset(WBpad[:, 0:112], 0.0)
            nc.gpsimd.memset(WBpad[:, 128:240], 0.0)
            nc.gpsimd.memset(WTpad[:, 0:112], 0.0)
            nc.gpsimd.memset(WTpad[:, 128:240], 0.0)
            nc.gpsimd.memset(ones[:, :], 1.0).then_inc(s_set, 1)

            pool.wait_ge(s_pad, 16 * 8)
            pool.wait_ge(s_rows, 2 * NC)
            pool.wait_ge(s_ids, 1)
            pool.wait_ge(s_dest, 1)
            for t in range(NT):
                for k in range(2):
                    nc.gpsimd.indirect_dma_start(
                        xsD[:, :], bass.IndirectOffsetOnAxis(ap=dest[k][:, t:t + 1], axis=0),
                        ROWS[k][:, t, :], None).then_inc(s_disp, 16)

            def results_out(j, k):
                pool.wait_ge(s_ys, j + 1)
                pool.sem_inc(s_turn, 1)
                for r in range(2):
                    nc.gpsimd.indirect_dma_start(
                        yD[:, :], bass.IndirectOffsetOnAxis(ap=rid[:, k, r:r + 1], axis=0),
                        YS[:, k, r, :], None).then_inc(s_yo[k], 16)

            with pool.Fori(0, NG // UT) as i:
                for k in range(UT):
                    results_out(i * UT + k, k)
            for c in range(NC):
                pool.wait_ge(s_yl[c], 32)
                cs = slice(c * TPC, (c + 1) * TPC)
                nc.gpsimd.tensor_tensor(YG[1][:, cs, :], YG[1][:, cs, :],
                                        w2[:, cs].unsqueeze(2).to_broadcast([P, TPC, D]), ALU.mult).then_inc(s_y2, 1)

        @block.scalar
        def _(act):
            act.wait_ge(s_const, 16 * 14)
            nc.scalar.activation(scT[:, :, :], cT[:, :, :], ACT.Silu).then_inc(s_cm, 1)

            def layer_norm(n):
                l, first = n // 2, 3 * (n % 2)
                act.wait_ge(s_mv, n + 1)
                nc.scalar.activation(SD[:, :], MV[:, :, 1], ACT.Sqrt, bias=epsc[:, :]).then_inc(s_sd, 1)
                for c in range(NC):
                    act.wait_ge(s_tr, n * NC + c + 1)
                    for s in range(2):
                        b = 2 * c + s
                        ins = nc.scalar.activation(hT[:, b * S:(b + 1) * S], bank[c % 2][:, s * S:(s + 1) * S],
                                                   ACT.Identity, scale=MOD[:, l, first + 1, b:b + 1],
                                                   bias=MOD[:, l, first, b:b + 1])
                    ins.then_inc(s_hT, 1)

            layer_norm(0)
            for h in range(2):
                act.wait_ge(s_ssm, h + 1)
                nc.scalar.activation(EZ[:, h, :], bank[2 + h][:, S:2 * S], ACT.Exp, scale=-1.0,
                                     bias=small[:, 4:5]).then_inc(s_ez, 1)
            for h in range(2):
                act.wait_ge(s_sig, h + 1)
                nc.scalar.activation(AE[:, h, :], SIG[:, h, :], ACT.Exp, scale=small[:, 5:6],
                                     bias=small[:, 6:7]).then_inc(s_ae, 1)

            layer_norm(1)
            act.wait_ge(s_lg, 1)
            nc.scalar.activation(PR[:, :, :], LG[:, :, :], ACT.Exp).then_inc(s_el, 1)

            def moe0(i, first):
                for j in range(2 * NC):
                    u = i * 2 * NC + j
                    act.wait_ge(s_up[0], u + 1)
                    wait(act, s_hm, u - 1)
                    nc.scalar.activation(SG[:, j % 2, :], bank[j % 2][:, :], ACT.Silu).then_inc(s_act[0], 1)

            moe0(0, True)
            with act.Fori(1, E // 2) as i:
                moe0(i, False)

            layer_norm(2)
            for c in range(NC):
                k = c % 2
                if c >= 2:
                    act.wait_ge(s_qst[k], 16 * 5 * (c // 2))
                for w, src in ((0, QR), (1, KR)):
                    act.wait_ge(s_rot, 6 * c + 3 * w + 3)
                    nc.scalar.copy(HI[:, k, w, :], src[:, k, :]).then_inc(s_hi, 1)

            def bias_high(i, banks=range(18)):
                if not isinstance(i, int) and banks[0] == 0:
                    act.wait_ge(s_r2, i * 24)
                for g in banks:
                    act.wait_ge(s_gen, i * 18 + g + 1)
                    at = g * 16
                    nc.scalar.copy(BH[:, :, at:at + 16].rearrange("p h q -> p q h"),
                                   bank[g % RING][:, :].rearrange("p (q h) -> p q h", h=HS)).then_inc(s_bh, 1)

            def exponentials(i):
                for r in range(24):
                    act.wait_ge(s_r2, i * 24 + r + 1)
                    dst = PT0[:, 2 * r:2 * r + 2, :] if r < 16 else PT1[:, 4 * (r - 16):4 * (r - 16) + 4, :]
                    q = S if r < 16 else P
                    nc.scalar.activation(dst, bank[r % RING][:, :].rearrange("p (h q) -> p h q", q=q),
                                         ACT.Exp).then_inc(s_ex, 1)

            def values_out(i, units=range(4)):
                for w in units:
                    act.wait_ge(s_pv, i * 4 + w + 1)
                    v = 128 * (2 * i + w // 2)
                    wait(act, s_cst[w % 2], v)
                    nc.scalar.copy(CTS[:, w % 2, :], bank[3 + w % 2][:, :]).then_inc(s_pe, 1)

            bias_high(0)
            exponentials(0)
            with act.Fori(1, NP) as i:
                values_out(i - 1, (0, 1))
                bias_high(i, range(0, 6))
                values_out(i - 1, (2,))
                bias_high(i, range(6, 12))
                values_out(i - 1, (3,))
                bias_high(i, range(12, 18))
                exponentials(i)
            values_out(NP - 1)

            layer_norm(3)
            act.wait_ge(s_lg, 2)
            nc.scalar.activation(PR[:, :, :], LG[:, :, :], ACT.Exp).then_inc(s_el, 1)
            for c in range(NC):
                act.wait_ge(s_back, c + 1)
                for k in range(2):
                    nc.scalar.copy(ROWS[k][:, c * TPC:(c + 1) * TPC, 0:D],
                                   bank[6 + c % 2][:, :].rearrange("p (t d) -> p t d", t=TPC)).then_inc(s_rows, 1)
            for c in range(NC + 1):
                if c < NC:
                    wait(act, s_sdn, c - 1)
                    for b in range(KB1):
                        act.wait_ge(s_sup, c * KB1 + b + 1)
                        nc.scalar.activation(HM1[:, c % 2, b, :], bank[b][:, :], ACT.Silu,
                                             bias=W1S[:, 2 * I1 + b:2 * I1 + b + 1]).then_inc(s_sact, 1)
                if c:
                    act.wait_ge(s_sdn, c)
                    nc.scalar.copy(ACC[:, (c - 1) * TPC:c * TPC, :].rearrange("p t f -> p (t f)"),
                                   bank[4 + (c - 1) % 2][:, :]).then_inc(s_sout, 1)
            act.wait_ge(s_lg, 3)
            nc.scalar.activation(w2[:, :], m2[:, :], ACT.Exp).then_inc(s_el, 1)

            def hidden(j, k):
                wait(act, s_dn[1], j - 1)
                for b in range(KB1):
                    act.wait_ge(s_up[1], 2 * j + b // 2 + 1)
                    nc.scalar.activation(HMT[:, k % 2, b, :], bank[2 * (k % 2) + b // 2][:, b % 2 * GT:(b % 2 + 1) * GT],
                                         ACT.Silu, bias=W1[:, k, 2 * I1 + b:2 * I1 + b + 1]).then_inc(s_act[1], 1)

            for k in range(UT):
                hidden(k, k)
            with act.Fori(1, NG // UT) as i:
                for k in range(UT):
                    hidden(i * UT + k, k)
            for c in range(NC):
                act.wait_ge(s_yl[c], 32)
                for t in range(TPC):
                    T = c * TPC + t
                    ins = nc.scalar.activation(YG[0][:, T, :], YG[0][:, T, :], ACT.Copy, scale=w1[:, T:T + 1])
                ins.then_inc(s_y1, 1)

        @block.vector
        def _(dve):
            chain = [0]

            def link(ins):
                chain[0] += 1
                ins.then_inc(s_dv, 1)
                dve.wait_ge(s_dv, chain[0])

            v = nc.vector
            v.memset(epsc[:, :], EPS)
            for i in range(8):
                link(v.memset(bank[i][:, :], 0.0))
            dve.wait_ge(s_const, 16 * 14)
            v.tensor_copy(identb[:, :], ident[:, :])
            v.tensor_scalar(small[:, 4:5], small[:, 2:3], -1.0, None, ALU.mult)
            v.tensor_scalar(small[:, 5:6], small[:, 1:2], 0.99, None, ALU.mult)
            v.tensor_scalar(small[:, 6:7], small[:, 1:2], 0.01, None, ALU.mult)
            link(v.tensor_scalar(M2[:, :], WoT[:, :], small[:, 3:4], None, ALU.mult))

            dve.wait_ge(s_mod, 1)
            link(v.tensor_copy(MOD[:, :, :, :].rearrange("p l m b -> p (l m b)"), bank[0][:, 0:2 * 6 * B]))
            for m in (1, 4):
                link(v.tensor_scalar(MOD[:, :, m, :], MOD[:, :, m, :], 1.0, None, ALU.add))
            gsrc = bank[1][0:B, :].rearrange("p (g f) -> p g f", g=4)
            v.tensor_scalar(GT1[:, :, :], gsrc, 0.0, 2.0, ALU.is_ge, ALU.mult)
            link(v.tensor_scalar(GG[:, :, :], gsrc, -1.0, None, ALU.mult))
            link(v.scalar_tensor_tensor(out=GG[:, :, :].rearrange("p g f -> p (g f)"),
                                        in0=GG[:, :, :].rearrange("p g f -> p (g f)"), scalar=0.25,
                                        in1=bank[1][0:B, :], op0=ALU.max, op1=ALU.max))
            ins = v.scalar_tensor_tensor(out=GG[:, :, :].rearrange("p g f -> p (g f)"),
                                         in0=GT1[:, :, :].rearrange("p g f -> p (g f)"), scalar=-1.0,
                                         in1=GG[:, :, :].rearrange("p g f -> p (g f)"), op0=ALU.add, op1=ALU.mult)
            ins.then_inc(s_gg, 1)
            dve.wait_ge(s_m1, 1)
            for b in range(8):
                v.tensor_scalar(ZM[:, b, :], bank[4][:, 0:D], blockmask[:, b:b + 1], None, ALU.mult)
            v.tensor_tensor(crow[0:1, :], bank[5][0:1, 0:D], borow[0:1, :], ALU.add).then_inc(s_zm, 1)

            def layer_norm(n):
                for t in range(NT):
                    if n == 0 and t % TPC == 0:
                        dve.wait_ge(s_x, 16 * NC)
                    ins = v.bn_stats(ST[:, t, :], X[:, t, :])
                link(ins)
                for t in range(NT):
                    ins = v.bn_aggr(MV[:, t, :], ST[:, t, :])
                ins.then_inc(s_mv, 1)
                dve.wait_ge(s_sd, n + 1)
                link(v.reciprocal(RSTD[:, :], SD[:, :]))
                for c in range(NC):
                    wait(dve, s_tr, n * NC + c - 1)
                    for t in range(TPC):
                        T = c * TPC + t
                        ins = v.tensor_scalar(XN[:, c % 2, t, :], X[:, T, :], MV[:, T, 0:1], RSTD[:, T:T + 1],
                                              ALU.subtract, ALU.mult)
                    ins.then_inc(s_xn, 1)

            def add_gated(c, src, g, done):
                t4 = TMP[:, c % 2, :].rearrange("p (b t f) -> p b t f", b=2, t=2)
                for b in range(2):
                    gate = GATE[:, g, 2 * c + b, :].unsqueeze(1).to_broadcast([P, 2, D])
                    ins = v.tensor_tensor(t4[:, b], src[:, b], gate, ALU.mult)
                link(ins)
                xs = X[:, c * TPC:(c + 1) * TPC, :].rearrange("p t f -> p (t f)")
                ins = v.tensor_tensor(xs, xs, TMP[:, c % 2, :], ALU.add)
                ins.then_inc(done, 1)

            layer_norm(0)
            for h in range(2):
                dve.wait_ge(s_ez, h + 1)
                link(v.tensor_scalar(SIG[:, h, :], EZ[:, h, :], 1.0, None, ALU.add))
                v.reciprocal(SIG[:, h, :], SIG[:, h, :]).then_inc(s_sig, 1)
            for h in range(2):
                link(v.tensor_scalar(BU[:, h, :], bank[2 + h][:, 0:S], small[:, 0:1], None, ALU.add))
                dve.wait_ge(s_ae, h + 1)
                v.tensor_tensor_scan(HSC[:, h, :], AE[:, h, :], BU[:, h, :], 0.0, ALU.mult, ALU.add).then_inc(s_hs, 1)
            dve.wait_ge(s_gld, 16)
            for c in range(NC):
                dve.wait_ge(s_y, c + 1)
                add_gated(c, bank[6 + c % 2][:, :].rearrange("p (b t f) -> p b t f", b=2, t=2), 0, s_yr)
            dve.wait_ge(s_yr, NC)

            def bc_e(a):
                return a.unsqueeze(2).to_broadcast([P, NT, E])

            iota3 = iota[:, :].unsqueeze(1).to_broadcast([P, NT, E])

            def pick(values, best, onehot):
                link(v.tensor_reduce(best, values, AX, ALU.max))
                link(v.tensor_tensor(EQ[:, :, :], values, bc_e(best), ALU.is_lt))
                link(v.tensor_scalar(EQ[:, :, :], EQ[:, :, :], float(E), None, ALU.mult))
                link(v.tensor_tensor(EQ[:, :, :], EQ[:, :, :], iota3, ALU.add))
                link(v.tensor_reduce(idx[:, :], EQ[:, :, :], AX, ALU.min))
                return v.tensor_tensor(onehot, iota3, bc_e(idx[:, :]), ALU.is_equal)

            def softmax_shift(m):
                lg = bank[2][:, 0:NE].rearrange("p (t e) -> p t e", t=NT)
                link(v.tensor_reduce(m1[:, :], lg, AX, ALU.max))
                v.tensor_tensor(LG[:, :, :], lg, bc_e(m1[:, :]), ALU.subtract).then_inc(s_lg, 1)

            def softmax_end():
                link(v.tensor_reduce(ssum[:, :], PR[:, :, :], AX, ALU.add))
                link(v.reciprocal(ssum[:, :], ssum[:, :]))
                link(v.tensor_tensor(PR[:, :, :], PR[:, :, :], bc_e(ssum[:, :]), ALU.mult))

            def second(m):
                link(v.tensor_tensor(CD[:, :, :], PR[:, :, :], OH1[:, :, :], ALU.subtract))
                link(v.scalar_tensor_tensor(out=CD[:, :, :], in0=OH1[:, :, :], scalar=-4.0, in1=CD[:, :, :],
                                            op0=ALU.mult, op1=ALU.add))
                link(pick(CD[:, :, :], m, OH2[:, :, :]))

            layer_norm(1)
            dve.wait_ge(s_wm[0], 16 * 3)
            dve.wait_ge(s_cnt, 1)
            softmax_shift(0)
            dve.wait_ge(s_el, 1)
            softmax_end()
            link(pick(PR[:, :, :], m1[:, :], OH1[:, :, :]))
            v.tensor_reduce(cnt[:, :], OH1[:, :, :].rearrange("p t e -> p e t"), AX, ALU.add).then_inc(s_oh, 1)
            second(m2[:, :])
            link(v.tensor_tensor(ssum[:, :], m1[:, :], m2[:, :], ALU.add))
            link(v.tensor_scalar(ssum[:, :], ssum[:, :], 1e-12, None, ALU.max))
            link(v.reciprocal(ssum[:, :], ssum[:, :]))
            v.tensor_tensor(w1[:, :], m1[:, :], ssum[:, :], ALU.mult)
            link(v.tensor_tensor(w2[:, :], m2[:, :], ssum[:, :], ALU.mult))
            v.tensor_tensor(OH1[:, :, :], OH1[:, :, :], bc_e(w1[:, :]), ALU.mult)
            link(v.tensor_tensor(OH2[:, :, :], OH2[:, :, :], bc_e(w2[:, :]), ALU.mult))
            link(v.tensor_tensor(WT[:, :, :], OH1[:, :, :], OH2[:, :, :], ALU.add))
            dve.wait_ge(s_cnt, 2)
            link(v.tensor_scalar(pm[:, :], bank[3][:, 0:E], 0.5, None, ALU.is_ge))
            pmj = pm[:, :].unsqueeze(1).to_broadcast([P, E, E])
            link(v.tensor_scalar(smq[:, :, :], pmj, 1.0, -LOWEST, ALU.subtract, ALU.mult))
            link(v.tensor_tensor(sm[:, :, :], sim[:, :, :], pmj, ALU.mult))
            link(v.tensor_tensor(sm[:, :, :], sm[:, :, :], smq[:, :, :], ALU.add))
            link(v.tensor_reduce(bs[:, :], sm[:, :, :], AX, ALU.max))
            link(v.tensor_tensor(smc[:, :, :], sm[:, :, :], bs[:, :].unsqueeze(2).to_broadcast([P, E, E]), ALU.is_lt))
            link(v.tensor_scalar(smc[:, :, :], smc[:, :, :], float(E), None, ALU.mult))
            iotaj = iota[:, :].unsqueeze(1).to_broadcast([P, E, E])
            link(v.tensor_tensor(smc[:, :, :], smc[:, :, :], iotaj, ALU.add))
            link(v.tensor_reduce(bj[:, :], smc[:, :, :], AX, ALU.min))
            link(v.tensor_scalar(cnd[:, :], bs[:, :], THRESHOLD, None, ALU.is_ge))
            link(v.scalar_tensor_tensor(out=cnd[:, :], in0=pm[:, :], scalar=0.5, in1=cnd[:, :],
                                        op0=ALU.is_lt, op1=ALU.mult))
            link(v.tensor_tensor(bj[:, :], bj[:, :], iota[:, :], ALU.subtract))
            link(v.tensor_tensor(bj[:, :], bj[:, :], cnd[:, :], ALU.mult))
            link(v.tensor_tensor(emap[:, :], bj[:, :], iota[:, :], ALU.add))
            link(v.tensor_tensor(MM[:, :, :], emap[:, :].unsqueeze(2).to_broadcast([P, E, E]), iotaj, ALU.is_equal))
            for i in range(E):
                wi = WT[:, :, i].unsqueeze(1).to_broadcast([P, E, NT])
                mi = MM[:, i, :].unsqueeze(2).to_broadcast([P, E, NT])
                dst = WD if i == 0 else CD.rearrange("p t e -> p (t e)").rearrange("p (e t) -> p e t", e=E)
                link(v.tensor_tensor(dst[:, :, :], wi, mi, ALU.mult))
                if i:
                    link(v.tensor_tensor(WD[:, :, :], WD[:, :, :], dst[:, :, :], ALU.add))
            link(v.memset(ACC[:, :, :], 0.0))

            def accumulate(m, u, j, src):
                c = j % NC
                dve.wait_ge(s_dn[m], u + 1)
                wait(dve, s_acc[m], u - NC + 1 + (NC if m else 0))
                for t in range(TPC):
                    T = c * TPC + t
                    ins = v.scalar_tensor_tensor(out=ACC[:, T, :], in0=src[:, t * D:(t + 1) * D],
                                                 scalar=wstep[:, (j // NC) % 2, T:T + 1], in1=ACC[:, T, :],
                                                 op0=ALU.mult, op1=ALU.add)
                ins.then_inc(s_acc[m], 1)

            def step_weights(m, i, table, e0, n):
                wait(dve, s_acc[m], e0)
                ins = v.tensor_copy(wstep[:, 0:n, :], table)
                ins.then_inc(s_ws[m], 1)

            def moe0(i):
                step_weights(0, i, WD[:, bass.ds(2 * i, 2), :], i * 2 * NC, 2)
                dve.wait_ge(s_ws[0], i + 1)
                for j in range(2 * NC):
                    u = i * 2 * NC + j
                    dve.wait_ge(s_act[0], u + 1)
                    wait(dve, s_dn[0], u - 1)
                    v.tensor_tensor(HM0[:, j % 2, :], SG[:, j % 2, :], bank[2 + j % 2][:, :], ALU.mult).then_inc(s_hm, 1)
                    if j:
                        accumulate(0, u - 1, j - 1, bank[4 + (j - 1) % 2])
                accumulate(0, u, 2 * NC - 1, bank[4 + 1])

            moe0(0)
            with dve.Fori(1, E // 2) as i:
                moe0(i)
            dve.wait_ge(s_acc[0], E * NC)
            for c in range(NC):
                add_gated(c, ACC[:, c * TPC:(c + 1) * TPC, :].rearrange("p (b t) f -> p b t f", b=2), 1, s_acc[0])
            dve.wait_ge(s_acc[0], E * NC + NC)

            layer_norm(2)
            dve.wait_ge(s_wp, 16 * 4)
            link(v.memset(VT[:, :, :, :], 1.0))
            for c in range(NC):
                k = c % 2
                for w in range(2):
                    rope = [ropes[:, 2 * w + r, :].unsqueeze(1).to_broadcast([P, 2, S]) for r in range(2)]
                    r1, r2 = ((RT_1[:, k, :], RT_2[:, k, :]))
                    if w == 1 or c:
                        dve.wait_ge(s_rot, 6 * c + 3 * w)
                    dve.wait_ge(s_pj, 5 * c + 2 * w + 1)
                    v.tensor_tensor(r1.rearrange("p (s t) -> p s t", s=2),
                                    bank[2 * w][:, :].rearrange("p (s t) -> p s t", s=2), rope[0], ALU.mult
                                    ).then_inc(s_rot, 1)
                    dve.wait_ge(s_pj, 5 * c + 2 * w + 2)
                    v.tensor_tensor(r2.rearrange("p (s t) -> p s t", s=2),
                                    bank[2 * w + 1][:, :].rearrange("p (s t) -> p s t", s=2), rope[1], ALU.mult
                                    ).then_inc(s_rot, 1)
                    dve.wait_ge(s_rot, 6 * c + 3 * w + 2)
                    if w == 0:
                        v.tensor_tensor(QR[:, k, :], r1, r2, ALU.add).then_inc(s_rot, 1)
                    else:
                        v.scalar_tensor_tensor(out=KR[:, k, :], in0=r1, scalar=rel0[:, 0:1], in1=r2,
                                               op0=ALU.add, op1=ALU.add).then_inc(s_rot, 1)
                if c >= 2:
                    dve.wait_ge(s_qst[k], 16 * 5 * (c // 2))
                dve.wait_ge(s_pj, 5 * c + 5)
                for t in range(TPC):
                    ins = v.tensor_tensor(VT[:, k, t, :].rearrange("p (h v) -> p h v", v=VW)[:, :, 0:HD],
                                          bank[4][:, t * D:(t + 1) * D].rearrange("p (h v) -> p h v", v=HD),
                                          relv[:, :].unsqueeze(1).to_broadcast([P, H, HD]), ALU.add)
                ins.then_inc(s_v, 1)
                dve.wait_ge(s_rot, 6 * c + 6)
                for w, src in ((0, QR), (1, KR)):
                    dve.wait_ge(s_hi, 2 * c + w + 1)
                    v.tensor_tensor(LO[:, k, w, :], src[:, k, :], HI[:, k, w, :], ALU.subtract).then_inc(s_lo, 1)

            for k in range(2):
                dve.wait_ge(s_qst[k], 16 * 5 * NC // 2)
            v.memset(QG[:, :, :].bitcast(F32), 0.0)
            v.memset(KG[:, :, :].bitcast(F32), 0.0).then_inc(s_tb, 1)
            link(v.memset(GTB[:, :], 0.0))
            dve.wait_ge(s_tab, 16 * 7)
            v.tensor_tensor(relk[:, :, :], relk[:, :, :], rel0r[:, :].unsqueeze(1).to_broadcast([P, X0, HD]), ALU.subtract)
            link(v.tensor_scalar(GTf[0:25, :], GTf[0:25, :], rel0c[0:25, :], None, ALU.subtract))
            link(v.tensor_copy(GTB[0:25, :], GTf[0:25, :]))
            link(v.tensor_tensor(GTf[0:25, :], GTf[0:25, :], GTB[0:25, :], ALU.subtract))
            link(v.tensor_scalar(GTf[0:25, :], GTf[0:25, :], half_mask[0:25, :], None, ALU.mult))
            link(v.tensor_scalar(rel0c[0:25, :], half_mask[0:25, :], -1.0, 1.0, ALU.mult, ALU.add))
            v.scalar_tensor_tensor(out=GTB[0:25, :], in0=GTB[0:25, :], scalar=rel0c[0:25, :], in1=GTf[0:25, :],
                                   op0=ALU.mult, op1=ALU.add).then_inc(s_tb, 1)

            def bias_low(i):
                for g in range(18):
                    dve.wait_ge(s_bh, i * 18 + g + 1)
                    at = g * 16
                    v.tensor_tensor(BL[:, :, at:at + 16].rearrange("p h q -> p q h"),
                                    bank[g % RING][:, :].rearrange("p (q h) -> p q h", h=HS),
                                    BH[:, :, at:at + 16].rearrange("p h q -> p q h"), ALU.subtract).then_inc(s_bl, 1)

            def maxima(i, relative=False):
                for r in range(24):
                    dve.wait_ge(s_r1, i * 24 + r + 1)
                    dst = MX0[:, 2 * r:2 * r + 2, :] if r < 16 else MX1[:, 4 * (r - 16):4 * (r - 16) + 4, :]
                    v.tensor_reduce(dst.rearrange("p h b -> p (h b)"),
                                    bank[r % RING][:, :].rearrange("p (b c) -> p b c", c=32), AX, ALU.max,
                                    apply_transpose=True).then_inc(s_mx, 1)
                    if relative and r in (7, 13, 19):
                        relative_out(i - 1, (r // 6 - 1,))
                dve.wait_ge(s_mx, (i + 1) * 24)
                v.tensor_tensor(MX0[:, :, 4:8], MX0[:, :, 4:8], MX1[:, :, :], ALU.max).then_inc(s_mc, 1)

            def row_maxima(i):
                dve.wait_ge(s_tm, i + 1)
                wait(dve, s_mr, i * 32)
                v.tensor_reduce(NM[:, :, :], bank[7][:, 0:2 * P].rearrange("p (h g c) -> p h c g", h=2, g=4),
                                AX, ALU.max, negate=True).then_inc(s_nm, 1)

            def relative_out(i, units=range(4)):
                for w in units:
                    dve.wait_ge(s_rl, i * 4 + w + 1)
                    if w == 0:
                        wait(dve, s_rst, i * 16 * 8)
                    v.tensor_copy(RS[:, :, 16 * w:16 * w + 16].rearrange("p h i -> p i h"),
                                  bank[5 + w % 2][:, :].rearrange("p (i h) -> p i h", h=HS)).then_inc(s_re, 1)

            bias_low(0)
            maxima(0)
            row_maxima(0)
            with dve.Fori(1, NP) as i:
                bias_low(i)
                maxima(i, relative=True)
                row_maxima(i)
                relative_out(i - 1, (3,))
            relative_out(NP - 1)

            dve.wait_ge(s_gld, 32)
            for c in range(NC + 1):
                if c < NC:
                    k = c % 2
                    dve.wait_ge(s_cin[k], 48 * (c // 2 + 1))
                    wait(dve, s_db, c - 1)
                    v.reciprocal(DR[0:H, k, :], DN[0:H, k, :]).then_inc(s_dr, 1)
                    link(v.tensor_tensor(C1[:, k, :], C1[:, k, :], R1[:, k, :], ALU.add))
                    dve.wait_ge(s_db, c + 1)
                    wait(dve, s_y, NC + c - 1)
                    v.tensor_tensor(CX[:, k, :], C1[:, k, :], bank[k][:, :], ALU.mult).then_inc(s_cx, 1)
                if c:
                    dve.wait_ge(s_y, NC + c)
                    add_gated(c - 1, bank[6 + (c - 1) % 2][:, :].rearrange("p (b t f) -> p b t f", b=2, t=2), 0, s_yr)
            dve.wait_ge(s_yr, 2 * NC)

            layer_norm(3)
            dve.wait_ge(s_wm[1], 16 * 8)
            link(v.memset(RT1[32:33, :, :], 1.0))
            for c in range(NC):
                dve.wait_ge(s_cnt, 3 + c)
                wait(dve, s_m1, 1 + c - 1)
                v.tensor_scalar(RT1[0:32, c % 2, :], bank[3 + c % 2][0:32, :], br1[0:32, :], 0.0, ALU.add, ALU.max
                                ).then_inc(s_oh, 1)
            dve.wait_ge(s_m1, 1 + NC)
            softmax_shift(1)
            dve.wait_ge(s_el, 2)
            softmax_end()
            link(pick(PR[:, :, :], m1[:, :], OH1[:, :, :]))
            second(m2[:, :])

            for k in range(2):
                ins = v.tensor_copy(ROWS[k][:, :, D:RW], rowid[:, k, :].unsqueeze(2))
            ins.then_inc(s_ids, 1)
            link(v.tensor_tensor(ME[:, :, :].rearrange("p e t -> p t e"), OH1[:, :, :], OH2[:, :, :], ALU.add))
            for e in range(E):
                ins = v.tensor_tensor_scan(IN[:, e, :], ones[:, 0:NT], ME[:, e, :], 0.0, ALU.mult, ALU.add)
            link(ins)
            v.tensor_copy(tot[:, :].unsqueeze(2), IN[:, :, NT - 1:NT]).then_inc(s_tot, 1)
            link(v.tensor_tensor(EX[:, :, :], IN[:, :, :], ME[:, :, :], ALU.subtract))
            dve.wait_ge(s_rank, 1)
            c3 = cmp[:, 0:E * KT].rearrange("p (e k) -> p e k", e=E)
            link(v.tensor_tensor(c3, bank[6][:, E:2 * E].unsqueeze(2).to_broadcast([P, E, KT]),
                                 steps[:, 1, 0:KT].unsqueeze(1).to_broadcast([P, E, KT]), ALU.is_gt))
            link(v.tensor_reduce(tiles[:, :], c3, AX, ALU.add))
            link(v.tensor_tensor_scan(upto[:, :], ones[:, 0:E], tiles[:, :], 0.0, ALU.mult, ALU.add))
            link(v.tensor_tensor(offs[:, :], upto[:, :], tiles[:, :], ALU.subtract))
            link(v.scalar_tensor_tensor(out=offs[:, :], in0=offs[:, :], scalar=float(GT), in1=bank[6][:, 0:E],
                                        op0=ALU.mult, op1=ALU.add))
            link(v.tensor_tensor(EX[:, :, :], EX[:, :, :], offs[:, :].unsqueeze(2).to_broadcast([P, E, NT]), ALU.add))
            for k, oh in ((0, OH1), (1, OH2)):
                link(v.tensor_tensor(EQ[:, :, :], oh[:, :, :], EX[:, :, :].rearrange("p e t -> p t e"), ALU.mult))
                link(v.tensor_reduce(idx[:, :], EQ[:, :, :], AX, ALU.add))
                link(v.tensor_copy(dest[k][:, :], idx[:, :]))
            c3 = cmp[:, 0:NG * E].rearrange("p (n e) -> p n e", e=E)
            link(v.tensor_tensor(c3, upto[:, :].unsqueeze(1).to_broadcast([P, NG, E]),
                                 steps[:, 0, 0:NG].unsqueeze(2).to_broadcast([P, NG, E]), ALU.is_le))
            link(v.tensor_reduce(texp[:, :], c3, AX, ALU.add))
            link(v.tensor_scalar(texp[:, :], texp[:, :], float(E - 1), None, ALU.min))
            v.tensor_copy(texpu[:, :], texp[:, :]).then_inc(s_dest, 1)

            link(v.tensor_tensor(m2[:, :], m2[:, :], m1[:, :], ALU.subtract))
            v.tensor_scalar(m2[:, :], m2[:, :], 0.5, None, ALU.mult).then_inc(s_lg, 1)
            dve.wait_ge(s_el, 3)
            link(v.tensor_scalar(ssum[:, :], w2[:, :], 1.0, None, ALU.add))
            link(v.reciprocal(w1[:, :], ssum[:, :]))
            link(v.tensor_tensor(w2[:, :], w2[:, :], w1[:, :], ALU.mult))
            v.tensor_tensor(OH1[:, :, :], OH1[:, :, :], bc_e(w1[:, :]), ALU.mult)
            link(v.tensor_tensor(OH2[:, :, :], OH2[:, :, :], bc_e(w2[:, :]), ALU.mult))
            v.memset(WE[:, 0, :], 1.0)
            v.tensor_tensor(WE[:, 1:, :].rearrange("p e t -> p t e"), OH1[:, :, :], OH2[:, :, :], ALU.add
                            ).then_inc(s_lg, 1)
            for c in range(NC):
                dve.wait_ge(s_wct, 2 * c + 1)
                v.tensor_copy(WCT[0:E + 1, c % 2, :], bank[c % 2][0:E + 1, :]).then_inc(s_wcc, 1)
                dve.wait_ge(s_wct, 2 * c + 2)
                dve.wait_ge(s_sout, c + 1)
                acc = ACC[:, c * TPC:(c + 1) * TPC, :].rearrange("p t f -> p (t f)")
                link(v.tensor_tensor(acc, acc, bank[2 + c % 2][:, :], ALU.add))
                add_gated(c, acc.rearrange("p (b t f) -> p b t f", b=2, t=2), 1, s_res)

            def tile_in(j, k):
                dve.wait_ge(s_xp, j + 1)
                if not isinstance(j, int) or j >= UT:
                    dve.wait_ge(s_yo[k], 32 * (j // UT) if isinstance(j, int) else step[0] * 32 + (32 if k < step[1] else 0))
                v.tensor_copy(rid[:, k, :].unsqueeze(2), XR[:, k, :, D:RW])
                wait(dve, s_up[1], 2 * (j - 1))
                v.tensor_copy(XT[:, k % 2, :], bank[4 + k % 2][:, 0:GT]).then_inc(s_xt, 1)

            def results(j, k):
                dve.wait_ge(s_dn[1], j + 1)
                v.tensor_copy(YS[:, k, :, :].rearrange("p r n -> p (r n)"), bank[6 + k % 2][:, 0:GT]).then_inc(s_ys, 1)

            step = [0, 0]
            tile_in(0, 0)
            for j in range(UT):
                tile_in(j + 1, (j + 1) % UT)
                if j:
                    results(j - 1, j - 1)
            with dve.Fori(1, NG // UT - 1) as i:
                for k in range(UT):
                    step[:] = (i, 0) if k < UT - 1 else (i + 1, 0)
                    tile_in(i * UT + k + 1, (k + 1) % UT)
                    results(i * UT + k - 1, (k - 1) % UT)
            last = NG - UT
            for k in range(UT):
                if k < UT - 1:
                    tile_in(last + k + 1, k + 1)
                results(last + k - 1, (k - 1) % UT)
            results(NG - 1, UT - 1)
            dve.wait_ge(s_res, NC)
            for c in range(NC):
                dve.wait_ge(s_y1, c + 1)
                dve.wait_ge(s_y2, c + 1)
                y = [YG[k][:, c * TPC:(c + 1) * TPC, :].rearrange("p t f -> p (t f)") for k in range(2)]
                link(v.tensor_tensor(y[0], y[0], y[1], ALU.add))
                add_gated(c, y[0].rearrange("p (b t f) -> p b t f", b=2, t=2), 1, s_fin)

        @block.tensor
        def _(pe):
            mm = nc.tensor.matmul

            pe.wait_ge(s_cm, 1)
            pe.wait_ge(s_set, 1)
            pe.wait_ge(s_dv, 8)
            for l in range(2):
                for m in range(6):
                    at = (l * 6 + m) * B
                    mm(bank[0][:, at:at + B], wmod[:, l, m * D:(m + 1) * D], scT[:, l, :], start=True, stop=True)
            for l in range(2):
                for g, m in ((0, 2), (1, 5)):
                    at = (2 * l + g) * D
                    ins = mm(bank[1][0:B, at:at + D], scT[:, l, :], wmod[:, l, m * D:(m + 1) * D], start=True, stop=True)
            ins.then_inc(s_mod, 1)
            mm(bank[4][:, 0:D], Wcr[:, :], WoT[:, :], start=True, stop=True)
            mm(bank[5][0:1, 0:D], bcol[:, :], WoT[:, :], start=True, stop=True).then_inc(s_m1, 1)

            def layer_norm(n):
                for c in range(NC):
                    pe.wait_ge(s_xn, n * NC + c + 1)
                    wait(pe, s_hT, n * NC + c - 1)
                    if n == 0 and c == 0:
                        pe.wait_ge(s_gg, 1)
                    for t in range(TPC):
                        ins = nc.tensor.transpose(bank[c % 2][:, t * P:(t + 1) * P], XN[:, c % 2, t, :], ident[:, :])
                    ins.then_inc(s_tr, 1)

            layer_norm(0)
            for h in range(2):
                pe.wait_ge(s_hT, (h + 1) * NC // 2)
                for pad, at in ((WTpad, S), (WBpad, 0)):
                    for b in range(8):
                        ins = mm(bank[2 + h][:, at:at + S], pad[:, 112 - N * b:240 - N * b],
                                 hT[:, (8 * h + b) * S:(8 * h + b + 1) * S], start=(b == 0), stop=(b == 7))
                ins.then_inc(s_ssm, 1)
            pe.wait_ge(s_zm, 1)
            for c in range(NC):
                pe.wait_ge(s_hs, c // 4 + 1)
                wait(pe, s_yr, c - 1)
                for t in range(TPC):
                    T = c * TPC + t
                    b = T // 2
                    dst = bank[6 + c % 2][:, t * D:(t + 1) * D]
                    at = (T % 2) * P
                    mm(dst, HSC[:, b // 8, at:at + P], ZM[:, b % 8, :], start=True, stop=False)
                    mm(dst, hT[:, T * P:(T + 1) * P], M2[:, :], start=False, stop=False)
                    ins = mm(dst, ones[0:1, :], crow[0:1, :], start=False, stop=True)
                ins.then_inc(s_y, 1)

            layer_norm(1)
            pe.wait_ge(s_wm[0], 16 * 3)
            for T in range(NT):
                if T % TPC == 0:
                    pe.wait_ge(s_hT, NC + T // TPC + 1)
                ins = mm(bank[2][:, T * E:(T + 1) * E], hT[:, T * P:(T + 1) * P], gateT[:, :], start=True, stop=True)
            ins.then_inc(s_cnt, 1)
            pe.wait_ge(s_oh, 1)
            mm(bank[3][:, 0:E], ones[:, :], cnt[:, :], start=True, stop=True).then_inc(s_cnt, 1)

            def down0(u, j):
                k = (j // NC) % 2
                pe.wait_ge(s_hm, u + 1)
                wait(pe, s_acc[0], u - 1)
                for t in range(TPC):
                    ins = mm(bank[4 + j % 2][:, t * D:(t + 1) * D], HM0[:, j % 2, t * P:(t + 1) * P],
                             W0[:, k, 2 * F0:3 * F0], start=True, stop=True)
                ins.then_inc(s_dn[0], 1)

            def moe0(i):
                for j in range(2 * NC):
                    u = i * 2 * NC + j
                    k, c = j // NC, j % NC
                    if c == 0:
                        pe.wait_ge(s_w[0][k], 16 * i + 16)
                    if j == 0 and isinstance(i, int):
                        pe.wait_ge(s_ws[0], 1)
                    wait(pe, s_hm, u - 1)
                    mm(bank[j % 2][:, :], W0[:, k, 0:F0], chunk(hT, c), start=True, stop=True)
                    mm(bank[2 + j % 2][:, :], W0[:, k, F0:2 * F0], chunk(hT, c), start=True, stop=True
                       ).then_inc(s_up[0], 1)
                    if j:
                        down0(u - 1, j - 1)
                down0(u, 2 * NC - 1)

            moe0(0)
            with pe.Fori(1, E // 2) as i:
                moe0(i)

            layer_norm(2)
            pe.wait_ge(s_wp, 16 * 4)
            for c in range(NC):
                pe.wait_ge(s_hT, 3 * NC)
                for w in range(4):
                    if c:
                        pe.wait_ge(s_rot, 6 * (c - 1) + 3 * (w // 2) + w % 2 + 1)
                    mm(bank[w][:, :], Wqkv[:, w, :], chunk(hT, c), start=True, stop=True).then_inc(s_pj, 1)
                wait(pe, s_v, c)
                for t in range(TPC):
                    T = c * TPC + t
                    ins = mm(bank[4][:, t * D:(t + 1) * D], hT[:, T * P:(T + 1) * P], Wqkv[:, 4, :],
                             start=True, stop=True)
                ins.then_inc(s_pj, 1)

            def relative_scores(i, banks):
                for g in banks:
                    if g < RING:
                        if not isinstance(i, int):
                            pe.wait_ge(s_ex, (i - 1) * 24 + 21 + g + 1)
                    else:
                        pe.wait_ge(s_bl, i * 18 + g - RING + 1)
                    for x in range(16):
                        q = g * 16 + x
                        local = q if q < X0 else q - X0
                        col = q if q < X0 else q - X0 + P
                        ins = mm(bank[g % RING][:, x * HS:(x + 1) * HS], GTB[:, X0 - local:X0 - local + P],
                                 QG[:, :, col], start=True, stop=True)
                    ins.then_inc(s_gen, 1)

            def scores(i, rnd, banks=range(24)):
                done = s_r1 if rnd == 1 else s_r2
                for r in banks:
                    if r < RING:
                        if rnd == 1:
                            pe.wait_ge(s_bl, i * 18 + 15 + r + 1)
                        else:
                            pe.wait_ge(s_mx, i * 24 + 21 + r + 1)
                    else:
                        pe.wait_ge(s_mx if rnd == 1 else s_ex, i * 24 + r - RING + 1)
                    if r == 0 and rnd == 1:
                        pe.wait_ge(s_bl, i * 18 + 18)
                    dst = bank[r % RING]
                    if r < 16:
                        d3 = dst[:, :].rearrange("p (h q) -> p h q", q=S)
                        for x in range(2):
                            h = 2 * r + x
                            mm(d3[:, x, :], KG[:, h, 0:P], QG[:, h, :], start=(x == 0), stop=False,
                               skip_group_check=True)
                        ins = mm(d3[:, :, 0:X0], identb[:, :], BH[:, 2 * r:2 * r + 2, 0:X0], start=False,
                                 stop=(rnd == 1), skip_group_check=True)
                        if rnd == 2:
                            ins = mm(d3[:, :, 0:X0], identb[:, :], BL[:, 2 * r:2 * r + 2, 0:X0], start=False,
                                     stop=True, skip_group_check=True)
                    else:
                        h0 = 4 * (r - 16)
                        for x in range(4):
                            mm(dst[:, x * P:(x + 1) * P], KG[:, h0 + x, P:S], QG[:, h0 + x, P:S], start=(x == 0),
                               stop=False, skip_group_check=True)
                        ins = mm(dst[:, :].rearrange("p (h q) -> p h q", q=P), identb[:, :], BH[:, h0:h0 + 4, X0:QB],
                                 start=False, stop=(rnd == 1), skip_group_check=True)
                        if rnd == 2:
                            ins = mm(dst[:, :].rearrange("p (h q) -> p h q", q=P), identb[:, :],
                                     BL[:, h0:h0 + 4, X0:QB], start=False, stop=True, skip_group_check=True)
                    ins.then_inc(done, 1)

            def transpose_maxima(i):
                pe.wait_ge(s_mc, i + 1)
                wait(pe, s_nm, i)
                for g in range(2):
                    ins = nc.tensor.transpose(bank[7][:, g * P:(g + 1) * P],
                                              MX0[:, g * H:(g + 1) * H, :].rearrange("p h b -> p (h b)"), ident[:, :])
                ins.then_inc(s_tm, 1)

            def weighted_values(i, units=range(4)):
                if units[0] == 0:
                    pe.wait_ge(s_vin, (i + 1) * 16)
                    pe.wait_ge(s_ex, (i + 1) * 24)
                for w in units:
                    s, hb = w // 2, w % 2
                    pe.wait_ge(s_pe, i * 4 + w - 1 if w >= 2 else i * 4)
                    for g in range(2):
                        for j in range(4):
                            h = 4 * (2 * hb + g) + j
                            mm(bank[3 + w % 2][32 * j:32 * j + VW, g * S:(g + 1) * S], VS[:, 2 * s, h, :],
                               PT0[:, 2 * h + s, :], start=True, stop=False, skip_group_check=True)
                        for j in range(4):
                            h = 4 * (2 * hb + g) + j
                            ins = mm(bank[3 + w % 2][32 * j:32 * j + VW, g * S + P:(g + 1) * S],
                                     VS[:, 2 * s + 1, h, :], PT1[:, 2 * h + s, :], start=False, stop=True,
                                     skip_group_check=True)
                    ins.then_inc(s_pv, 1)

            def weighted_relative(i, parts=range(8)):
                for part in parts:
                    w = part // 2
                    if part % 2 == 0:
                        pe.wait_ge(s_re, i * 4 + w - 1 if w >= 2 else i * 4)
                    for x in range(8 * (part % 2), 8 * (part % 2) + 8):
                        a = 16 * w + x
                        for j in range(4):
                            q = 64 * j + a
                            dst = bank[5 + w % 2][32 * j:32 * j + HD, x * HS:(x + 1) * HS]
                            if q < P:
                                ins = mm(dst, relk[:, q, :], PT0[:, :, q], start=True, stop=True,
                                         skip_group_check=True)
                            else:
                                near = q < P + REL - 1
                                ins = mm(dst, relk[:, q - P, :], PT1[:, :, q - P], start=True, stop=not near,
                                         skip_group_check=True)
                                if near:
                                    ins = mm(dst, relk[:, q, :], PT0[:, :, q], start=False, stop=True,
                                             skip_group_check=True)
                    if part % 2:
                        ins.then_inc(s_rl, 1)

            pe.wait_ge(s_tab, 16 * 7)
            pe.wait_ge(s_tb, 2)
            pe.wait_ge(s_in, 16 * 7)
            relative_scores(0, range(18))
            scores(0, 1)
            transpose_maxima(0)
            pe.wait_ge(s_mr, 32)
            scores(0, 2)
            with pe.Fori(1, NP) as i:
                weighted_values(i - 1, (0, 1))
                pe.wait_ge(s_in, (i + 1) * 16 * 7)
                relative_scores(i, range(0, 6))
                weighted_values(i - 1, (2,))
                relative_scores(i, range(6, 12))
                weighted_values(i - 1, (3,))
                relative_scores(i, range(12, 18))
                for part in range(8):
                    scores(i, 1, range(3 * part, 3 * part + 3))
                    weighted_relative(i - 1, (part,))
                transpose_maxima(i)
                pe.wait_ge(s_mr, (i + 1) * 32)
                scores(i, 2)
            weighted_values(NP - 1)
            weighted_relative(NP - 1)

            pe.wait_ge(s_wo, 32)
            for c in range(NC + 1):
                if c < NC:
                    pe.wait_ge(s_dr, c + 1)
                    wait(pe, s_cx, c - 1)
                    mm(bank[c % 2][:, :], sel16[0:H, :], DR[0:H, c % 2, :], start=True, stop=True).then_inc(s_db, 1)
                if c:
                    k = (c - 1) % 2
                    pe.wait_ge(s_cx, c)
                    wait(pe, s_yr, NC + c - 2)
                    for t in range(TPC):
                        ins = mm(bank[6 + k][:, t * D:(t + 1) * D], CX[:, k, t * P:(t + 1) * P], woT1[:, :],
                                 start=True, stop=True)
                    ins.then_inc(s_y, 1)

            layer_norm(3)
            pe.wait_ge(s_wm[1], 16 * 8)
            for c in range(NC + 1):
                if c < NC:
                    pe.wait_ge(s_hT, 3 * NC + c + 1)
                    wait(pe, s_oh, 1 + c - 1) if c >= 2 else None
                    mm(bank[3 + c % 2][0:32, :], Wr1[:, :], chunk(hT, c), start=True, stop=True).then_inc(s_cnt, 1)
                if c:
                    pe.wait_ge(s_oh, 1 + c)
                    for t in range(TPC):
                        T = (c - 1) * TPC + t
                        ins = mm(bank[2][:, T * E:(T + 1) * E], RT1[0:33, (c - 1) % 2, t * P:(t + 1) * P],
                                 Wr2[0:33, :], start=True, stop=True)
                    ins.then_inc(s_m1, 1)
            for c in range(NC):
                if c >= 2:
                    pe.wait_ge(s_rows, 2 * (c - 1))
                for t in range(TPC):
                    T = c * TPC + t
                    ins = nc.tensor.transpose(bank[6 + c % 2][:, t * P:(t + 1) * P], hT[:, T * P:(T + 1) * P],
                                              ident[:, :])
                ins.then_inc(s_back, 1)

            def ranks():
                pe.wait_ge(s_tot, 1)
                pe.wait_ge(s_rows, 2 * NC)
                mm(bank[6][:, 0:E], below[:, :], tot[:, :], start=True, stop=True, skip_group_check=True)
                mm(bank[6][:, E:2 * E], ones[:, :], tot[:, :], start=True, stop=True, skip_group_check=True
                   ).then_inc(s_rank, 1)

            pe.wait_ge(s_sw, 16)
            for c in range(NC + 1):
                if c < NC:
                    for b in range(KB1):
                        if c:
                            pe.wait_ge(s_sact, (c - 1) * KB1 + b + 1)
                        elif b >= 3:
                            pe.wait_ge(s_oh, 1 + NC)
                        mm(bank[b][:, :], W1S[:, b * P:(b + 1) * P], chunk(hT, c), start=True, stop=True
                           ).then_inc(s_sup, 1)
                if c == RANK_AT:
                    ranks()
                if c:
                    pe.wait_ge(s_sact, c * KB1)
                    wait(pe, s_sout, c - 2)
                    for t in range(TPC):
                        for b in range(KB1):
                            ins = mm(bank[4 + (c - 1) % 2][:, t * D:(t + 1) * D],
                                     HM1[:, (c - 1) % 2, b, t * P:(t + 1) * P],
                                     W1S[:, I1 + b * D:I1 + (b + 1) * D], start=(b == 0), stop=(b == KB1 - 1))
                    ins.then_inc(s_sdn, 1)
            pe.wait_ge(s_lg, 4)
            for c in range(NC):
                if c >= 2:
                    pe.wait_ge(s_wcc, c - 1)
                for t in range(TPC):
                    T = c * TPC + t
                    ins = nc.tensor.transpose(bank[c % 2][0:E + 1, t * P:(t + 1) * P], WE[:, :, T], ident[:, :])
                ins.then_inc(s_wct, 1)
                pe.wait_ge(s_wcc, c + 1)
                wait(pe, s_res, c - 1)
                for t in range(TPC):
                    ins = mm(bank[2 + c % 2][:, t * D:(t + 1) * D], WCT[0:E + 1, c % 2, t * P:(t + 1) * P],
                             be2[0:E + 1, :], start=True, stop=True)
                ins.then_inc(s_wct, 1)

            def transpose_tile(j, k, arrived):
                pe.wait_ge(s_xr[k], arrived)
                wait(pe, s_xt, j - 1)
                for r in range(2):
                    ins = nc.tensor.transpose(bank[4 + k % 2][:, r * P:(r + 1) * P], XR[:, k, r, 0:D], ident[:, :])
                ins.then_inc(s_xp, 1)

            def up_tile(j, k, arrived):
                pe.wait_ge(s_xt, j + 1)
                pe.wait_ge(s_ew[k], arrived)
                for b in range(KB1):
                    if b % 2 == 0:
                        wait(pe, s_act[1], (j - 2) * KB1 + b + 2)
                    ins = mm(bank[2 * (k % 2) + b // 2][:, b % 2 * GT:(b % 2 + 1) * GT], W1[:, k, b * P:(b + 1) * P],
                             XT[:, k % 2, :], start=True, stop=True, skip_group_check=True)
                    if b % 2:
                        ins.then_inc(s_up[1], 1)

            def down_tile(j, k):
                pe.wait_ge(s_act[1], (j + 1) * KB1)
                wait(pe, s_ys, j - 1)
                for r in range(2):
                    for b in range(KB1):
                        ins = mm(bank[6 + k % 2][:, r * D:(r + 1) * D], HMT[:, k % 2, b, r * P:(r + 1) * P],
                                 W1[:, k, I1 + b * D:I1 + (b + 1) * D], start=(b == 0), stop=(b == KB1 - 1),
                                 skip_group_check=True)
                ins.then_inc(s_dn[1], 1)

            pe.wait_ge(s_res, NC)
            transpose_tile(0, 0, 16)
            for j in range(UT):
                up_tile(j, j, 16)
                transpose_tile(j + 1, (j + 1) % UT, 16 if j < UT - 1 else 32)
                if j:
                    down_tile(j - 1, j - 1)
            with pe.Fori(1, NG // UT - 1) as i:
                for k in range(UT):
                    up_tile(i * UT + k, k, 16 * i + 16)
                    transpose_tile(i * UT + k + 1, (k + 1) % UT, 16 * i + (16 if k < UT - 1 else 32))
                    down_tile(i * UT + k - 1, (k - 1) % UT)
            last = NG - UT
            for k in range(UT):
                up_tile(last + k, k, 16 * (NG // UT))
                if k < UT - 1:
                    transpose_tile(last + k + 1, k + 1, 16 * (NG // UT))
                down_tile(last + k - 1, (k - 1) % UT)
            down_tile(NG - 1, UT - 1)


_SHAPE = (16, 256, 128)


def constants():
    import numpy as np
    k = {}
    k["ident"] = np.eye(P, dtype=np.float32)
    k["below"] = np.triu(np.ones((P, P), dtype=np.float32), 1)
    token = (np.arange(NT)[None, :] * P + np.arange(P)[:, None]).astype(np.float32)
    k["rowid"] = np.stack([token, token + np.float32(TOK)], axis=1)
    count = np.arange(64, dtype=np.float32)
    k["steps"] = np.tile(np.stack([count, count * np.float32(GT)])[None], (P, 1, 1))
    k["padding"] = np.zeros((NG * GT // 8, RW), dtype=np.float32)
    k["padding"][:, D] = 2 * TOK + np.arange(NG * GT // 8)
    k["blockmask"] = np.repeat(np.eye(8, dtype=np.float32), N, axis=0)
    k["iota"] = np.tile(np.arange(E, dtype=np.float32), (P, 1))
    k["onesrow"] = np.ones((1, HS, S), dtype=np.uint16) * np.uint16(0x3F80)
    k["zerorow"] = np.zeros((1, HS, S), dtype=np.uint16)
    k["sel16"] = np.repeat(np.eye(H, dtype=np.float32), HD, axis=1)
    low = np.zeros((25, 1), np.float32)
    low[8:16] = 1
    k["lowrows"] = low
    freq = (np.float32(1.0) / np.float32(10000.0) ** (np.arange(0, HD, 2, dtype=np.float32) / np.float32(HD)))
    ang = np.outer(np.arange(S, dtype=np.float32), freq.astype(np.float32)).astype(np.float32)
    cos = np.repeat(np.cos(ang), 2, axis=1).T
    sin = np.repeat(np.sin(ang), 2, axis=1).T.copy()
    sin[0::2] *= -1
    cos, sin = np.tile(cos, (H, 1)), np.tile(sin, (H, 1))
    r = np.float32(HD) ** np.float32(-0.5)
    k["ropes"] = np.stack([cos * r, sin * r, cos, sin], axis=1).astype(np.float32)
    return k


def kernel(**inputs):
    import numpy as np
    import concourse.bacc as bacc
    from concourse.bass_utils import run_bass_kernel_spmd

    a = {n: np.asarray(x) for n, x in inputs.items()}
    k = constants()
    L = {}
    L["x"] = a["L0_attn_x"].reshape(TOK, D)
    L["cT"] = np.stack([a["L0_c"].T, a["L1_c"].T], axis=1)
    L["wmod"] = np.stack([a["L0_wmod"], a["L1_wmod"]], axis=1)
    L["wbT"] = a["L0_attn_W_b"].T
    L["wt16"] = np.repeat(a["L0_attn_W_t"].T, N, axis=1)
    L["wc8"] = np.tile(a["L0_attn_W_c"], (1, 8))
    L["woT0"] = a["L0_attn_W_o"].T
    L["bb8"] = np.tile(a["L0_attn_b_b"], 8)[:, None]
    L["A8"] = np.tile(a["L0_attn_A"], 8)[:, None]
    L["bt"] = np.tile(a["L0_attn_b_t"], P)[:, None]
    L["Dv"] = a["L0_attn_D"][:, None]
    L["bc"] = a["L0_attn_b_c"][:, None]
    L["bo"] = a["L0_attn_b_o"][None, :]
    L["gateT"] = a["L0_ffn_gate_weight"].T
    L["sim"] = np.tile(a["L0_ffn_similarity_matrix"][None], (P, 1, 1))
    L["w0"] = np.concatenate([a["L0_ffn_gate_up_proj"].transpose(0, 2, 1), a["L0_ffn_down_proj"].transpose(0, 2, 1)],
                             axis=2)
    swap = np.arange(D).reshape(-1, 2)[:, ::-1].reshape(-1)
    wq, wk, wv = a["L1_attn_w_q"], a["L1_attn_w_k"], a["L1_attn_w_v"]
    L["wqkv"] = np.stack([wq.T, wq[swap].T, wk.T, wk[swap].T, wv.T], axis=1)
    L["woT1"] = a["L1_attn_w_o"].T
    rel = a["L1_attn_rel_emb"]
    L["rel0"] = np.tile(rel[0], H)[:, None]
    L["rel0r"] = np.tile(rel[0][None], (P, 1))
    L["relk"] = rel[np.clip(np.arange(P)[:, None] - np.arange(X0)[None, :], -REL, REL) + REL]
    gt = rel[np.clip(np.arange(X0 + P) - X0, -REL, REL) + REL].T
    mask = np.where(np.arange(X0 + P)[None, :] > X0, np.float32(NEG), np.float32(0.0))
    L["gt"] = np.concatenate([gt, gt, gt, mask], axis=0)
    L["rel0c"] = np.concatenate([rel[0], rel[0], rel[0], np.zeros(1, np.float32)])[:, None]
    L["wr1"] = a["L1_ffn_Wr1"]
    L["wr2"] = np.concatenate([a["L1_ffn_Wr2"], a["L1_ffn_br2"][None]], axis=0)
    L["br1"] = a["L1_ffn_br1"][:, None]
    L["be2"] = np.concatenate([a["L1_ffn_bs2"][None], a["L1_ffn_be2"]], axis=0)
    up = np.concatenate([a["L1_ffn_Ws1"][None], a["L1_ffn_We1"]], axis=0)
    down = np.concatenate([a["L1_ffn_Ws2"][None], a["L1_ffn_We2"]], axis=0)
    down = down.reshape(E + 1, KB1, P, D).transpose(0, 2, 1, 3).reshape(E + 1, P, KB1 * D)
    bias = np.concatenate([a["L1_ffn_bs1"][None], a["L1_ffn_be1"]], axis=0).reshape(E + 1, KB1, P).transpose(0, 2, 1)
    packed = np.concatenate([up, down, bias], axis=2)
    L["w1s"], L["w1"] = packed[0], packed[1:]
    L.update(k)

    nc = bacc.Bacc("TRN2", target_bir_lowering=False, num_devices=1)
    arrays, args = {}, {}
    for name, v in L.items():
        v = np.ascontiguousarray(v)
        arrays[f"in_{name}"] = v
        dt = BF16 if v.dtype == np.uint16 else mybir.dt.from_np(v.dtype)
        if v.dtype == np.uint16:
            import ml_dtypes
            v = v.view(ml_dtypes.bfloat16)
            arrays[f"in_{name}"] = v
        args[name] = nc.dram_tensor(f"in_{name}", v.shape, dt, kind="ExternalInput").ap()
    out = nc.dram_tensor("out_dram", (TOK, D), F32, kind="ExternalOutput").ap()
    build(nc, args, out)
    r = run_bass_kernel_spmd(nc, [arrays], core_ids=[0])
    return r.results[0]["out_dram"].reshape(_SHAPE)
```

```python
from contextlib import ExitStack

import concourse.bass as bass
from concourse import mybir

F32 = mybir.dt.float32
BF16 = mybir.dt.bfloat16
U32 = mybir.dt.uint32
ALU = mybir.AluOpType
ACT = mybir.ActivationFunctionType
AX = mybir.AxisListType.X

P = 128
B, S, D = 16, 256, 128
TOK = B * S
NT = TOK // P
CH = 512
NC = TOK // CH
TPC = CH // P
N = 16
H, HD = 16, 8
REL = 32
EPS = 1e-5
NEG = -1e18
E = 8
F0 = 128
I1 = 512
KB1 = I1 // P
THRESHOLD = 0.7
RANK_AT = 0
NP = B // 2
HS = 2 * H
X0 = 160
QB = X0 + P
RING = 3
RING2 = 5
VW = HD + 1
LOWEST = -3e38
W1W = I1 + I1 + KB1 + D
OB = I1 + I1 + KB1
GT = 256
UT = 4
NG = (2 * TOK + E * (GT - 1)) // GT
FULL = (NG - 1) // UT
LAST = NG - FULL * UT
RW = D + 1
KT = TOK // GT


def build(nc, A, out):
    ctx = ExitStack()
    with ctx:
        def sb(name, shape, dt=F32):
            return ctx.enter_context(nc.sbuf_tensor("sb_" + name, shape, dt))

        def sem(name):
            return ctx.enter_context(nc.semaphore(name))

        bank = [ctx.enter_context(nc.psum_tensor(f"bank{i}", [P, 512], F32)) for i in range(8)]

        def scratch(name, shape, dt=F32):
            return nc.dram_tensor(name, shape, dt).ap()

        X = sb("X", [P, NT, D])
        GATE = sb("GATE", [P, 2, B, D])
        ident = sb("ident", [P, P])
        identb = sb("identb", [P, P], BF16)
        ones = sb("ones", [P, P])
        cT = sb("cT", [P, 2, B])
        scT = sb("scT", [P, 2, B])
        MOD = sb("MOD", [P, 2, 6, B])
        GG = sb("GG", [B, 4, D])
        GT1 = sb("GT1", [B, 4, D])
        ST = sb("ST", [P, NT, 6])
        MV = sb("MV", [P, NT, 2])
        RSTD = sb("RSTD", [P, NT])
        SD = sb("SD", [P, NT])
        XN = sb("XN", [P, 2, TPC, D])
        epsc = sb("epsc", [P, 1])
        TMP = sb("TMP", [P, 2, CH])
        ARENA = 154 * 1024 // 4
        arena = sb("arena", [P, ARENA])

        class Region:

            def __init__(self, at=0):
                self.at = at

            def take(self, n, dt=F32):
                words = n if dt == F32 else (n + 1) // 2
                v = arena[:, self.at:self.at + words]
                self.at += words
                assert self.at <= ARENA, self.at * 4
                return v if dt == F32 else v.bitcast(BF16)

        R = Region()
        hT = R.take(TOK)
        ACC = R.take(NT * D).rearrange("p (t d) -> p t d", t=NT)
        dense_base = R.at

        R = Region(dense_base)
        wmod = R.take(2 * 6 * D).rearrange("p (l n) -> p l n", l=2)
        WBpad = R.take(240)
        WTpad = R.take(240)
        Wcr = R.take(P)
        WoT = R.take(D)
        M2 = R.take(D)
        small = R.take(16)
        bcol = R.take(1)
        borow = R.take(D)
        crow = R.take(D)
        blockmask = R.take(8)
        ZM = R.take(8 * D).rearrange("p (b o) -> p b o", b=8)
        EZ = R.take(2 * S).rearrange("p (h t) -> p h t", h=2)
        SIG = R.take(2 * S).rearrange("p (h t) -> p h t", h=2)
        AE = R.take(2 * S).rearrange("p (h t) -> p h t", h=2)
        BU = R.take(2 * S).rearrange("p (h t) -> p h t", h=2)
        HSC = R.take(2 * S).rearrange("p (h t) -> p h t", h=2)

        scan_end = R.at

        R = Region(dense_base)
        gateT = R.take(E)
        sim = R.take(E * E).rearrange("p (i j) -> p i j", i=E)
        iota = R.take(E)
        NE = NT * E
        def table(n=NE):
            return R.take(n)
        LG, PR, EQ, OH1, OH2, CD, WT = [table().rearrange("p (t e) -> p t e", t=NT) for _ in range(7)]
        m1, m2, ssum, idx, w1, w2 = [table(NT) for _ in range(6)]
        cnt, pm = table(E), table(E)
        sm, smq, smc = [table(E * E).rearrange("p (i j) -> p i j", i=E) for _ in range(3)]
        bs, bj, cnd, emap = [table(E) for _ in range(4)]
        MM = table(E * E).rearrange("p (i j) -> p i j", i=E)
        WD = R.take(NE).rearrange("p (e t) -> p e t", e=E)
        wstep = R.take(2 * NT).rearrange("p (s t) -> p s t", s=2)
        moe_base = R.at
        W0 = R.take(2 * 3 * F0).rearrange("p (s n) -> p s n", s=2)
        SG = R.take(2 * CH).rearrange("p (s n) -> p s n", s=2)
        HM0 = R.take(2 * CH).rearrange("p (s n) -> p s n", s=2)
        cmp4 = R.take(E * NE)
        moe0_end = R.at
        R = Region(moe_base)
        Wr1 = R.take(32)
        Wr2 = R.take(E)
        br1 = R.take(1)
        RT1 = R.take(2 * CH).rearrange("p (s n) -> p s n", s=2)
        rowid = R.take(2 * NT).rearrange("p (k t) -> p k t", k=2)
        steps = R.take(2 * 64).rearrange("p (k n) -> p k n", k=2)
        below = R.take(P)
        ME, IN, EX = [R.take(NE).rearrange("p (e t) -> p e t", e=E) for _ in range(3)]
        tot, tiles, upto, offs = [R.take(E) for _ in range(4)]
        cmp = R.take(64 * E)
        dest = [R.take(NT).bitcast(U32) for _ in range(2)]
        texp = R.take(NG)
        texpu = R.take(NG).bitcast(U32)
        ROWS = [R.take(NT * RW).rearrange("p (t n) -> p t n", t=NT) for _ in range(2)]
        W1S = R.take(W1W)
        W1 = R.take(UT * W1W).rearrange("p (s n) -> p s n", s=UT)
        moe_units = R.at
        HM1 = R.take(2 * KB1 * CH).rearrange("p (s k n) -> p s k n", s=2, k=KB1)
        R = Region(moe_units)
        HMT = R.take(2 * KB1 * GT).rearrange("p (s k n) -> p s k n", s=2, k=KB1)
        XR = R.take(UT * 2 * RW).rearrange("p (s r n) -> p s r n", s=UT, r=2)
        rid = R.take(UT * 2).rearrange("p (s r) -> p s r", s=UT).bitcast(U32)
        XT = R.take(2 * GT).rearrange("p (s n) -> p s n", s=2)
        YS = R.take(UT * GT).rearrange("p (s r n) -> p s r n", s=UT, r=2)
        YG = [r.rearrange("p t n -> p (t n)")[:, 0:NT * D].rearrange("p (t n) -> p t n", t=NT) for r in ROWS]

        R = Region(dense_base)
        Wqkv = R.take(5 * D).rearrange("p (w n) -> p w n", w=5)
        ropes = R.take(4 * S).rearrange("p (w t) -> p w t", w=4)
        rel0 = R.take(1)
        relv = R.take(HD)
        RT_1 = R.take(2 * CH).rearrange("p (s n) -> p s n", s=2)
        RT_2 = R.take(2 * CH).rearrange("p (s n) -> p s n", s=2)
        QR = R.take(2 * CH).rearrange("p (s n) -> p s n", s=2)
        KR = R.take(2 * CH).rearrange("p (s n) -> p s n", s=2)
        HI = R.take(4 * CH, BF16).rearrange("p (s w n) -> p s w n", s=2, w=2)
        LO = R.take(4 * CH, BF16).rearrange("p (s w n) -> p s w n", s=2, w=2)
        VT = R.take(2 * TPC * H * VW).rearrange("p (s t n) -> p s t n", s=2, t=TPC)

        before_attention = max(R.at, scan_end, moe0_end)

        R = Region(0)
        BH = R.take(HS * QB, BF16).rearrange("p (h q) -> p h q", h=HS)
        BL = R.take(HS * QB, BF16).rearrange("p (h q) -> p h q", h=HS)
        PT1 = R.take(HS * P).rearrange("p (h q) -> p h q", h=HS)
        PT0 = R.take(HS * S).rearrange("p (h q) -> p h q", h=HS)
        early = R.at
        assert early >= before_attention
        QG = R.take(HS * S, BF16).rearrange("p (h q) -> p h q", h=HS)
        KG = R.take(HS * S, BF16).rearrange("p (h q) -> p h q", h=HS)
        relk = R.take(X0 * HD).rearrange("p (x d) -> p x d", d=HD)
        GTf = R.take(X0 + P)
        GTB = R.take(X0 + P, BF16)
        rel0r = R.take(HD)
        rel0c = R.take(1)
        MX0 = R.take(HS * 8).rearrange("p (h b) -> p h b", h=HS)
        MX1 = R.take(HS * 4).rearrange("p (h b) -> p h b", h=HS)
        NM = R.take(2 * 32, BF16).rearrange("p (c n) -> p c n", c=2)
        VS = R.take(TPC * H * VW).rearrange("p (t h v) -> p t h v", t=TPC, h=H)
        CTS = R.take(2 * CH).rearrange("p (s n) -> p s n", s=2)
        RS = R.take(HS * 64).rearrange("p (h i) -> p h i", h=HS)
        half_mask = R.take(1)
        attn_end = R.at

        R = Region(0)
        C1 = R.take(TOK)
        R1 = R.take(TOK)
        R = Region(early)
        DN = R.take(CH)
        DR = R.take(CH)
        DN7, DR7 = R.take(CH), R.take(CH)
        CX = R.take(2 * CH).rearrange("p (s n) -> p s n", s=2)
        selp = R.take(NP * P).rearrange("p (c n) -> p c n", c=NP)
        woT1 = R.take(D)

        gD = scratch("gates", [4, B, D])
        qD = scratch("q_parts", [H, 3 * HD, TOK], BF16)
        kD = scratch("k_parts", [H, 3 * HD, TOK], BF16)
        vD = scratch("v_rows", [TOK, H * VW])
        cD = scratch("context", [H * VW, TOK])
        rD = scratch("context_rel", [P, TOK])
        xsD = scratch("dispatched_rows", [NG * GT, RW])
        yD = scratch("expert_results", [2 * TOK + NG * GT // 8, D])

        s_const = sem("s_const")
        s_cw = sem("s_cw")
        s_x = [sem(f"s_xin{c}") for c in range(NC)]
        s_set = sem("s_set")
        s_cm = sem("s_cm")
        s_mod = sem("s_mod")
        s_gg = sem("s_gg")
        s_gst = sem("s_gst")
        s_gld = sem("s_gld")
        s_dv = sem("s_dv")
        s_mv = sem("s_mv")
        s_sd = sem("s_sd")
        s_xn = sem("s_xn")
        s_tr = sem("s_tr")
        s_hT = sem("s_hT")
        s_m1 = sem("s_m1")
        s_zm = sem("s_zm")
        s_ssm = sem("s_ssm")
        s_ez = sem("s_ez")
        s_sig = sem("s_sig")
        s_ae = sem("s_ae")
        s_hs = sem("s_hs")
        s_y = sem("s_y")
        s_yr = sem("s_yr")
        s_wm = [sem("s_wm0"), sem("s_wm1")]
        s_lg = sem("s_lg")
        s_el = sem("s_el")
        s_cnt = sem("s_cnt")
        s_oh = sem("s_oh")
        s_w = [[sem(f"s_w{m}{k}") for k in range(2)] for m in range(2)]
        s_up = [sem("s_up0"), sem("s_up1")]
        s_act = [sem("s_act0"), sem("s_act1")]
        s_hm = sem("s_hm")
        s_dn = [sem("s_dn0"), sem("s_dn1")]
        s_acc = [sem("s_acc0"), sem("s_acc1")]
        s_ws = [sem("s_ws0"), sem("s_ws1")]
        s_wp = sem("s_wp")
        s_pj = sem("s_pj")
        s_rot = sem("s_rot")
        s_qr = sem("s_qr")
        s_hi = sem("s_hi")
        s_lo = sem("s_lo")
        s_v = sem("s_v")
        s_qst = [sem("s_qst0"), sem("s_qst1")]
        s_r0 = sem("s_r0")
        s_gt = sem("s_gt")
        s_gt0 = sem("s_gt0")
        s_y0 = sem("s_y0")
        s_x0 = sem("s_x0")
        s_zero = sem("s_zero")
        s_din = sem("s_din")
        s_din7 = sem("s_din7")
        s_cr = sem("s_cr")
        s_tab = sem("s_tab")
        s_tb = sem("s_tb")
        s_in = sem("s_in")
        s_vin = sem("s_vin")
        s_gen = sem("s_gen")
        s_bh = sem("s_bh")
        s_bl = sem("s_bl")
        s_r1 = sem("s_r1")
        s_mx = sem("s_mx")
        s_mc = sem("s_mc")
        s_tm = sem("s_tm")
        s_nm = sem("s_nm")
        s_mr = sem("s_mr")
        s_r2 = sem("s_r2")
        s_ba = sem("s_ba")
        s_ex = sem("s_ex")
        s_pv = sem("s_pv")
        s_pe = sem("s_pe")
        s_rl = sem("s_rl")
        s_re = sem("s_re")
        s_cst = [sem("s_cst0"), sem("s_cst1")]
        s_rst = sem("s_rst")
        s_cin = [sem(f"s_cin{k}") for k in range(3)]
        s_wo = sem("s_wo")
        s_dr = sem("s_dr")
        s_db = sem("s_db")
        s_cx = sem("s_cx")
        s_out = sem("s_out")
        s_one = sem("s_one")
        s_rh = sem("s_rh")
        s_relu = sem("s_relu")
        s_pad = sem("s_pad")
        s_back = sem("s_back")
        s_rows = sem("s_rows")
        s_ids = sem("s_ids")
        s_tot = sem("s_tot")
        s_rank = sem("s_rank")
        s_dest = sem("s_dest")
        s_disp = sem("s_disp")
        s_sw = sem("s_sw")
        s_sup = sem("s_sup")
        s_sact = sem("s_sact")
        s_sdn = sem("s_sdn")
        s_sout = sem("s_sout")
        s_res = sem("s_res")
        s_ew = [sem(f"s_ew{k}") for k in range(UT)]
        s_xr = [sem(f"s_xr{k}") for k in range(UT)]
        s_xp = sem("s_xp")
        s_xt = sem("s_xt")
        s_ys = sem("s_ys")
        s_yo = [sem(f"s_yo{k}") for k in range(UT)]
        s_yl = [sem(f"s_yl{c}") for c in range(NC)]
        s_turn = sem("s_turn")
        s_y1 = sem("s_y1")
        s_y2 = sem("s_y2")
        s_fin = sem("s_fin")

        block = ctx.enter_context(nc.Block())

        def chunk(ap, c):
            return ap[:, c * CH:(c + 1) * CH]

        def wait(eng, s, v):
            if isinstance(v, int) and v <= 0:
                return
            eng.wait_ge(s, v)

        @block.sync
        def _(sp):
            n = [0]

            def const(dst, src):
                sp.dma_start(dst, src).then_inc(s_const, 16)
                n[0] += 1

            sp.dma_start(cT[:, :, :], A["cT"]).then_inc(s_cw, 16)
            sp.dma_start(wmod[:, :, :], A["wmod"]).then_inc(s_cw, 16)
            for c in range(NC):
                sp.dma_start(X[:, c * TPC:(c + 1) * TPC, :],
                             A["x"][c * CH:(c + 1) * CH, :].rearrange("(t p) d -> p t d", p=P)).then_inc(s_x[c], 16)
            const(ident[:, :], A["ident"])
            const(WBpad[:, 112:128], A["wbT"])
            const(WTpad[:, 112:128], A["wt16"])
            const(Wcr[:, :], A["wc8"])
            const(WoT[:, :], A["woT0"])
            const(small[:, 0:1], A["bb8"])
            const(small[:, 1:2], A["A8"])
            const(small[:, 2:3], A["bt"])
            const(small[:, 3:4], A["Dv"])
            const(bcol[:, :], A["bc"])
            const(borow[0:1, :], A["bo"])
            const(blockmask[:, :], A["blockmask"])
            assert n[0] == 12
            half = NG * GT // 8
            for x in range(8):
                sp.dma_start(xsD[x * half:(x + 1) * half, :], A["padding"]).then_inc(s_pad, 16)
            for dst, src in ((relk[:, :, :], A["relk"]), (GTf[0:25, :], A["gt"]), (rel0r[:, :], A["rel0r"]),
                             (rel0c[0:25, :], A["rel0c"]), (half_mask[0:25, :], A["lowrows"])):
                sp.dma_start(dst, src).then_inc(s_tab, 16)
            sp.wait_ge(s_zero, 1)
            sp.dma_start(QG[24:25, :, :], A["onesrow"]).then_inc(s_tab, 16)
            sp.dma_start(KG[25:26, :, :], A["onesrow"]).then_inc(s_tab, 16)
            sp.wait_ge(s_gg, 1)
            sp.dma_start(gD.rearrange("g b f -> b g f"), GG[:, :, :]).then_inc(s_gst, 16)
            sp.wait_ge(s_gst, 16)
            sp.dma_start(GATE[:, :, :, :].rearrange("p g b f -> p (g b f)"),
                         gD[0:2].rearrange("g b f -> (g b f)").partition_broadcast(P)).then_inc(s_gld, 16)

            sp.wait_ge(s_yr, NC)
            for dst, src in ((gateT[:, :], A["gateT"]), (sim[:, :, :], A["sim"]), (iota[:, :], A["iota"])):
                sp.dma_start(dst, src).then_inc(s_wm[0], 16)

            def w0_load(e, k):
                sp.dma_start(W0[:, k, :], A["w0"][e]).then_inc(s_w[0][k], 16)

            w0_load(0, 0)
            w0_load(1, 1)
            with sp.Fori(0, E // 2 - 1) as i:
                for k in range(2):
                    sp.wait_ge(s_dn[0], (2 * i + k + 1) * NC)
                    w0_load(2 * i + k + 2, k)

            sp.wait_ge(s_r0, NC)
            sp.dma_start(GATE[:, :, :, :].rearrange("p g b f -> p (g b f)"),
                         gD[2:4].rearrange("g b f -> (g b f)").partition_broadcast(P)).then_inc(s_gld, 16)
            for dst, src in ((Wqkv[:, :, :], A["wqkv"]), (ropes[:, :, :], A["ropes"]), (rel0[:, :], A["rel0"]),
                             (relv[:, :], A["rel0r"])):
                sp.dma_start(dst, src).then_inc(s_wp, 16)
            def load_pair(i, first):
                at = i * CH
                if not first:
                    sp.wait_ge(s_r2, i * 24)
                for dst, src in ((QG, qD), (KG, kD)):
                    sp.dma_start(dst[0:3 * HD, :, :].rearrange("p (h s) q -> p h (s q)", h=H),
                                 src[:, :, bass.ds(at, CH)].rearrange("h r t -> r h t")).then_inc(s_in, 16)
                sp.dma_start(QG[25:26, :, :], A["zerorow"]).then_inc(s_in, 16)

            for c in range(NC):
                sp.wait_ge(s_hi, 2 * (c + 1))
                sp.wait_ge(s_lo, 2 * (c + 1))
                sp.wait_ge(s_v, c + 1)
                k = c % 2
                for w, dst, parts in ((0, qD, (HI, HI, LO)), (1, kD, (HI, LO, HI))):
                    for r, src in enumerate(parts):
                        sp.dma_start(dst[:, HD * r:HD * (r + 1), c * CH:(c + 1) * CH], src[:, k, w, :]
                                     ).then_inc(s_qst[k], 16)
                sp.dma_start(vD[c * CH:(c + 1) * CH, :].rearrange("(t p) n -> p t n", p=P),
                             VT[:, k, :, :]).then_inc(s_qst[k], 16)
                if c == 1:
                    sp.wait_ge(s_qst[0], 16 * 7)
                    load_pair(0, True)
            for k in range(2):
                sp.wait_ge(s_qst[k], 16 * 7 * NC // 2)

            def load_values(i, first):
                if not first:
                    sp.wait_ge(s_pv, i * 4)
                sp.dma_start(VS[:, :, :, :].rearrange("p t h v -> p t (h v)"),
                             vD[bass.ds(i * CH, CH), :].rearrange("(t p) n -> p t n", p=P)).then_inc(s_vin, 16)

            def move_maxima(i):
                sp.wait_ge(s_nm, i + 1)
                for g in range(2):
                    sp.dma_start(QG[25:26, g * H:(g + 1) * H, :].rearrange("o h q -> o (h q)"),
                                 NM[:, g, :]).then_inc(s_mr, 16)

            def store_values(i):
                for w in range(4):
                    s, hb = w % 2, w // 2
                    sp.wait_ge(s_pe, i * 4 + w + 1)
                    at = i * CH + s * S
                    for j in range(4):
                        src = CTS[32 * j:32 * j + VW, w % 2, :].rearrange("v (g q) -> v g q", g=2)
                        sp.dma_start(
                            cD.rearrange("(g j v) t -> j v g t", g=4, j=4)[j, :, 2 * hb:2 * hb + 2, bass.ds(at, S)],
                            src).then_inc(s_cst[w % 2], 16)

            def store_relative(i):
                sp.wait_ge(s_re, i * 4 + 4)
                for s in range(2):
                    for j in range(4):
                        sp.dma_start(
                            rD.rearrange("(h d) t -> d h t", h=H)[:, :, bass.ds(i * CH + s * S + 64 * j, 64)],
                            RS[32 * j:32 * j + HD, :, :].rearrange("d (h s) i -> d h s i", s=2)[:, :, s, :]
                        ).then_inc(s_rst, 16)

            load_values(0, True)
            move_maxima(0)
            with sp.Fori(1, NP) as i:
                load_pair(i, False)
                store_values(i - 1)
                load_values(i, False)
                move_maxima(i)
                store_relative(i - 1)

            sp.wait_ge(s_ba, 24 * NP)
            for s, k in ((s_cst[0], 16 * 8), (s_cst[1], 16 * 8), (s_rst, 16 * 8)):
                sp.wait_ge(s, k * (NP - 1))
            part = (NP - 1) * CH
            values = cD.rearrange("(h v) t -> h v t", v=VW)
            sp.dma_start(DN[0:H * (NP - 1), :], values[:, HD, 0:part].rearrange("h (c t) -> c h t", c=NP - 1)
                         ).then_inc(s_din, 16)
            sp.dma_start(selp[:, :, :], A["selp"]).then_inc(s_wo, 16)
            sp.dma_start(woT1[:, :], A["woT1"]).then_inc(s_wo, 16)
            for k, (lo, hi) in enumerate(((0, 2 * CH), (2 * CH, part))):
                sp.dma_start(C1[:, lo:hi], values[:, 0:HD, lo:hi]).then_inc(s_cin[k], 16)
                sp.dma_start(R1[:, lo:hi], rD[:, lo:hi]).then_inc(s_cin[k], 16)
            store_values(NP - 1)
            for k in range(2):
                sp.wait_ge(s_cst[k], 16 * 8 * NP)
            sp.dma_start(DN7[0:H, :], values[:, HD, part:TOK]).then_inc(s_din7, 16)
            sp.dma_start(chunk(C1, NP - 1), values[:, 0:HD, part:TOK]).then_inc(s_cin[2], 16)
            store_relative(NP - 1)
            sp.wait_ge(s_rst, 16 * 8 * NP)
            sp.dma_start(chunk(R1, NP - 1), chunk(rD, NP - 1)).then_inc(s_cin[2], 16)

            for dst, src in ((Wr1[:, :], A["wr1"]), (Wr2[0:33, :], A["wr2"]), (br1[0:32, :], A["br1"]),
                             (iota[:, :], A["iota"])):
                sp.dma_start(dst, src).then_inc(s_wm[1], 16)

            for dst, src in ((rowid[:, :, :], A["rowid"]), (steps[:, :, :], A["steps"]), (below[:, :], A["below"])):
                sp.dma_start(dst, src).then_inc(s_wm[1], 16)
            sp.wait_ge(s_yr, 2 * NC)
            sp.dma_start(W1S[:, :], A["w1s"]).then_inc(s_sw, 16)

            def load_tile(j, k):
                sp.dma_start(XR[:, k, :, :], xsD[bass.ds(j * GT, GT), :].rearrange("(r p) n -> p r n", p=P)
                             ).then_inc(s_xr[k], 16)
                e = sp.value_load(texpu[0:1, bass.ds(j, 1)], min_val=0, max_val=E - 1)
                sp.dma_start(W1[:, k, :], A["w1"][bass.ds(e, 1)].rearrange("o p n -> p (o n)")).then_inc(s_ew[k], 16)

            sp.wait_ge(s_dest, 3)
            sp.wait_ge(s_sdn, NC)
            sp.wait_ge(s_disp, 16 * 2 * NT)
            for k in range(UT):
                load_tile(k, k)
            def next_tiles(i, n):
                for k in range(n):
                    sp.wait_ge(s_ys, i * UT - UT + k + 1)
                    load_tile(i * UT + k, k)

            with sp.Fori(1, FULL) as i:
                next_tiles(i, UT)
            next_tiles(FULL, LAST)

            for k in range(UT):
                sp.wait_ge(s_yo[k], 32 * (FULL + (k < LAST)))
            for c in range(NC):
                for k in range(2):
                    at = k * TOK + c * CH
                    sp.dma_start(YG[k][:, c * TPC:(c + 1) * TPC, :],
                                 yD[at:at + CH, :].rearrange("(t p) d -> p t d", p=P)).then_inc(s_yl[c], 16)
            for c in range(NC):
                sp.wait_ge(s_fin, c + 1)
                sp.dma_start(out[c * CH:(c + 1) * CH, :].rearrange("(t p) d -> p t d", p=P),
                             X[:, c * TPC:(c + 1) * TPC, :]).then_inc(s_out, 16)
            sp.wait_ge(s_out, 16 * NC)

        @block.gpsimd
        def _(pool):
            nc.gpsimd.memset(WBpad[:, 0:112], 0.0)
            nc.gpsimd.memset(WBpad[:, 128:240], 0.0)
            nc.gpsimd.memset(WTpad[:, 0:112], 0.0)
            nc.gpsimd.memset(WTpad[:, 128:240], 0.0)
            nc.gpsimd.memset(ones[:, :], 1.0).then_inc(s_set, 1)
            nc.gpsimd.memset(QG[:, :, :].bitcast(F32), 0.0)
            nc.gpsimd.memset(KG[:, :, :].bitcast(F32), 0.0).then_inc(s_zero, 1)
            nc.gpsimd.memset(ACC[:, :, :], 0.0).then_inc(s_zero, 1)

            def residual(c, u):
                pool.wait_ge(s_gt, u + 1)
                xs = X[:, c * TPC:(c + 1) * TPC, :].rearrange("p t f -> p (t f)")
                nc.gpsimd.tensor_tensor(xs, xs, TMP[:, c % 2, :], ALU.add).then_inc(s_yr, 1)

            for c in range(NC):
                residual(c, c)

            for c in range(NC):
                pool.wait_ge(s_acc[0], (E - 1) * NC + c + 1)
                t4 = TMP[:, c % 2, :].rearrange("p (b t f) -> p b t f", b=2, t=2)
                a4 = ACC[:, c * TPC:(c + 1) * TPC, :].rearrange("p (b t) f -> p b t f", b=2)
                for b in range(2):
                    gate = GATE[:, 1, 2 * c + b, :].unsqueeze(1).to_broadcast([P, 2, D])
                    ins = nc.gpsimd.tensor_tensor(t4[:, b], a4[:, b], gate, ALU.mult)
                ins.then_inc(s_gt0, 1)
                pool.wait_ge(s_gt0, c + 1)
                xs = X[:, c * TPC:(c + 1) * TPC, :].rearrange("p t f -> p (t f)")
                nc.gpsimd.tensor_tensor(xs, xs, TMP[:, c % 2, :], ALU.add).then_inc(s_r0, 1)

            for c in range(NC):
                k = c % 2
                pool.wait_ge(s_rot, 5 * c + 2)
                wait(pool, s_lo, 2 * (c - 1))
                nc.gpsimd.tensor_tensor(QR[:, k, :], RT_1[:, 0, :], RT_2[:, 0, :], ALU.add).then_inc(s_qr, 1)
                if c >= 2:
                    pool.wait_ge(s_qst[k], 16 * 7 * (c // 2))
                for w, src in ((0, QR), (1, KR)):
                    pool.wait_ge(s_hi, 2 * c + w + 1)
                    nc.gpsimd.tensor_tensor(LO[:, k, w, :], src[:, k, :], HI[:, k, w, :], ALU.subtract
                                            ).then_inc(s_lo, 1)

            def join(c):
                pool.wait_ge(s_cin[0 if c < 2 else 1 if c < NC - 1 else 2], 32)
                nc.gpsimd.tensor_tensor(chunk(C1, c), chunk(C1, c), chunk(R1, c), ALU.add).then_inc(s_cr, 1)

            for c in range(NC - 1):
                join(c)
                if c >= 3:
                    residual(c - 3, NC + c - 3)
            for c in (NC - 4, NC - 3):
                residual(c, NC + c)
            join(NC - 1)
            for c in (NC - 2, NC - 1):
                residual(c, NC + c)
            pool.wait_ge(s_yr, 2 * NC)
            nc.gpsimd.memset(RT1[32:33, :, :], 1.0).then_inc(s_one, 1)

            pool.wait_ge(s_pad, 16 * 8)
            pool.wait_ge(s_rows, 2 * NC)
            pool.wait_ge(s_ids, 1)
            for k in range(2):
                pool.wait_ge(s_dest, k + 1)
                for t in range(NT):
                    nc.gpsimd.indirect_dma_start(
                        xsD[:, :], bass.IndirectOffsetOnAxis(ap=dest[k][:, t:t + 1], axis=0),
                        ROWS[k][:, t, :], None).then_inc(s_disp, 16)

            def results_out(j, k):
                pool.wait_ge(s_ys, j + 1)
                pool.sem_inc(s_turn, 1)
                for r in range(2):
                    nc.gpsimd.indirect_dma_start(
                        yD[:, :], bass.IndirectOffsetOnAxis(ap=rid[:, k, r:r + 1], axis=0),
                        YS[:, k, r, :], None).then_inc(s_yo[k], 16)

            with pool.Fori(0, FULL) as i:
                for k in range(UT):
                    results_out(i * UT + k, k)
            for k in range(LAST):
                results_out(FULL * UT + k, k)
            pool.wait_ge(s_lg, 4)
            for c in range(NC):
                pool.wait_ge(s_yl[c], 32)
                cs = slice(c * TPC, (c + 1) * TPC)
                nc.gpsimd.tensor_tensor(YG[1][:, cs, :], YG[1][:, cs, :],
                                        w2[:, cs].unsqueeze(2).to_broadcast([P, TPC, D]), ALU.mult).then_inc(s_y2, 1)

        @block.scalar
        def _(act):
            act.wait_ge(s_cw, 32)
            nc.scalar.activation(scT[:, :, :], cT[:, :, :], ACT.Silu).then_inc(s_cm, 1)

            def layer_norm(n, then=None):
                l, first = n // 2, 3 * (n % 2)
                act.wait_ge(s_mv, (n + 1) * NC)
                nc.scalar.activation(SD[:, :], MV[:, :, 1], ACT.Sqrt, bias=epsc[:, :]).then_inc(s_sd, 1)
                for c in range(NC):
                    act.wait_ge(s_tr, n * NC + c + 1)
                    for s in range(2):
                        b = 2 * c + s
                        ins = nc.scalar.activation(hT[:, b * S:(b + 1) * S], bank[c % 2][:, s * S:(s + 1) * S],
                                                   ACT.Identity, scale=MOD[:, l, first + 1, b:b + 1],
                                                   bias=MOD[:, l, first, b:b + 1])
                    ins.then_inc(s_hT, 1)
                    if then:
                        then(c)

            layer_norm(0)
            for h in range(2):
                act.wait_ge(s_ssm, h + 1)
                nc.scalar.activation(EZ[:, h, :], bank[2 + h][:, S:2 * S], ACT.Exp, scale=-1.0,
                                     bias=small[:, 4:5]).then_inc(s_ez, 1)
            for h in range(2):
                act.wait_ge(s_sig, h + 1)
                nc.scalar.activation(AE[:, h, :], SIG[:, h, :], ACT.Exp, scale=small[:, 5:6],
                                     bias=small[:, 6:7]).then_inc(s_ae, 1)

            layer_norm(1)
            act.wait_ge(s_lg, 1)
            nc.scalar.activation(PR[:, :, :], LG[:, :, :], ACT.Exp).then_inc(s_el, 1)

            def moe0(i, first):
                for j in range(2 * NC):
                    u = i * 2 * NC + j
                    act.wait_ge(s_up[0], u + 1)
                    wait(act, s_hm, u - 1)
                    nc.scalar.activation(SG[:, j % 2, :], bank[j % 2][:, :], ACT.Silu).then_inc(s_act[0], 1)

            moe0(0, True)
            with act.Fori(1, E // 2) as i:
                moe0(i, False)

            layer_norm(2)
            for c in range(NC):
                k = c % 2
                if c >= 2:
                    act.wait_ge(s_qst[k], 16 * 7 * (c // 2))
                for w, src in ((0, QR), (1, KR)):
                    act.wait_ge(s_rot, 5 * c + 5) if w else act.wait_ge(s_qr, c + 1)
                    nc.scalar.copy(HI[:, k, w, :], src[:, k, :]).then_inc(s_hi, 1)

            def bias_high(i, banks=range(18)):
                if not isinstance(i, int) and banks[0] == 0:
                    act.wait_ge(s_r2, i * 24)
                for g in banks:
                    act.wait_ge(s_gen, i * 18 + g + 1)
                    at = g * 16
                    nc.scalar.copy(BH[:, :, at:at + 16].rearrange("p h q -> p q h"),
                                   bank[g % RING][:, :].rearrange("p (q h) -> p q h", h=HS)).then_inc(s_bh, 1)

            def exponentials(i):
                for r in range(24):
                    act.wait_ge(s_ba, i * 24 + r + 1)
                    dst = PT0[:, 2 * r:2 * r + 2, :] if r < 16 else PT1[:, 4 * (r - 16):4 * (r - 16) + 4, :]
                    q = S if r < 16 else P
                    nc.scalar.activation(dst, bank[r % RING2][:, :].rearrange("p (h q) -> p h q", q=q),
                                         ACT.Exp).then_inc(s_ex, 1)

            def values_out(i, units=range(4)):
                for w in units:
                    act.wait_ge(s_pv, i * 4 + w + 1)
                    v = 16 * 4 * (2 * i + w // 2)
                    wait(act, s_cst[w % 2], v)
                    nc.scalar.copy(CTS[:, w % 2, :], bank[4 - w % 2][:, :]).then_inc(s_pe, 1)

            bias_high(0)
            exponentials(0)
            with act.Fori(1, NP) as i:
                values_out(i - 1, (0, 1))
                bias_high(i, range(0, 8))
                values_out(i - 1, (2,))
                bias_high(i, range(8, 14))
                values_out(i - 1, (3,))
                bias_high(i, range(14, 18))
                exponentials(i)
            values_out(NP - 1)

            def relu(c):
                if c >= 0:
                    act.wait_ge(s_rh, c + 1)
                    wait(act, s_m1, c)
                    nc.scalar.activation(RT1[0:32, c % 2, :], bank[3 + c % 2][0:32, :], ACT.Relu, bias=br1[0:32, :]
                                         ).then_inc(s_relu, 1)

            act.wait_ge(s_wm[1], 16 * 7)
            layer_norm(3, lambda c: relu(c - 1))
            relu(NC - 1)
            act.wait_ge(s_lg, 2)
            nc.scalar.activation(PR[:, :, :], LG[:, :, :], ACT.Exp).then_inc(s_el, 1)
            for c in range(NC):
                act.wait_ge(s_back, c + 1)
                for k in range(2):
                    nc.scalar.copy(ROWS[k][:, c * TPC:(c + 1) * TPC, 0:D],
                                   bank[6 + c % 2][:, :].rearrange("p (t d) -> p t d", t=TPC)).then_inc(s_rows, 1)
            for c in range(NC):
                wait(act, s_sdn, c - 1)
                for b in range(KB1):
                    act.wait_ge(s_sup, c * KB1 + b + 1)
                    nc.scalar.activation(HM1[:, c % 2, b, :], bank[b][:, :], ACT.Silu,
                                         bias=W1S[:, 2 * I1 + b:2 * I1 + b + 1]).then_inc(s_sact, 1)
            act.wait_ge(s_lg, 3)
            nc.scalar.activation(w2[:, :], m2[:, :], ACT.Exp).then_inc(s_el, 1)

            def hidden(j, k):
                wait(act, s_dn[1], j - 1)
                for b in range(KB1):
                    act.wait_ge(s_up[1], 2 * j + b // 2 + 1)
                    nc.scalar.activation(HMT[:, k % 2, b, :], bank[2 * (k % 2) + b // 2][:, b % 2 * GT:(b % 2 + 1) * GT],
                                         ACT.Silu, bias=W1[:, k, 2 * I1 + b:2 * I1 + b + 1]).then_inc(s_act[1], 1)

            for k in range(UT):
                hidden(k, k)
            with act.Fori(1, FULL) as i:
                for k in range(UT):
                    hidden(i * UT + k, k)
            for k in range(LAST):
                hidden(FULL * UT + k, k)
            act.wait_ge(s_lg, 4)
            for c in range(NC):
                act.wait_ge(s_yl[c], 32)
                for t in range(TPC):
                    T = c * TPC + t
                    ins = nc.scalar.activation(YG[0][:, T, :], YG[0][:, T, :], ACT.Copy, scale=w1[:, T:T + 1])
                ins.then_inc(s_y1, 1)

        @block.vector
        def _(dve):
            chain = [0]

            def link(ins):
                chain[0] += 1
                ins.then_inc(s_dv, 1)
                dve.wait_ge(s_dv, chain[0])

            v = nc.vector

            def statistics(c):
                for t in range(TPC):
                    ins = v.bn_stats(ST[:, c * TPC + t, :], X[:, c * TPC + t, :])
                link(ins)
                for t in range(TPC):
                    ins = v.bn_aggr(MV[:, c * TPC + t, :], ST[:, c * TPC + t, :])
                ins.then_inc(s_mv, 1)

            v.memset(epsc[:, :], EPS)
            for i in range(8):
                link(v.memset(bank[i][:, :], 0.0))
            for c in range(NC):
                dve.wait_ge(s_x[c], 16)
                statistics(c)
            dve.wait_ge(s_const, 16 * 12)
            v.tensor_copy(identb[:, :], ident[:, :])
            v.tensor_scalar(small[:, 4:5], small[:, 2:3], -1.0, None, ALU.mult)
            v.tensor_scalar(small[:, 5:6], small[:, 1:2], 0.99, None, ALU.mult)
            v.tensor_scalar(small[:, 6:7], small[:, 1:2], 0.01, None, ALU.mult)
            link(v.tensor_scalar(M2[:, :], WoT[:, :], small[:, 3:4], None, ALU.mult))

            dve.wait_ge(s_mod, 1)
            link(v.tensor_copy(MOD[:, :, :, :].rearrange("p l m b -> p (l m b)"), bank[0][:, 0:2 * 6 * B]))
            for m in (1, 4):
                link(v.tensor_scalar(MOD[:, :, m, :], MOD[:, :, m, :], 1.0, None, ALU.add))
            gsrc = bank[1][0:B, :].rearrange("p (g f) -> p g f", g=4)
            v.tensor_scalar(GT1[:, :, :], gsrc, 0.0, 2.0, ALU.is_ge, ALU.mult)
            link(v.tensor_scalar(GG[:, :, :], gsrc, -1.0, None, ALU.mult))
            link(v.scalar_tensor_tensor(out=GG[:, :, :].rearrange("p g f -> p (g f)"),
                                        in0=GG[:, :, :].rearrange("p g f -> p (g f)"), scalar=0.25,
                                        in1=bank[1][0:B, :], op0=ALU.max, op1=ALU.max))
            ins = v.scalar_tensor_tensor(out=GG[:, :, :].rearrange("p g f -> p (g f)"),
                                         in0=GT1[:, :, :].rearrange("p g f -> p (g f)"), scalar=-1.0,
                                         in1=GG[:, :, :].rearrange("p g f -> p (g f)"), op0=ALU.add, op1=ALU.mult)
            ins.then_inc(s_gg, 1)
            dve.wait_ge(s_m1, 1)
            for b in range(8):
                v.tensor_scalar(ZM[:, b, :], bank[4][:, 0:D], blockmask[:, b:b + 1], None, ALU.mult)
            v.tensor_tensor(crow[0:1, :], bank[5][0:1, 0:D], borow[0:1, :], ALU.add).then_inc(s_zm, 1)

            def normalise(n):
                dve.wait_ge(s_sd, n + 1)
                link(v.reciprocal(RSTD[:, :], SD[:, :]))
                for c in range(NC):
                    wait(dve, s_tr, n * NC + c - 1)
                    for t in range(TPC):
                        T = c * TPC + t
                        ins = v.tensor_scalar(XN[:, c % 2, t, :], X[:, T, :], MV[:, T, 0:1], RSTD[:, T:T + 1],
                                              ALU.subtract, ALU.mult)
                    ins.then_inc(s_xn, 1)

            def gated(c, src, g, u0):
                wait(dve, s_yr, u0 + c - 1 if c >= 2 else 0)
                t4 = TMP[:, c % 2, :].rearrange("p (b t f) -> p b t f", b=2, t=2)
                for b in range(2):
                    gate = GATE[:, g, 2 * c + b, :].unsqueeze(1).to_broadcast([P, 2, D])
                    ins = v.tensor_tensor(t4[:, b], src[:, b], gate, ALU.mult)
                ins.then_inc(s_gt, 1)

            def add_gated(c, src, g, done):
                t4 = TMP[:, c % 2, :].rearrange("p (b t f) -> p b t f", b=2, t=2)
                for b in range(2):
                    gate = GATE[:, g, 2 * c + b, :].unsqueeze(1).to_broadcast([P, 2, D])
                    ins = v.tensor_tensor(t4[:, b], src[:, b], gate, ALU.mult)
                link(ins)
                xs = X[:, c * TPC:(c + 1) * TPC, :].rearrange("p t f -> p (t f)")
                ins = v.tensor_tensor(xs, xs, TMP[:, c % 2, :], ALU.add)
                ins.then_inc(done, 1)

            normalise(0)
            dve.wait_ge(s_gld, 16)
            dve.wait_ge(s_y0, 1)
            for c in range(NC):
                for b in range(2):
                    ins = v.tensor_tensor(TMP[:, c % 2, b * D:(b + 1) * D], GATE[:, 0, 2 * c + b, :],
                                          bank[5][:, 0:D], ALU.mult)
                link(ins)
                x4 = X[:, c * TPC:(c + 1) * TPC, :].rearrange("p (b t) f -> p b t f", b=2)
                v.tensor_tensor(x4, x4, TMP[:, c % 2, 0:2 * D].rearrange("p (b f) -> p b f", b=2).unsqueeze(2)
                                .to_broadcast([P, 2, 2, D]), ALU.add).then_inc(s_x0, 1)
            for h in range(2):
                dve.wait_ge(s_ez, h + 1)
                link(v.tensor_scalar(SIG[:, h, :], EZ[:, h, :], 1.0, None, ALU.add))
                v.reciprocal(SIG[:, h, :], SIG[:, h, :]).then_inc(s_sig, 1)
            for h in range(2):
                link(v.tensor_scalar(BU[:, h, :], bank[2 + h][:, 0:S], small[:, 0:1], None, ALU.add))
                dve.wait_ge(s_ae, h + 1)
                v.tensor_tensor_scan(HSC[:, h, :], AE[:, h, :], BU[:, h, :], 0.0, ALU.mult, ALU.add).then_inc(s_hs, 1)
            dve.wait_ge(s_x0, NC)
            for c in range(NC):
                dve.wait_ge(s_y, c + 1)
                gated(c, bank[6 + c % 2][:, :].rearrange("p (b t f) -> p b t f", b=2, t=2), 0, 0)
                if c:
                    dve.wait_ge(s_yr, c)
                    statistics(c - 1)
            dve.wait_ge(s_yr, NC)
            statistics(NC - 1)

            def bc_e(a):
                return a.unsqueeze(2).to_broadcast([P, NT, E])

            iota3 = iota[:, :].unsqueeze(1).to_broadcast([P, NT, E])

            def pick(values, best, onehot):
                link(v.tensor_reduce(best, values, AX, ALU.max))
                link(v.tensor_tensor(EQ[:, :, :], values, bc_e(best), ALU.is_lt))
                link(v.tensor_scalar(EQ[:, :, :], EQ[:, :, :], float(E), None, ALU.mult))
                link(v.tensor_tensor(EQ[:, :, :], EQ[:, :, :], iota3, ALU.add))
                link(v.tensor_reduce(idx[:, :], EQ[:, :, :], AX, ALU.min))
                return v.tensor_tensor(onehot, iota3, bc_e(idx[:, :]), ALU.is_equal)

            def softmax_shift(m):
                lg = bank[2 if m else 6][:, 0:NE].rearrange("p (t e) -> p t e", t=NT)
                link(v.tensor_reduce(m1[:, :], lg, AX, ALU.max))
                v.tensor_tensor(LG[:, :, :], lg, bc_e(m1[:, :]), ALU.subtract).then_inc(s_lg, 1)

            def softmax_end():
                link(v.tensor_reduce(ssum[:, :], PR[:, :, :], AX, ALU.add))
                link(v.reciprocal(ssum[:, :], ssum[:, :]))
                link(v.tensor_tensor(PR[:, :, :], PR[:, :, :], bc_e(ssum[:, :]), ALU.mult))

            def second(m):
                link(v.tensor_tensor(CD[:, :, :], PR[:, :, :], OH1[:, :, :], ALU.subtract))
                link(v.scalar_tensor_tensor(out=CD[:, :, :], in0=OH1[:, :, :], scalar=-4.0, in1=CD[:, :, :],
                                            op0=ALU.mult, op1=ALU.add))
                link(pick(CD[:, :, :], m, OH2[:, :, :]))

            normalise(1)
            dve.wait_ge(s_wm[0], 16 * 3)
            dve.wait_ge(s_cnt, NC)
            softmax_shift(0)
            dve.wait_ge(s_el, 1)
            softmax_end()
            link(pick(PR[:, :, :], m1[:, :], OH1[:, :, :]))
            v.tensor_reduce(cnt[:, :], OH1[:, :, :].rearrange("p t e -> p e t"), AX, ALU.add).then_inc(s_oh, 1)
            second(m2[:, :])
            link(v.tensor_tensor(ssum[:, :], m1[:, :], m2[:, :], ALU.add))
            link(v.tensor_scalar(ssum[:, :], ssum[:, :], 1e-12, None, ALU.max))
            link(v.reciprocal(ssum[:, :], ssum[:, :]))
            v.tensor_tensor(w1[:, :], m1[:, :], ssum[:, :], ALU.mult)
            link(v.tensor_tensor(w2[:, :], m2[:, :], ssum[:, :], ALU.mult))
            v.tensor_tensor(OH1[:, :, :], OH1[:, :, :], bc_e(w1[:, :]), ALU.mult)
            link(v.tensor_tensor(OH2[:, :, :], OH2[:, :, :], bc_e(w2[:, :]), ALU.mult))
            link(v.tensor_tensor(WT[:, :, :], OH1[:, :, :], OH2[:, :, :], ALU.add))
            dve.wait_ge(s_cnt, NC + 1)
            link(v.tensor_scalar(pm[:, :], bank[7][:, 0:E], 0.5, None, ALU.is_ge))
            pmj = pm[:, :].unsqueeze(1).to_broadcast([P, E, E])
            link(v.tensor_scalar(smq[:, :, :], pmj, 1.0, -LOWEST, ALU.subtract, ALU.mult))
            link(v.tensor_tensor(sm[:, :, :], sim[:, :, :], pmj, ALU.mult))
            link(v.tensor_tensor(sm[:, :, :], sm[:, :, :], smq[:, :, :], ALU.add))
            link(v.tensor_reduce(bs[:, :], sm[:, :, :], AX, ALU.max))
            link(v.tensor_tensor(smc[:, :, :], sm[:, :, :], bs[:, :].unsqueeze(2).to_broadcast([P, E, E]), ALU.is_lt))
            link(v.tensor_scalar(smc[:, :, :], smc[:, :, :], float(E), None, ALU.mult))
            iotaj = iota[:, :].unsqueeze(1).to_broadcast([P, E, E])
            link(v.tensor_tensor(smc[:, :, :], smc[:, :, :], iotaj, ALU.add))
            link(v.tensor_reduce(bj[:, :], smc[:, :, :], AX, ALU.min))
            link(v.tensor_scalar(cnd[:, :], bs[:, :], THRESHOLD, None, ALU.is_ge))
            link(v.scalar_tensor_tensor(out=cnd[:, :], in0=pm[:, :], scalar=0.5, in1=cnd[:, :],
                                        op0=ALU.is_lt, op1=ALU.mult))
            link(v.tensor_tensor(bj[:, :], bj[:, :], iota[:, :], ALU.subtract))
            link(v.tensor_tensor(bj[:, :], bj[:, :], cnd[:, :], ALU.mult))
            link(v.tensor_tensor(emap[:, :], bj[:, :], iota[:, :], ALU.add))
            link(v.tensor_tensor(MM[:, :, :], emap[:, :].unsqueeze(2).to_broadcast([P, E, E]), iotaj, ALU.is_equal))
            w4 = cmp4[:, :].rearrange("p (e t i) -> p e t i", e=E, t=NT)
            link(v.tensor_tensor(w4, WT[:, :, :].unsqueeze(1).to_broadcast([P, E, NT, E]),
                                 MM[:, :, :].rearrange("p i e -> p e i").unsqueeze(2).to_broadcast([P, E, NT, E]),
                                 ALU.mult))
            link(v.tensor_reduce(WD[:, :, :], w4, AX, ALU.add))

            def accumulate(m, u, j, src):
                c = j % NC
                dve.wait_ge(s_dn[m], u + 1)
                wait(dve, s_acc[m], u - NC + 1 + (NC if m else 0))
                for t in range(TPC):
                    T = c * TPC + t
                    ins = v.scalar_tensor_tensor(out=ACC[:, T, :], in0=src[:, t * D:(t + 1) * D],
                                                 scalar=wstep[:, (j // NC) % 2, T:T + 1], in1=ACC[:, T, :],
                                                 op0=ALU.mult, op1=ALU.add)
                ins.then_inc(s_acc[m], 1)

            def step_weights(m, i, table, e0, n):
                wait(dve, s_acc[m], e0)
                ins = v.tensor_copy(wstep[:, 0:n, :], table)
                ins.then_inc(s_ws[m], 1)

            def moe0(i, last=False):
                step_weights(0, i, WD[:, bass.ds(2 * i, 2), :], i * 2 * NC, 2)
                dve.wait_ge(s_ws[0], i + 1)
                for j in range(2 * NC):
                    u = i * 2 * NC + j
                    dve.wait_ge(s_act[0], u + 1)
                    wait(dve, s_dn[0], u - 1)
                    v.tensor_tensor(HM0[:, j % 2, :], SG[:, j % 2, :], bank[2 + j % 2][:, :], ALU.mult).then_inc(s_hm, 1)
                    if j:
                        accumulate(0, u - 1, j - 1, bank[4 + (j - 1) % 2])
                        if last and j > NC + 1:
                            statistics0(j - 2 - NC)
                accumulate(0, u, 2 * NC - 1, bank[4 + 1])
                if last:
                    statistics0(NC - 2)
                    statistics0(NC - 1)

            def statistics0(c):
                dve.wait_ge(s_r0, c + 1)
                statistics(c)

            dve.wait_ge(s_zero, 2)
            moe0(0)

            link(v.memset(GTB[:, :], 0.0))
            dve.wait_ge(s_tab, 16 * 7)
            v.tensor_tensor(relk[:, :, :], relk[:, :, :], rel0r[:, :].unsqueeze(1).to_broadcast([P, X0, HD]), ALU.subtract)
            link(v.tensor_scalar(GTf[0:25, :], GTf[0:25, :], rel0c[0:25, :], None, ALU.subtract))
            link(v.tensor_copy(GTB[0:25, :], GTf[0:25, :]))
            link(v.tensor_tensor(GTf[0:25, :], GTf[0:25, :], GTB[0:25, :], ALU.subtract))
            link(v.tensor_scalar(GTf[0:25, :], GTf[0:25, :], half_mask[0:25, :], None, ALU.mult))
            link(v.tensor_scalar(rel0c[0:25, :], half_mask[0:25, :], -1.0, 1.0, ALU.mult, ALU.add))
            v.scalar_tensor_tensor(out=GTB[0:25, :], in0=GTB[0:25, :], scalar=rel0c[0:25, :], in1=GTf[0:25, :],
                                   op0=ALU.mult, op1=ALU.add).then_inc(s_tb, 1)

            with dve.Fori(1, E // 2 - 1) as i:
                moe0(i)
            moe0(E // 2 - 1, last=True)

            normalise(2)
            dve.wait_ge(s_wp, 16 * 4)
            link(v.memset(VT[:, :, :, :], 1.0))
            for c in range(NC):
                k = c % 2
                for w in range(2):
                    rope = [ropes[:, 2 * w + r, :].unsqueeze(1).to_broadcast([P, 2, S]) for r in range(2)]
                    r1, r2 = RT_1[:, w, :], RT_2[:, w, :]
                    if c:
                        dve.wait_ge(s_rot, 5 * c) if w else dve.wait_ge(s_qr, c)
                    dve.wait_ge(s_pj, 5 * c + 2 * w + 1)
                    v.tensor_tensor(r1.rearrange("p (s t) -> p s t", s=2),
                                    bank[2 * w][:, :].rearrange("p (s t) -> p s t", s=2), rope[0], ALU.mult
                                    ).then_inc(s_rot, 1)
                    dve.wait_ge(s_pj, 5 * c + 2 * w + 2)
                    v.tensor_tensor(r2.rearrange("p (s t) -> p s t", s=2),
                                    bank[2 * w + 1][:, :].rearrange("p (s t) -> p s t", s=2), rope[1], ALU.mult
                                    ).then_inc(s_rot, 1)
                dve.wait_ge(s_rot, 5 * c + 4)
                wait(dve, s_lo, 2 * (c - 1))
                v.scalar_tensor_tensor(out=KR[:, k, :], in0=RT_1[:, 1, :], scalar=rel0[:, 0:1], in1=RT_2[:, 1, :],
                                       op0=ALU.add, op1=ALU.add).then_inc(s_rot, 1)
                if c >= 2:
                    dve.wait_ge(s_qst[k], 16 * 7 * (c // 2))
                dve.wait_ge(s_pj, 5 * c + 5)
                for t in range(TPC):
                    ins = v.tensor_tensor(VT[:, k, t, :].rearrange("p (h v) -> p h v", v=VW)[:, :, 0:HD],
                                          bank[4][:, t * D:(t + 1) * D].rearrange("p (h v) -> p h v", v=HD),
                                          relv[:, :].unsqueeze(1).to_broadcast([P, H, HD]), ALU.add)
                ins.then_inc(s_v, 1)

            def bias_low(i):
                for g in range(18):
                    dve.wait_ge(s_bh, i * 18 + g + 1)
                    at = g * 16
                    v.tensor_tensor(BL[:, :, at:at + 16].rearrange("p h q -> p q h"),
                                    bank[g % RING][:, :].rearrange("p (q h) -> p q h", h=HS),
                                    BH[:, :, at:at + 16].rearrange("p h q -> p q h"), ALU.subtract).then_inc(s_bl, 1)

            def maxima(i, relative=False):
                for r in range(24):
                    dve.wait_ge(s_r1, i * 24 + r + 1)
                    dst = MX0[:, 2 * r:2 * r + 2, :] if r < 16 else MX1[:, 4 * (r - 16):4 * (r - 16) + 4, :]
                    v.tensor_reduce(dst.rearrange("p h b -> p (h b)"),
                                    bank[r % RING][:, :].rearrange("p (b c) -> p b c", c=32), AX, ALU.max,
                                    apply_transpose=True).then_inc(s_mx, 1)
                    if relative and r in (2, 13):
                        relative_out(i - 1, (r // 8,))
                dve.wait_ge(s_mx, (i + 1) * 24)
                v.tensor_tensor(MX0[:, :, 4:8], MX0[:, :, 4:8], MX1[:, :, :], ALU.max).then_inc(s_mc, 1)

            def row_maxima(i):
                dve.wait_ge(s_tm, i + 1)
                wait(dve, s_mr, i * 32)
                v.tensor_reduce(NM[:, :, :], bank[7][:, 0:2 * P].rearrange("p (h g c) -> p h c g", h=2, g=4),
                                AX, ALU.max, negate=True).then_inc(s_nm, 1)

            def relative_out(i, units=range(4)):
                for w in units:
                    dve.wait_ge(s_rl, i * 4 + w + 1)
                    if w == 0:
                        wait(dve, s_rst, i * 16 * 8)
                    v.tensor_copy(RS[:, :, 16 * w:16 * w + 16].rearrange("p h i -> p i h"),
                                  bank[5 + w % 2][:, :].rearrange("p (i h) -> p i h", h=HS)).then_inc(s_re, 1)

            def add_low(i):
                for r in range(24):
                    dve.wait_ge(s_r2, i * 24 + r + 1)
                    if r < 16:
                        dst = bank[r % RING2][:, :].rearrange("p (h q) -> p h q", q=S)[:, :, 0:X0]
                        low = BL[:, 2 * r:2 * r + 2, 0:X0]
                    else:
                        dst = bank[r % RING2][:, :].rearrange("p (h q) -> p h q", q=P)
                        low = BL[:, 4 * (r - 16):4 * (r - 16) + 4, X0:QB]
                    v.tensor_tensor(dst, dst, low, ALU.add).then_inc(s_ba, 1)

            bias_low(0)
            maxima(0)
            row_maxima(0)
            add_low(0)
            with dve.Fori(1, NP) as i:
                bias_low(i)
                maxima(i, relative=True)
                row_maxima(i)
                relative_out(i - 1, (2, 3))
                add_low(i)
            dve.wait_ge(s_din, 16)
            v.reciprocal(DR[0:H * (NP - 1), :], DN[0:H * (NP - 1), :]).then_inc(s_dr, 1)
            relative_out(NP - 1)

            dve.wait_ge(s_gld, 32)
            for c in range(NC + 1):
                if c == NC - 3:
                    dve.wait_ge(s_din7, 16)
                    v.reciprocal(DR7[0:H, :], DN7[0:H, :]).then_inc(s_dr, 1)
                if c < NC:
                    dve.wait_ge(s_cr, c + 1)
                    dve.wait_ge(s_db, c + 1)
                    wait(dve, s_y, NC + c - 1)
                    v.tensor_tensor(CX[:, c % 2, :], chunk(C1, c), bank[c % 2][:, :], ALU.mult).then_inc(s_cx, 1)
                if c:
                    dve.wait_ge(s_y, NC + c)
                    gated(c - 1, bank[6 + (c - 1) % 2][:, :].rearrange("p (b t f) -> p b t f", b=2, t=2), 0, NC)
                if c >= 2:
                    dve.wait_ge(s_yr, NC + c - 1)
                    statistics(c - 2)
            dve.wait_ge(s_yr, 2 * NC)
            statistics(NC - 1)

            normalise(3)
            dve.wait_ge(s_wm[1], 16 * 7)
            dve.wait_ge(s_m1, 1 + NC)
            softmax_shift(1)
            dve.wait_ge(s_el, 2)
            softmax_end()
            link(pick(PR[:, :, :], m1[:, :], OH1[:, :, :]))
            second(m2[:, :])

            for k in range(2):
                ins = v.tensor_copy(ROWS[k][:, :, D:RW], rowid[:, k, :].unsqueeze(2))
            ins.then_inc(s_ids, 1)
            link(v.tensor_tensor(ME[:, :, :].rearrange("p e t -> p t e"), OH1[:, :, :], OH2[:, :, :], ALU.add))
            for e in range(E):
                ins = v.tensor_tensor_scan(IN[:, e, :], ones[:, 0:NT], ME[:, e, :], 0.0, ALU.mult, ALU.add)
            link(ins)
            v.tensor_copy(tot[:, :].unsqueeze(2), IN[:, :, NT - 1:NT]).then_inc(s_tot, 1)
            link(v.tensor_tensor(EX[:, :, :], IN[:, :, :], ME[:, :, :], ALU.subtract))
            dve.wait_ge(s_rank, 1)
            c3 = cmp[:, 0:E * KT].rearrange("p (e k) -> p e k", e=E)
            link(v.tensor_tensor(c3, bank[6][:, E:2 * E].unsqueeze(2).to_broadcast([P, E, KT]),
                                 steps[:, 1, 0:KT].unsqueeze(1).to_broadcast([P, E, KT]), ALU.is_gt))
            link(v.tensor_reduce(tiles[:, :], c3, AX, ALU.add))
            link(v.tensor_tensor_scan(upto[:, :], ones[:, 0:E], tiles[:, :], 0.0, ALU.mult, ALU.add))
            link(v.tensor_tensor(offs[:, :], upto[:, :], tiles[:, :], ALU.subtract))
            link(v.scalar_tensor_tensor(out=offs[:, :], in0=offs[:, :], scalar=float(GT), in1=bank[6][:, 0:E],
                                        op0=ALU.mult, op1=ALU.add))
            link(v.tensor_tensor(EX[:, :, :], EX[:, :, :], offs[:, :].unsqueeze(2).to_broadcast([P, E, NT]), ALU.add))
            for k, oh in ((0, OH1), (1, OH2)):
                if k:
                    dve.wait_ge(s_dest, 1)
                link(v.tensor_tensor(EQ[:, :, :], oh[:, :, :], EX[:, :, :].rearrange("p e t -> p t e"), ALU.mult))
                link(v.tensor_reduce(idx[:, :], EQ[:, :, :], AX, ALU.add))
                v.tensor_copy(dest[k][:, :], idx[:, :]).then_inc(s_dest, 1)
            c3 = cmp[:, 0:NG * E].rearrange("p (n e) -> p n e", e=E)
            link(v.tensor_tensor(c3, upto[:, :].unsqueeze(1).to_broadcast([P, NG, E]),
                                 steps[:, 0, 0:NG].unsqueeze(2).to_broadcast([P, NG, E]), ALU.is_le))
            link(v.tensor_reduce(texp[:, :], c3, AX, ALU.add))
            link(v.tensor_scalar(texp[:, :], texp[:, :], float(E - 1), None, ALU.min))
            v.tensor_copy(texpu[:, :], texp[:, :]).then_inc(s_dest, 1)

            link(v.tensor_tensor(m2[:, :], m2[:, :], m1[:, :], ALU.subtract))
            v.tensor_scalar(m2[:, :], m2[:, :], 0.5, None, ALU.mult).then_inc(s_lg, 1)
            for c in range(NC):
                dve.wait_ge(s_sdn, c + 1)
                acc = ACC[:, c * TPC:(c + 1) * TPC, :]
                ins = v.tensor_tensor(acc, bank[4 + c % 2][:, :].rearrange("p (t f) -> p t f", t=TPC),
                                      W1S[:, OB:OB + D].unsqueeze(1).to_broadcast([P, TPC, D]), ALU.add)
                ins.then_inc(s_sout, 1)
                dve.wait_ge(s_sout, c + 1)
                add_gated(c, acc.rearrange("p (b t) f -> p b t f", b=2), 1, s_res)
            dve.wait_ge(s_el, 3)
            link(v.tensor_scalar(ssum[:, :], w2[:, :], 1.0, None, ALU.add))
            link(v.reciprocal(w1[:, :], ssum[:, :]))
            v.tensor_tensor(w2[:, :], w2[:, :], w1[:, :], ALU.mult).then_inc(s_lg, 1)

            def tile_in(j, k):
                dve.wait_ge(s_xp, j + 1)
                if not isinstance(j, int) or j >= UT:
                    dve.wait_ge(s_yo[k], 32 * (j // UT) if isinstance(j, int) else step[0] * 32 + (32 if k < step[1] else 0))
                v.tensor_copy(rid[:, k, :].unsqueeze(2), XR[:, k, :, D:RW])
                wait(dve, s_up[1], 2 * (j - 1))
                v.tensor_copy(XT[:, k % 2, :], bank[4 + k % 2][:, 0:GT]).then_inc(s_xt, 1)

            def results(j, k):
                dve.wait_ge(s_dn[1], j + 1)
                v.tensor_tensor(YS[:, k, :, :], bank[6 + k % 2][:, 0:GT].rearrange("p (r n) -> p r n", r=2),
                                W1[:, k, OB:OB + D].unsqueeze(1).to_broadcast([P, 2, D]), ALU.add).then_inc(s_ys, 1)

            step = [0, 0]
            tile_in(0, 0)
            for j in range(UT):
                tile_in(j + 1, (j + 1) % UT)
                if j:
                    results(j - 1, j - 1)
            with dve.Fori(1, FULL) as i:
                for k in range(UT):
                    step[:] = (i, 0) if k < UT - 1 else (i + 1, 0)
                    tile_in(i * UT + k + 1, (k + 1) % UT)
                    results(i * UT + k - 1, (k - 1) % UT)
            last = FULL * UT
            for k in range(LAST):
                if k < LAST - 1:
                    tile_in(last + k + 1, k + 1)
                results(last + k - 1, (k - 1) % UT)
            results(NG - 1, LAST - 1)
            dve.wait_ge(s_res, NC)
            for c in range(NC):
                dve.wait_ge(s_y1, c + 1)
                dve.wait_ge(s_y2, c + 1)
                y = [YG[k][:, c * TPC:(c + 1) * TPC, :].rearrange("p t f -> p (t f)") for k in range(2)]
                link(v.tensor_tensor(y[0], y[0], y[1], ALU.add))
                add_gated(c, y[0].rearrange("p (b t f) -> p b t f", b=2, t=2), 1, s_fin)

        @block.tensor
        def _(pe):
            mm = nc.tensor.matmul

            pe.wait_ge(s_cm, 1)
            pe.wait_ge(s_set, 1)
            pe.wait_ge(s_dv, 8)
            for l in range(2):
                for m in range(6):
                    at = (l * 6 + m) * B
                    mm(bank[0][:, at:at + B], wmod[:, l, m * D:(m + 1) * D], scT[:, l, :], start=True, stop=True)
            for l in range(2):
                for g, m in ((0, 2), (1, 5)):
                    at = (2 * l + g) * D
                    ins = mm(bank[1][0:B, at:at + D], scT[:, l, :], wmod[:, l, m * D:(m + 1) * D], start=True, stop=True)
            ins.then_inc(s_mod, 1)
            pe.wait_ge(s_const, 16 * 12)
            mm(bank[4][:, 0:D], Wcr[:, :], WoT[:, :], start=True, stop=True)
            mm(bank[5][0:1, 0:D], bcol[:, :], WoT[:, :], start=True, stop=True).then_inc(s_m1, 1)

            def layer_norm(n, then=None):
                for c in range(NC):
                    pe.wait_ge(s_xn, n * NC + c + 1)
                    wait(pe, s_hT, n * NC + c - 1)
                    if n == 0 and c == 0:
                        pe.wait_ge(s_gg, 1)
                    for t in range(TPC):
                        ins = nc.tensor.transpose(bank[c % 2][:, t * P:(t + 1) * P], XN[:, c % 2, t, :], ident[:, :])
                    ins.then_inc(s_tr, 1)
                    if then:
                        then(c)

            pe.wait_ge(s_zm, 1)
            mm(bank[5][:, 0:D], ones[0:1, :], crow[0:1, :], start=True, stop=True).then_inc(s_y0, 1)
            layer_norm(0)
            for h in range(2):
                pe.wait_ge(s_hT, (h + 1) * NC // 2)
                for pad, at in ((WTpad, S), (WBpad, 0)):
                    for b in range(8):
                        ins = mm(bank[2 + h][:, at:at + S], pad[:, 112 - N * b:240 - N * b],
                                 hT[:, (8 * h + b) * S:(8 * h + b + 1) * S], start=(b == 0), stop=(b == 7))
                ins.then_inc(s_ssm, 1)
            for c in range(NC):
                pe.wait_ge(s_hs, c // 4 + 1)
                wait(pe, s_gt, c - 1)
                for t in range(TPC):
                    T = c * TPC + t
                    b = T // 2
                    dst = bank[6 + c % 2][:, t * D:(t + 1) * D]
                    at = (T % 2) * P
                    mm(dst, HSC[:, b // 8, at:at + P], ZM[:, b % 8, :], start=True, stop=False)
                    ins = mm(dst, hT[:, T * P:(T + 1) * P], M2[:, :], start=False, stop=True)
                ins.then_inc(s_y, 1)

            def logits0(c):
                pe.wait_ge(s_hT, NC + c + 1)
                for T in range(c * TPC, (c + 1) * TPC):
                    ins = mm(bank[6][:, T * E:(T + 1) * E], hT[:, T * P:(T + 1) * P], gateT[:, :], start=True, stop=True)
                ins.then_inc(s_cnt, 1)

            layer_norm(1)
            pe.wait_ge(s_wm[0], 16 * 3)
            for c in range(NC):
                logits0(c)
            pe.wait_ge(s_oh, 1)
            mm(bank[7][:, 0:E], ones[:, :], cnt[:, :], start=True, stop=True).then_inc(s_cnt, 1)

            def down0(u, j):
                k = (j // NC) % 2
                pe.wait_ge(s_hm, u + 1)
                wait(pe, s_acc[0], u - 1)
                for t in range(TPC):
                    ins = mm(bank[4 + j % 2][:, t * D:(t + 1) * D], HM0[:, j % 2, t * P:(t + 1) * P],
                             W0[:, k, 2 * F0:3 * F0], start=True, stop=True)
                ins.then_inc(s_dn[0], 1)

            def moe0(i):
                for j in range(2 * NC):
                    u = i * 2 * NC + j
                    k, c = j // NC, j % NC
                    if c == 0:
                        pe.wait_ge(s_w[0][k], 16 * i + 16)
                    wait(pe, s_hm, u - 1)
                    mm(bank[j % 2][:, :], W0[:, k, 0:F0], chunk(hT, c), start=True, stop=True)
                    mm(bank[2 + j % 2][:, :], W0[:, k, F0:2 * F0], chunk(hT, c), start=True, stop=True
                       ).then_inc(s_up[0], 1)
                    if j:
                        down0(u - 1, j - 1)
                down0(u, 2 * NC - 1)

            moe0(0)
            with pe.Fori(1, E // 2) as i:
                moe0(i)

            layer_norm(2)
            pe.wait_ge(s_wp, 16 * 4)
            for c in range(NC):
                pe.wait_ge(s_hT, 3 * NC)
                for w in range(4):
                    if c:
                        pe.wait_ge(s_rot, 5 * (c - 1) + w + 1)
                    mm(bank[w][:, :], Wqkv[:, w, :], chunk(hT, c), start=True, stop=True).then_inc(s_pj, 1)
                wait(pe, s_v, c)
                for t in range(TPC):
                    T = c * TPC + t
                    ins = mm(bank[4][:, t * D:(t + 1) * D], hT[:, T * P:(T + 1) * P], Wqkv[:, 4, :],
                             start=True, stop=True)
                ins.then_inc(s_pj, 1)

            def relative_scores(i, banks):
                for g in banks:
                    if g < RING:
                        if not isinstance(i, int):
                            pe.wait_ge(s_ex, (i - 1) * 24 + 21 + g + 1)
                    else:
                        pe.wait_ge(s_bl, i * 18 + g - RING + 1)
                    for x in range(16):
                        q = g * 16 + x
                        local = q if q < X0 else q - X0
                        col = q if q < X0 else q - X0 + P
                        ins = mm(bank[g % RING][:, x * HS:(x + 1) * HS], GTB[:, X0 - local:X0 - local + P],
                                 QG[:, :, col], start=True, stop=True)
                    ins.then_inc(s_gen, 1)

            def scores(i, rnd, banks=range(24)):
                done = s_r1 if rnd == 1 else s_r2
                ring = RING if rnd == 1 else RING2
                for r in banks:
                    if r < RING:
                        if rnd == 1:
                            pe.wait_ge(s_bl, i * 18 + 15 + r + 1)
                        else:
                            pe.wait_ge(s_mx, i * 24 + 21 + r + 1)
                    elif r < ring:
                        wait(pe, s_pe, 4 * i)
                    else:
                        pe.wait_ge(s_mx if rnd == 1 else s_ex, i * 24 + r - ring + 1)
                    if r == 0 and rnd == 1:
                        pe.wait_ge(s_bl, i * 18 + 18)
                    dst = bank[r % ring]
                    if r < 16:
                        d3 = dst[:, :].rearrange("p (h q) -> p h q", q=S)
                        for x in range(2):
                            h = 2 * r + x
                            mm(d3[:, x, :], KG[:, h, 0:P], QG[:, h, :], start=(x == 0), stop=False,
                               skip_group_check=True)
                        ins = mm(d3[:, :, 0:X0], identb[:, :], BH[:, 2 * r:2 * r + 2, 0:X0], start=False,
                                 stop=True, skip_group_check=True)
                    else:
                        h0 = 4 * (r - 16)
                        for x in range(4):
                            mm(dst[:, x * P:(x + 1) * P], KG[:, h0 + x, P:S], QG[:, h0 + x, P:S], start=(x == 0),
                               stop=False, skip_group_check=True)
                        ins = mm(dst[:, :].rearrange("p (h q) -> p h q", q=P), identb[:, :], BH[:, h0:h0 + 4, X0:QB],
                                 start=False, stop=True, skip_group_check=True)
                    ins.then_inc(done, 1)

            def transpose_maxima(i):
                pe.wait_ge(s_mc, i + 1)
                wait(pe, s_nm, i)
                for g in range(2):
                    ins = nc.tensor.transpose(bank[7][:, g * P:(g + 1) * P],
                                              MX0[:, g * H:(g + 1) * H, :].rearrange("p h b -> p (h b)"), ident[:, :])
                ins.then_inc(s_tm, 1)

            def weighted_values(i, halves=range(8)):
                if halves[0] == 0:
                    pe.wait_ge(s_vin, (i + 1) * 16)
                for half in halves:
                    w, g = half // 2, half % 2
                    s, hb = w % 2, w // 2
                    if half in (0, 2):
                        pe.wait_ge(s_ex, i * 24 + (20 if half == 0 else 24))
                    if g == 0:
                        pe.wait_ge(s_pe, i * 4 + w - 1 if w >= 2 else i * 4)
                    for j in range(4):
                        h = 4 * (2 * hb + g) + j
                        mm(bank[4 - w % 2][32 * j:32 * j + VW, g * S:(g + 1) * S], VS[:, 2 * s, h, :],
                           PT0[:, 2 * h + s, :], start=True, stop=False, skip_group_check=True)
                    for j in range(4):
                        h = 4 * (2 * hb + g) + j
                        ins = mm(bank[4 - w % 2][32 * j:32 * j + VW, g * S + P:(g + 1) * S],
                                 VS[:, 2 * s + 1, h, :], PT1[:, 2 * h + s, :], start=False, stop=True,
                                 skip_group_check=True)
                    if g:
                        ins.then_inc(s_pv, 1)

            def weighted_relative(i, parts=range(8)):
                for part in parts:
                    w = part // 2
                    if part % 2 == 0:
                        pe.wait_ge(s_re, i * 4 + w - 1 if w >= 2 else i * 4)
                    for x in range(8 * (part % 2), 8 * (part % 2) + 8):
                        a = 16 * w + x
                        for j in range(4):
                            q = 64 * j + a
                            dst = bank[5 + w % 2][32 * j:32 * j + HD, x * HS:(x + 1) * HS]
                            if q < P:
                                ins = mm(dst, relk[:, q, :], PT0[:, :, q], start=True, stop=True,
                                         skip_group_check=True)
                            else:
                                near = q < P + REL - 1
                                ins = mm(dst, relk[:, q - P, :], PT1[:, :, q - P], start=True, stop=not near,
                                         skip_group_check=True)
                                if near:
                                    ins = mm(dst, relk[:, q, :], PT0[:, :, q], start=False, stop=True,
                                             skip_group_check=True)
                    if part % 2:
                        ins.then_inc(s_rl, 1)

            pe.wait_ge(s_tab, 16 * 7)
            pe.wait_ge(s_tb, 1)
            pe.wait_ge(s_rot, 5 * NC)
            pe.wait_ge(s_v, NC)
            pe.wait_ge(s_in, 16 * 3)
            relative_scores(0, range(18))
            scores(0, 1)
            transpose_maxima(0)
            pe.wait_ge(s_mr, 32)
            scores(0, 2)
            with pe.Fori(1, NP) as i:
                weighted_values(i - 1, range(4))
                pe.wait_ge(s_in, (i + 1) * 16 * 3)
                for half, banks in ((4, (0, 4)), (5, (4, 7)), (6, (7, 10)), (7, (10, 13))):
                    relative_scores(i, range(*banks))
                    weighted_values(i - 1, (half,))
                relative_scores(i, range(13, 16))
                weighted_relative(i - 1, (0,))
                relative_scores(i, range(16, 18))
                weighted_relative(i - 1, (1,))
                for part in range(2, 6):
                    scores(i, 1, range(6 * part - 12, 6 * part - 6))
                    weighted_relative(i - 1, (part,))
                transpose_maxima(i)
                weighted_relative(i - 1, (6, 7))
                pe.wait_ge(s_mr, (i + 1) * 32)
                scores(i, 2)
            weighted_values(NP - 1)
            weighted_relative(NP - 1)

            pe.wait_ge(s_wo, 32)
            pe.wait_ge(s_dr, 1)
            for c in range(NC + 1):
                if c < NC:
                    wait(pe, s_cx, c - 1)
                    if c < NC - 1:
                        rows = slice(0, H * (NP - 1))
                        ins = mm(bank[c % 2][:, :], selp[rows, c, :], DR[rows, :], start=True, stop=True)
                    else:
                        pe.wait_ge(s_dr, 2)
                        ins = mm(bank[c % 2][:, :], selp[0:H, 0, :], DR7[0:H, :], start=True, stop=True)
                    ins.then_inc(s_db, 1)
                if c:
                    k = (c - 1) % 2
                    pe.wait_ge(s_cx, c)
                    wait(pe, s_gt, NC + c - 2)
                    for t in range(TPC):
                        ins = mm(bank[6 + k][:, t * D:(t + 1) * D], CX[:, k, t * P:(t + 1) * P], woT1[:, :],
                                 start=True, stop=True)
                    ins.then_inc(s_y, 1)

            def route(c):
                if 1 <= c <= NC:
                    pe.wait_ge(s_hT, 3 * NC + c)
                    wait(pe, s_relu, c - 2)
                    mm(bank[3 + (c - 1) % 2][0:32, :], Wr1[:, :], chunk(hT, c - 1), start=True, stop=True
                       ).then_inc(s_rh, 1)
                if c == 2:
                    pe.wait_ge(s_one, 1)
                if c >= 2:
                    pe.wait_ge(s_relu, c - 1)
                    for t in range(TPC):
                        T = (c - 2) * TPC + t
                        ins = mm(bank[2][:, T * E:(T + 1) * E], RT1[0:33, (c - 2) % 2, t * P:(t + 1) * P],
                                 Wr2[0:33, :], start=True, stop=True)
                    ins.then_inc(s_m1, 1)

            pe.wait_ge(s_wm[1], 16 * 7)
            layer_norm(3, route)
            route(NC)
            route(NC + 1)
            for c in range(NC):
                if c >= 2:
                    pe.wait_ge(s_rows, 2 * (c - 1))
                for t in range(TPC):
                    T = c * TPC + t
                    ins = nc.tensor.transpose(bank[6 + c % 2][:, t * P:(t + 1) * P], hT[:, T * P:(T + 1) * P],
                                              ident[:, :])
                ins.then_inc(s_back, 1)

            def ranks():
                pe.wait_ge(s_tot, 1)
                pe.wait_ge(s_rows, 2 * NC)
                mm(bank[6][:, 0:E], below[:, :], tot[:, :], start=True, stop=True, skip_group_check=True)
                mm(bank[6][:, E:2 * E], ones[:, :], tot[:, :], start=True, stop=True, skip_group_check=True
                   ).then_inc(s_rank, 1)

            pe.wait_ge(s_sw, 16)
            for c in range(NC + 1):
                if c < NC:
                    for b in range(KB1):
                        if c:
                            pe.wait_ge(s_sact, (c - 1) * KB1 + b + 1)
                        elif b >= 3:
                            pe.wait_ge(s_relu, NC)
                        mm(bank[b][:, :], W1S[:, b * P:(b + 1) * P], chunk(hT, c), start=True, stop=True
                           ).then_inc(s_sup, 1)
                if c == RANK_AT:
                    ranks()
                if c:
                    pe.wait_ge(s_sact, c * KB1)
                    wait(pe, s_sout, c - 2)
                    for t in range(TPC):
                        for b in range(KB1):
                            ins = mm(bank[4 + (c - 1) % 2][:, t * D:(t + 1) * D],
                                     HM1[:, (c - 1) % 2, b, t * P:(t + 1) * P],
                                     W1S[:, I1 + b * D:I1 + (b + 1) * D], start=(b == 0), stop=(b == KB1 - 1))
                    ins.then_inc(s_sdn, 1)
            def transpose_tile(j, k, arrived):
                pe.wait_ge(s_xr[k], arrived)
                wait(pe, s_xt, j - 1)
                for r in range(2):
                    ins = nc.tensor.transpose(bank[4 + k % 2][:, r * P:(r + 1) * P], XR[:, k, r, 0:D], ident[:, :])
                ins.then_inc(s_xp, 1)

            def up_tile(j, k, arrived):
                pe.wait_ge(s_xt, j + 1)
                pe.wait_ge(s_ew[k], arrived)
                for b in range(KB1):
                    if b % 2 == 0:
                        wait(pe, s_act[1], (j - 2) * KB1 + b + 2)
                    ins = mm(bank[2 * (k % 2) + b // 2][:, b % 2 * GT:(b % 2 + 1) * GT], W1[:, k, b * P:(b + 1) * P],
                             XT[:, k % 2, :], start=True, stop=True, skip_group_check=True)
                    if b % 2:
                        ins.then_inc(s_up[1], 1)

            def down_tile(j, k):
                pe.wait_ge(s_act[1], (j + 1) * KB1)
                wait(pe, s_ys, j - 1)
                for r in range(2):
                    for b in range(KB1):
                        ins = mm(bank[6 + k % 2][:, r * D:(r + 1) * D], HMT[:, k % 2, b, r * P:(r + 1) * P],
                                 W1[:, k, I1 + b * D:I1 + (b + 1) * D], start=(b == 0), stop=(b == KB1 - 1),
                                 skip_group_check=True)
                ins.then_inc(s_dn[1], 1)

            pe.wait_ge(s_res, NC)
            transpose_tile(0, 0, 16)
            for j in range(UT):
                up_tile(j, j, 16)
                transpose_tile(j + 1, (j + 1) % UT, 16 if j < UT - 1 else 32)
                if j:
                    down_tile(j - 1, j - 1)
            with pe.Fori(1, FULL) as i:
                for k in range(UT):
                    up_tile(i * UT + k, k, 16 * i + 16)
                    transpose_tile(i * UT + k + 1, (k + 1) % UT, 16 * i + (16 if k < UT - 1 else 32))
                    down_tile(i * UT + k - 1, (k - 1) % UT)
            last = FULL * UT
            for k in range(LAST):
                up_tile(last + k, k, 16 * (FULL + 1))
                if k < LAST - 1:
                    transpose_tile(last + k + 1, k + 1, 16 * (FULL + 1))
                down_tile(last + k - 1, (k - 1) % UT)
            down_tile(NG - 1, LAST - 1)


_SHAPE = (16, 256, 128)


def constants():
    import numpy as np
    k = {}
    k["ident"] = np.eye(P, dtype=np.float32)
    k["below"] = np.triu(np.ones((P, P), dtype=np.float32), 1)
    token = (np.arange(NT)[None, :] * P + np.arange(P)[:, None]).astype(np.float32)
    k["rowid"] = np.stack([token, token + np.float32(TOK)], axis=1)
    count = np.arange(64, dtype=np.float32)
    k["steps"] = np.tile(np.stack([count, count * np.float32(GT)])[None], (P, 1, 1))
    k["padding"] = np.zeros((NG * GT // 8, RW), dtype=np.float32)
    k["padding"][:, D] = 2 * TOK + np.arange(NG * GT // 8)
    k["blockmask"] = np.repeat(np.eye(8, dtype=np.float32), N, axis=0)
    k["iota"] = np.tile(np.arange(E, dtype=np.float32), (P, 1))
    k["onesrow"] = np.ones((1, HS, S), dtype=np.uint16) * np.uint16(0x3F80)
    k["zerorow"] = np.zeros((1, HS, S), dtype=np.uint16)
    k["selp"] = np.zeros((NP, H, NP, H, HD), dtype=np.float32)
    for c in range(NP):
        k["selp"][c, :, c] = np.eye(H, dtype=np.float32)[:, :, None]
    k["selp"] = k["selp"].reshape(NP * H, NP, H * HD)
    low = np.zeros((25, 1), np.float32)
    low[8:16] = 1
    k["lowrows"] = low
    freq = (np.float32(1.0) / np.float32(10000.0) ** (np.arange(0, HD, 2, dtype=np.float32) / np.float32(HD)))
    ang = np.outer(np.arange(S, dtype=np.float32), freq.astype(np.float32)).astype(np.float32)
    cos = np.repeat(np.cos(ang), 2, axis=1).T
    sin = np.repeat(np.sin(ang), 2, axis=1).T.copy()
    sin[0::2] *= -1
    cos, sin = np.tile(cos, (H, 1)), np.tile(sin, (H, 1))
    r = np.float32(HD) ** np.float32(-0.5)
    k["ropes"] = np.stack([cos * r, sin * r, cos, sin], axis=1).astype(np.float32)
    return k


def kernel(**inputs):
    import numpy as np
    import concourse.bacc as bacc
    from concourse.bass_utils import run_bass_kernel_spmd

    a = {n: np.asarray(x) for n, x in inputs.items()}
    k = constants()
    L = {}
    L["x"] = a["L0_attn_x"].reshape(TOK, D)
    L["cT"] = np.stack([a["L0_c"].T, a["L1_c"].T], axis=1)
    L["wmod"] = np.stack([a["L0_wmod"], a["L1_wmod"]], axis=1)
    L["wbT"] = a["L0_attn_W_b"].T
    L["wt16"] = np.repeat(a["L0_attn_W_t"].T, N, axis=1)
    L["wc8"] = np.tile(a["L0_attn_W_c"], (1, 8))
    L["woT0"] = a["L0_attn_W_o"].T
    L["bb8"] = np.tile(a["L0_attn_b_b"], 8)[:, None]
    L["A8"] = np.tile(a["L0_attn_A"], 8)[:, None]
    L["bt"] = np.tile(a["L0_attn_b_t"], P)[:, None]
    L["Dv"] = a["L0_attn_D"][:, None]
    L["bc"] = a["L0_attn_b_c"][:, None]
    L["bo"] = a["L0_attn_b_o"][None, :]
    L["gateT"] = a["L0_ffn_gate_weight"].T
    L["sim"] = np.tile(a["L0_ffn_similarity_matrix"][None], (P, 1, 1))
    L["w0"] = np.concatenate([a["L0_ffn_gate_up_proj"].transpose(0, 2, 1), a["L0_ffn_down_proj"].transpose(0, 2, 1)],
                             axis=2)
    swap = np.arange(D).reshape(-1, 2)[:, ::-1].reshape(-1)
    wq, wk, wv = a["L1_attn_w_q"], a["L1_attn_w_k"], a["L1_attn_w_v"]
    L["wqkv"] = np.stack([wq.T, wq[swap].T, wk.T, wk[swap].T, wv.T], axis=1)
    L["woT1"] = a["L1_attn_w_o"].T
    rel = a["L1_attn_rel_emb"]
    L["rel0"] = np.tile(rel[0], H)[:, None]
    L["rel0r"] = np.tile(rel[0][None], (P, 1))
    L["relk"] = rel[np.clip(np.arange(P)[:, None] - np.arange(X0)[None, :], -REL, REL) + REL]
    gt = rel[np.clip(np.arange(X0 + P) - X0, -REL, REL) + REL].T
    mask = np.where(np.arange(X0 + P)[None, :] > X0, np.float32(NEG), np.float32(0.0))
    L["gt"] = np.concatenate([gt, gt, gt, mask], axis=0)
    L["rel0c"] = np.concatenate([rel[0], rel[0], rel[0], np.zeros(1, np.float32)])[:, None]
    L["wr1"] = a["L1_ffn_Wr1"]
    L["wr2"] = np.concatenate([a["L1_ffn_Wr2"], a["L1_ffn_br2"][None]], axis=0)
    L["br1"] = a["L1_ffn_br1"][:, None]
    up = np.concatenate([a["L1_ffn_Ws1"][None], a["L1_ffn_We1"]], axis=0)
    down = np.concatenate([a["L1_ffn_Ws2"][None], a["L1_ffn_We2"]], axis=0)
    down = down.reshape(E + 1, KB1, P, D).transpose(0, 2, 1, 3).reshape(E + 1, P, KB1 * D)
    bias = np.concatenate([a["L1_ffn_bs1"][None], a["L1_ffn_be1"]], axis=0).reshape(E + 1, KB1, P).transpose(0, 2, 1)
    below = np.concatenate([a["L1_ffn_bs2"][None], a["L1_ffn_be2"]], axis=0)[:, None, :].repeat(P, axis=1)
    packed = np.concatenate([up, down, bias, below], axis=2)
    L["w1s"], L["w1"] = packed[0], packed[1:]
    L.update(k)

    nc = bacc.Bacc("TRN2", target_bir_lowering=False, num_devices=1)
    arrays, args = {}, {}
    for name, v in L.items():
        v = np.ascontiguousarray(v)
        arrays[f"in_{name}"] = v
        dt = BF16 if v.dtype == np.uint16 else mybir.dt.from_np(v.dtype)
        if v.dtype == np.uint16:
            import ml_dtypes
            v = v.view(ml_dtypes.bfloat16)
            arrays[f"in_{name}"] = v
        args[name] = nc.dram_tensor(f"in_{name}", v.shape, dt, kind="ExternalInput").ap()
    out = nc.dram_tensor("out_dram", (TOK, D), F32, kind="ExternalOutput").ap()
    build(nc, args, out)
    r = run_bass_kernel_spmd(nc, [arrays], core_ids=[0])
    return r.results[0]["out_dram"].reshape(_SHAPE)
```
